# Optimizing a Trainium2 kernel written in Bass

```python
import numpy as np
import jax
import jax.numpy as jnp

def _softmax(x, axis=-1):
    return jax.nn.softmax(x, axis=axis)

def _gelu(x):
    return jax.nn.gelu(x, approximate=True)

def _silu(x):
    return jax.nn.silu(x)

def _sigmoid(x):
    return jax.nn.sigmoid(x)

def _layernorm(x, axis=-1, eps=1e-05):
    m = jnp.mean(x, axis=axis, keepdims=True)
    v = jnp.var(x, axis=axis, keepdims=True)
    return (x - m) / jnp.sqrt(v + eps)

def _scatter_add(tgt, idx, src, axis=0):
    return tgt.at[idx].add(src)

def _segment_sum(src, seg, n):
    return jax.ops.segment_sum(src, seg, n)
kernel_name = 'mk_xattn_seq_d1_seqx_r4_68bafb'

def setup_inputs(seed: int=0):
    np.random.seed(seed)
    _w = jnp.asarray

    def _rec_inputs():
        import jax
        import jax.numpy as jnp
        _rk = jax.random.key(seed)
        x = -0.0002928 + 1 * jax.random.normal(jax.random.fold_in(_rk, 1), (8, 256, 256), jnp.float32)
        _lenS = 256 - jax.random.randint(jax.random.fold_in(_rk, 7), (8,), 0, max(1, 256 // 4) + 1, jnp.int32)
        _lenS2 = 77 - jax.random.randint(jax.random.fold_in(_rk, 8), (8,), 0, max(1, 77 // 4) + 1, jnp.int32)
        _ctx_1024P = jax.random.normal(jax.random.fold_in(_rk, 11), (8, 16, 256), jnp.float32)
        _ctx_1024c = jax.random.dirichlet(jax.random.fold_in(_rk, 511), 0.3 * jnp.ones((16,), jnp.float32), (8, 77))
        _ctx_1024t = jnp.einsum('bsk,bkd->bsd', _ctx_1024c, _ctx_1024P)
        _ctx_1024t = _ctx_1024t * jax.lax.rsqrt(jnp.mean(jnp.square(_ctx_1024t)) + 1e-12) * 0.953939
        ctx_1024 = -1.39393e-06 + 0.999914 * (_ctx_1024t + 0.3 * jax.random.normal(jax.random.fold_in(_rk, 611), (8, 77, 256), jnp.float32))
        return (x, ctx_1024)
    x, ctx_1024 = _rec_inputs()

    def _L0_xattn_setup():
        import jax, jax.numpy as jnp
        import numpy as np
        B, S, SE, D, H, FF, E, K = (2, 512, 512, 256, 16, 1024, 8, 2)
        HD = D // H

        def _layernorm(x, g, b):
            m = x.mean(-1, keepdims=True)
            v = ((x - m) ** 2).mean(-1, keepdims=True)
            return (x - m) / jnp.sqrt(v + 1e-05) * g + b

        def _attn(q_in, k_in, v_in, wq, bq, wk, bk, wv, bv, wo, bo, causal):
            Bq, Sq, Dm = q_in.shape
            Sk = k_in.shape[1]
            Q = (q_in @ wq + bq).reshape(Bq, Sq, H, HD)
            Kp = (k_in @ wk + bk).reshape(Bq, Sk, H, HD)
            V = (v_in @ wv + bv).reshape(Bq, Sk, H, HD)
            scores = jnp.einsum('bqhd,bkhd->bhqk', Q, Kp) / jnp.sqrt(jnp.float32(HD))
            if causal:
                mask = jnp.tril(jnp.ones((Sq, Sk), bool))
                scores = jnp.where(mask, scores, -jnp.inf)
            a = jax.nn.softmax(scores, axis=-1)
            o = jnp.einsum('bhqk,bkhd->bqhd', a, V).reshape(Bq, Sq, Dm)
            return o @ wo + bo

        def _moe(x, rw, rb, w1, b1, w2, b2):
            T = x.shape[0] * x.shape[1]
            xf = x.reshape(T, D)
            router_weights = jax.nn.softmax(xf @ rw + rb, axis=-1)
            topw, topi = jax.lax.top_k(router_weights, K)
            topw = jax.nn.softmax(topw, axis=-1)
            combine = jnp.zeros((T, E), xf.dtype).at[jnp.arange(T)[:, None], topi].add(topw)
            h = jax.nn.gelu(jnp.einsum('td,edf->etf', xf, w1) + b1[:, None, :], approximate=False)
            eo = jnp.einsum('etf,efd->etd', h, w2) + b2[:, None, :]
            out = jnp.einsum('etd,te->td', eo, combine)
            return out.reshape(x.shape)
        key = jax.random.key(seed)
        ks = jax.random.split(key, 32)
        w = lambda k, shape: jax.random.normal(k, shape, jnp.float32) * 0.02
        inp = {'x': jax.random.normal(ks[0], (B, S, D), jnp.float32), 'encoder_output': jax.random.normal(ks[1], (B, SE, D), jnp.float32), 'sa_wq': w(ks[2], (D, D)), 'sa_bq': jnp.zeros((D,), jnp.float32), 'sa_wk': w(ks[3], (D, D)), 'sa_bk': jnp.zeros((D,), jnp.float32), 'sa_wv': w(ks[4], (D, D)), 'sa_bv': jnp.zeros((D,), jnp.float32), 'sa_wo': w(ks[5], (D, D)), 'sa_bo': jnp.zeros((D,), jnp.float32), 'ca_wq': w(ks[6], (D, D)), 'ca_bq': jnp.zeros((D,), jnp.float32), 'ca_wk': w(ks[7], (D, D)), 'ca_bk': jnp.zeros((D,), jnp.float32), 'ca_wv': w(ks[8], (D, D)), 'ca_bv': jnp.zeros((D,), jnp.float32), 'ca_wo': w(ks[9], (D, D)), 'ca_bo': jnp.zeros((D,), jnp.float32), 'ln1_g': jnp.ones((D,), jnp.float32), 'ln1_b': jnp.zeros((D,), jnp.float32), 'ln2_g': jnp.ones((D,), jnp.float32), 'ln2_b': jnp.zeros((D,), jnp.float32), 'ln3_g': jnp.ones((D,), jnp.float32), 'ln3_b': jnp.zeros((D,), jnp.float32), 'router_w': w(ks[10], (D, E)), 'router_b': jnp.zeros((E,), jnp.float32), 'e_w1': w(ks[11], (E, D, FF)), 'e_b1': jnp.zeros((E, FF), jnp.float32), 'e_w2': w(ks[12], (E, FF, D)), 'e_b2': jnp.zeros((E, D), jnp.float32)}
        return inp
    _L0_xattn_all = _L0_xattn_setup()
    _L0_xattn_in = {k: v for k, v in _L0_xattn_all.items() if k in ('sa_wq', 'sa_bq', 'sa_wk', 'sa_bk', 'sa_wv', 'sa_bv', 'sa_wo', 'sa_bo', 'ca_wq', 'ca_bq', 'ca_wk', 'ca_bk', 'ca_wv', 'ca_bv', 'ca_wo', 'ca_bo', 'ln1_g', 'ln1_b', 'ln2_g', 'ln2_b', 'ln3_g', 'ln3_b', 'router_w', 'router_b', 'e_w1', 'e_b1', 'e_w2', 'e_b2')}
    del _L0_xattn_all
    return {'x': x, 'ctx_1024': ctx_1024, 'L0_xattn_sa_wq': _L0_xattn_in['sa_wq'], 'L0_xattn_sa_bq': _L0_xattn_in['sa_bq'], 'L0_xattn_sa_wk': _L0_xattn_in['sa_wk'], 'L0_xattn_sa_bk': _L0_xattn_in['sa_bk'], 'L0_xattn_sa_wv': _L0_xattn_in['sa_wv'], 'L0_xattn_sa_bv': _L0_xattn_in['sa_bv'], 'L0_xattn_sa_wo': _L0_xattn_in['sa_wo'], 'L0_xattn_sa_bo': _L0_xattn_in['sa_bo'], 'L0_xattn_ca_wq': _L0_xattn_in['ca_wq'], 'L0_xattn_ca_bq': _L0_xattn_in['ca_bq'], 'L0_xattn_ca_wk': _L0_xattn_in['ca_wk'], 'L0_xattn_ca_bk': _L0_xattn_in['ca_bk'], 'L0_xattn_ca_wv': _L0_xattn_in['ca_wv'], 'L0_xattn_ca_bv': _L0_xattn_in['ca_bv'], 'L0_xattn_ca_wo': _L0_xattn_in['ca_wo'], 'L0_xattn_ca_bo': _L0_xattn_in['ca_bo'], 'L0_xattn_ln1_g': _L0_xattn_in['ln1_g'], 'L0_xattn_ln1_b': _L0_xattn_in['ln1_b'], 'L0_xattn_ln2_g': _L0_xattn_in['ln2_g'], 'L0_xattn_ln2_b': _L0_xattn_in['ln2_b'], 'L0_xattn_ln3_g': _L0_xattn_in['ln3_g'], 'L0_xattn_ln3_b': _L0_xattn_in['ln3_b'], 'L0_xattn_router_w': _L0_xattn_in['router_w'], 'L0_xattn_router_b': _L0_xattn_in['router_b'], 'L0_xattn_e_w1': _L0_xattn_in['e_w1'], 'L0_xattn_e_b1': _L0_xattn_in['e_b1'], 'L0_xattn_e_w2': _L0_xattn_in['e_w2'], 'L0_xattn_e_b2': _L0_xattn_in['e_b2']}

def reference(x, ctx_1024, L0_xattn_sa_wq, L0_xattn_sa_bq, L0_xattn_sa_wk, L0_xattn_sa_bk, L0_xattn_sa_wv, L0_xattn_sa_bv, L0_xattn_sa_wo, L0_xattn_sa_bo, L0_xattn_ca_wq, L0_xattn_ca_bq, L0_xattn_ca_wk, L0_xattn_ca_bk, L0_xattn_ca_wv, L0_xattn_ca_bv, L0_xattn_ca_wo, L0_xattn_ca_bo, L0_xattn_ln1_g, L0_xattn_ln1_b, L0_xattn_ln2_g, L0_xattn_ln2_b, L0_xattn_ln3_g, L0_xattn_ln3_b, L0_xattn_router_w, L0_xattn_router_b, L0_xattn_e_w1, L0_xattn_e_b1, L0_xattn_e_w2, L0_xattn_e_b2):
    import jax
    import jax.numpy as jnp

    def _L0_xattn_ref(x, encoder_output, sa_wq, sa_bq, sa_wk, sa_bk, sa_wv, sa_bv, sa_wo, sa_bo, ca_wq, ca_bq, ca_wk, ca_bk, ca_wv, ca_bv, ca_wo, ca_bo, ln1_g, ln1_b, ln2_g, ln2_b, ln3_g, ln3_b, router_w, router_b, e_w1, e_b1, e_w2, e_b2):
        import jax, jax.numpy as jnp
        import numpy as np
        B, S, SE, D, H, FF, E, K = (2, 512, 512, 256, 16, 1024, 8, 2)
        HD = D // H

        def _layernorm(x, g, b):
            m = x.mean(-1, keepdims=True)
            v = ((x - m) ** 2).mean(-1, keepdims=True)
            return (x - m) / jnp.sqrt(v + 1e-05) * g + b

        def _attn(q_in, k_in, v_in, wq, bq, wk, bk, wv, bv, wo, bo, causal):
            Bq, Sq, Dm = q_in.shape
            Sk = k_in.shape[1]
            Q = (q_in @ wq + bq).reshape(Bq, Sq, H, HD)
            Kp = (k_in @ wk + bk).reshape(Bq, Sk, H, HD)
            V = (v_in @ wv + bv).reshape(Bq, Sk, H, HD)
            scores = jnp.einsum('bqhd,bkhd->bhqk', Q, Kp) / jnp.sqrt(jnp.float32(HD))
            if causal:
                mask = jnp.tril(jnp.ones((Sq, Sk), bool))
                scores = jnp.where(mask, scores, -jnp.inf)
            a = jax.nn.softmax(scores, axis=-1)
            o = jnp.einsum('bhqk,bkhd->bqhd', a, V).reshape(Bq, Sq, Dm)
            return o @ wo + bo

        def _moe(x, rw, rb, w1, b1, w2, b2):
            T = x.shape[0] * x.shape[1]
            xf = x.reshape(T, D)
            router_weights = jax.nn.softmax(xf @ rw + rb, axis=-1)
            topw, topi = jax.lax.top_k(router_weights, K)
            topw = jax.nn.softmax(topw, axis=-1)
            combine = jnp.zeros((T, E), xf.dtype).at[jnp.arange(T)[:, None], topi].add(topw)
            h = jax.nn.gelu(jnp.einsum('td,edf->etf', xf, w1) + b1[:, None, :], approximate=False)
            eo = jnp.einsum('etf,efd->etd', h, w2) + b2[:, None, :]
            out = jnp.einsum('etd,te->td', eo, combine)
            return out.reshape(x.shape)
        x = _layernorm(x + _attn(x, x, x, sa_wq, sa_bq, sa_wk, sa_bk, sa_wv, sa_bv, sa_wo, sa_bo, True), ln1_g, ln1_b)
        x = _layernorm(x + _attn(x, encoder_output, encoder_output, ca_wq, ca_bq, ca_wk, ca_bk, ca_wv, ca_bv, ca_wo, ca_bo, False), ln2_g, ln2_b)
        x = _layernorm(x + _moe(x, router_w, router_b, e_w1, e_b1, e_w2, e_b2), ln3_g, ln3_b)
        return x
    x = _L0_xattn_ref(x, ctx_1024, L0_xattn_sa_wq, L0_xattn_sa_bq, L0_xattn_sa_wk, L0_xattn_sa_bk, L0_xattn_sa_wv, L0_xattn_sa_bv, L0_xattn_sa_wo, L0_xattn_sa_bo, L0_xattn_ca_wq, L0_xattn_ca_bq, L0_xattn_ca_wk, L0_xattn_ca_bk, L0_xattn_ca_wv, L0_xattn_ca_bv, L0_xattn_ca_wo, L0_xattn_ca_bo, L0_xattn_ln1_g, L0_xattn_ln1_b, L0_xattn_ln2_g, L0_xattn_ln2_b, L0_xattn_ln3_g, L0_xattn_ln3_b, L0_xattn_router_w, L0_xattn_router_b, L0_xattn_e_w1, L0_xattn_e_b1, L0_xattn_e_w2, L0_xattn_e_b2)
    return x

_drawn_inputs = setup_inputs


def setup_inputs(seed=0):
    import zlib

    import numpy as np

    out = dict(_drawn_inputs(seed))
    spreads = {'L0_xattn_sa_bq': (0.0, 0.8),
     'L0_xattn_sa_bk': (0.0, 0.8),
     'L0_xattn_sa_bv': (0.0, 0.1),
     'L0_xattn_sa_bo': (0.0, 0.1),
     'L0_xattn_ca_bq': (0.0, 0.8),
     'L0_xattn_ca_bk': (0.0, 0.8),
     'L0_xattn_ca_bv': (0.0, 0.1),
     'L0_xattn_ca_bo': (0.0, 0.1),
     'L0_xattn_ln1_g': (1.0, 0.2),
     'L0_xattn_ln1_b': (0.0, 0.1),
     'L0_xattn_ln2_g': (1.0, 0.2),
     'L0_xattn_ln2_b': (0.0, 0.1),
     'L0_xattn_ln3_g': (1.0, 0.2),
     'L0_xattn_ln3_b': (0.0, 0.1),
     'L0_xattn_router_b': (0.0, 0.1),
     'L0_xattn_e_b1': (0.0, 0.34),
     'L0_xattn_e_b2': (0.0, 0.1)}
    factors = {'L0_xattn_sa_wq': 8.0,
     'L0_xattn_sa_wk': 8.0,
     'L0_xattn_sa_wv': 3.186,
     'L0_xattn_ca_wq': 8.0,
     'L0_xattn_ca_wk': 8.0}
    for name, (base, spread) in spreads.items():
        noise = np.random.default_rng([zlib.crc32(name.encode()), seed]).standard_normal(out[name].shape)
        drawn = base * np.exp(spread * noise) if base else spread * noise
        out[name] = jnp.asarray(drawn.astype(out[name].dtype))
    for name, factor in factors.items():
        out[name] = (out[name] * factor).astype(out[name].dtype)
    return out
```

```python
from contextlib import ExitStack

import concourse.bass as bass
from concourse import mybir

ALU = mybir.AluOpType
ACT = mybir.ActivationFunctionType
AX = mybir.AxisListType.X
F32 = mybir.dt.float32
BF16 = mybir.dt.bfloat16
I32 = mybir.dt.int32
U32 = mybir.dt.uint32

P = 128
B, S, D = 8, 256, 256
H = 16
HD = D // H
SE = 77
E, FF, TOPK = 8, 1024, 2
T = B * S
QT_N = S // P
DC = D // P
FC = FF // P
HC = H // DC
STRIPS = 4
EPS = 1e-5
MASKED = -1e30

ROW = D + 2
REGION = T + P
NBLK = T * TOPK // P + E - 1
NDUMMY = NBLK - T * TOPK // P
XS_ROWS = E * REGION + NDUMMY * P
Y_PAD = T * TOPK
Y_ROWS = Y_PAD + (E + NDUMMY) * P

UA, UB = 12, 8
UNITS = UA + UB
RING = 4


def a_unit(m):
    c, r = divmod(m, 6)
    return (c, 0, range(4 * r, 4 * r + 4), P) if r < 2 else (c, 1, range(2 * r - 4, 2 * r - 2), S)


def b_unit(m):
    q, c, par = m // 4, m // 2 % 2, m % 2
    return c, q, range(4 * par, 4 * par + 4)


def head_of(c, slot):
    return c * HC + 2 * (slot % STRIPS) + slot // STRIPS


class WorkUse:

    def __init__(self, first, step, i, had):
        self.bank = first % 2
        self.filled = first + 1 + (step * i if i is not None else 0)
        self.had = had


def batch_script(loop):
    units_a = lambda b: [("A", b, m) for m in range(UA)]
    units_b = lambda b: [("B", b, m) for m in range(UB)]

    def pipeline(units, hooks):
        n = len(units)
        for k in range(n + 2):
            if k < n:
                yield ("scores", units[k])
            if 0 <= k - 1 < n:
                yield ("turn", units[k - 1])
            if k >= 2:
                yield ("values", units[k - 2])
            for h in hooks.get(k, ()):
                yield h

    def first():
        yield from [(s, 0) for s in ("xT", "q", "k", "v")]
        yield from pipeline(units_a(0), {12: [("rTA", 0)], 13: [("RA", 0)]})
        yield from [(s, 0) for s in ("oTA", "woA")]

    def body(b):
        yield from [(s, b + 1) for s in ("xT", "q", "k", "v")]
        yield from [(s, b) for s in ("cT", "k2", "v2", "x1T", "q2")]
        hooks = {9: [("rTB", b)], 10: [("RB", b), ("oTB", b)], 12: [("woB", b)], 16: [("x2T", b)], 17: [("route", b)],
                 20: [("rTA", b + 1)], 21: [("rank", b), ("RA", b + 1), ("oTA", b + 1)]}
        yield from pipeline(units_b(b) + units_a(b + 1), hooks)
        yield ("woA", b + 1)

    def last(b):
        yield from [(s, b) for s in ("cT", "k2", "v2", "x1T", "q2")]
        yield from pipeline(units_b(b), {9: [("rTB", b), ("RB", b), ("oTB", b)]})
        yield from [(s, b) for s in ("woB", "x2T", "route", "rank")]

    no_bank = {"scores", "turn", "values", "oTA", "oTB"}
    n, had = 0, [None, None]

    def numbered(steps, step, i):
        nonlocal n
        for name, what in steps:
            if name in no_bank:
                yield name, what, None
            else:
                yield name, what, WorkUse(n, step, i, had[n % 2])
                had[n % 2] = name, what
                n += 1

    yield from numbered(first(), 0, None)
    per = sum(name not in no_bank for name, _ in body(0))
    left = [(name, b) for name, b in first() if name not in no_bank][-2:]
    assert per % 2 == 0 and left == [(name, 0) for name, b in body(-1) if name not in no_bank][-2:]
    yield "enter", None, None
    i = loop()
    had[n % 2], had[(n + 1) % 2] = (left[0][0], i), (left[1][0], i)
    before = n
    yield from numbered(body(i), per, i)
    n = before + per * (B - 1)
    had[n % 2], had[(n + 1) % 2] = (left[0][0], B - 1), (left[1][0], B - 1)
    yield "leave", None, None
    yield from numbered(last(B - 1), 0, None)


class Chain:

    def __init__(self, eng, sem, per, turns):
        self.eng, self.sem, self.per, self.turns, self.n, self.i = eng, sem, per, turns, 0, None

    def enter(self, i):
        self.i, self.before = i, self.n

    def leave(self):
        assert self.n - self.before == self.per, ("links in the loop", self.n - self.before)
        self.n, self.i = self.before + self.per * self.turns, None

    def link(self, ins):
        self.n += 1
        ins.then_inc(self.sem, 1)
        self.eng.wait_ge(self.sem, self.n if self.i is None else self.n + self.per * self.i)


def decoder_layer(nc, t, out):
    ctx = ExitStack()
    with ctx:
        def sb(name, shape, dt=F32):
            return ctx.enter_context(nc.sbuf_tensor(name, shape, dt))

        def sem(name):
            return ctx.enter_context(nc.semaphore(name))

        xs_dram = nc.dram_tensor("dispatched", (XS_ROWS, ROW), F32, kind="Internal").ap()
        y_dram = nc.dram_tensor("expert_rows", (Y_ROWS, D), F32, kind="Internal").ap()
        x2_dram = nc.dram_tensor("x2_rows", (T, D), F32, kind="Internal").ap()

        w1 = sb("w1", [P, DC, E, FF])
        w2 = sb("w2", [P, E, FC, D])
        kz = w2[:, E - 2:E, :, :]
        SHARED = 5120
        shared = sb("shared", [P, SHARED])
        at = [0]

        def part(n):
            at[0] += n
            assert at[0] <= SHARED, at[0]
            return shared[:, at[0] - n:at[0]]
        wA = {k: part(DC * D).rearrange("p (k n) -> p k n", k=DC) for k in ("wq", "wk", "wv", "wo")}
        x_in = part(QT_N * D).rearrange("p (t d) -> p t d", t=QT_N)
        xres = part(QT_N * D).rearrange("p (t d) -> p t d", t=QT_N)
        qT = part(DC * S).rearrange("p (c n) -> p c n", c=DC)
        kT = part(DC * S).rearrange("p (c n) -> p c n", c=DC)
        vz = part(QT_N * H * 32).rearrange("p (t n) -> p t n", t=QT_N)
        at[0] = 0
        xb = [part(ROW) for _ in range(RING)]
        b2b = [part(D) for _ in range(RING)]
        xbT = part(DC * P).rearrange("p (c n) -> p c n", c=DC)
        hid = part(FF)
        gT = part(FF).rearrange("p (f n) -> p f n", f=FC)
        ge = part(NBLK * E).rearrange("p (j e) -> p j e", j=NBLK)
        skipped, blkf = part(NBLK), part(NBLK)
        y_a = xres

        wB = {k: sb(f"{k}_cross", [P, DC, D]) for k in ("wq", "wk", "wv", "wo")}
        vecs = {k: sb(k, [P, D]) for k in ("bvA", "boA", "bvB", "boB", "g1", "be1", "g2", "be2", "g3", "be3")}
        rw = sb("router_w", [P, DC, E])
        rb = sb("router_b", [P, E])
        bias_rows = sb("bias_rows", [4 * DC, P])
        b1_rows = sb("b1_rows", [E * FC, P])
        bias = sb("bias", [P, 4 * DC])
        b1 = sb("b1", [P, E * FC])

        xT = sb("xT", [P, DC, S])
        q2T = sb("q2T", [P, DC, S])
        x1 = sb("x1", [P, QT_N, D])
        x1res = sb("x1res", [P, QT_N, D])
        y_b = x1res
        ctx_in = sb("ctx_in", [SE, D])
        cT = sb("cT", [P, DC, SE])
        k2T = sb("k2T", [P, DC, SE])
        k2z = sb("k2z", [P, DC, HC, SE])
        v2z = sb("v2z", [SE, H * 32])
        probs = [sb(f"probs{k}", [P, 512]) for k in range(2)]
        probsT = [sb(f"probsT{k}", [P, 512]) for k in range(2)]
        nmax = [sb(f"nmax{k}", [P, 4]) for k in range(2)]
        sums = {k: sb(f"sums{k}", [P, QT_N, H]) for k in "AB"}
        rinv = {k: sb(f"rinv{k}", [P, QT_N, H]) for k in "AB"}
        rT = sb("rT", [H, S])
        rexp = sb("rexp", [P, DC, S])
        oT = sb("oT", [P, DC, S])
        rows = sb("rows", [P, TOPK, QT_N, ROW])
        stats = {k: sb(f"stats{k}", [P, QT_N, 6]) for k in "AB"}
        mv = {k: sb(f"mv{k}", [P, QT_N, 2]) for k in "AB"}
        var = {k: sb(f"var{k}", [P, QT_N]) for k in "AB"}
        rstd = {k: sb(f"rstd{k}", [P, QT_N]) for k in "AB"}
        lg = sb("logits", [P, QT_N, E])
        top = sb("top", [P, QT_N, 8])
        topi = sb("topi", [P, QT_N, 8], U32)
        topf = sb("topf", [P, QT_N, TOPK])
        ntop = sb("ntop", [P, QT_N])
        etop = sb("etop", [P, QT_N, 8])
        esum = sb("esum", [P, QT_N])
        erec = sb("erec", [P, QT_N])
        pdif = sb("pdif", [P, QT_N])
        pexp = sb("pexp", [P, QT_N])
        den = sb("den", [P, QT_N])
        cw = sb("cw", [P, TOPK, QT_N])
        hot = [sb(f"hot{k}", [P, QT_N, E]) for k in range(TOPK)]
        member = sb("member", [P, QT_N, E], BF16)
        run = sb("run", [P, E])
        run1 = sb("run1", [P, E])
        base = sb("base", [P, E])
        place = sb("place", [P, QT_N, E])
        picked = sb("picked", [P, E])
        slotf = sb("slotf", [P, TOPK, QT_N])
        slot = sb("slot", [P, TOPK, QT_N], U32)
        idf = sb("idf", [P, TOPK, QT_N])

        ident = sb("ident", [P, P])
        identb = sb("identb", [P, P], BF16)
        causal = sb("causal", [P, P], BF16)
        before = sb("before", [P, P], BF16)
        onesb = sb("onesb", [P, P], BF16)
        hmask = sb("hmask", [P, HC])
        spread = sb("spread", [H, DC, P])
        iota8 = sb("iota8", [P, E])
        half = sb("half", [P, QT_N])
        padmeta = sb("padmeta", [P, E + NDUMMY, 2])
        zrow = sb("zrow", [P, D])
        jgrid = sb("jgrid", [P, NBLK])
        nb = sb("nb", [P, E])
        nbi = sb("nbi", [P, E], I32)
        ones8 = sb("ones8", [P, E])
        cum = sb("cum", [P, E])
        blk_row = sb("blk_row", [P, NBLK], I32)
        blk_e = sb("blk_e", [P, NBLK], I32)
        pad_row = sb("pad_row", [P, E], I32)

        bank = [ctx.enter_context(nc.psum_tensor(f"bank{k}", [P, 512], F32)) for k in range(8)]
        s_bank, t_bank, w_bank = bank[0:2], bank[2:4], bank[4:6]
        o_bank = {"A": bank[6], "B": bank[7]}

        consts_dve = sem("consts_dve")
        consts_pool = sem("consts_pool")
        pool_own = sem("pool_own")
        pool_late = sem("pool_late")
        dve_own = sem("dve_own")
        dve_moe = sem("dve_moe")
        dve_tail = sem("dve_tail")
        act_own = sem("act_own")
        wA_loaded, wB_loaded, vec_loaded = sem("wA_loaded"), sem("wB_loaded"), sem("vec_loaded")
        rows_loaded = sem("rows_loaded")
        bias_turned, bias_ready = sem("bias_turned"), sem("bias_ready")
        experts_loaded, late_loaded = sem("experts_loaded"), sem("late_loaded")
        x_loaded, ctx_loaded = sem("x_loaded"), sem("ctx_loaded")
        work_filled = sem("work_filled")
        xT_ready, xres_ready = sem("xT_ready"), sem("xres_ready")
        q_ready, kT_ready, kz_ready, vz_ready = sem("q_ready"), sem("kT_ready"), sem("kz_ready"), sem("vz_ready")
        cT_ready, k2T_ready, k2z_ready, v2z_ready = sem("cT_ready"), sem("k2T_ready"), sem("k2z_ready"), sem("v2z_ready")
        x1T_ready, q2_ready, x2T_ready = sem("x1T_ready"), sem("q2_ready"), sem("x2T_ready")
        scores_ready, max_ready, probs_ready = sem("scores_ready"), sem("max_ready"), sem("probs_ready")
        turned = sem("turned")
        probsT_ready = [sem(f"probsT_ready{k}") for k in range(2)]
        values_done = sem("values_done")
        rinv_ready, rT_ready, rexp_ready, oT_ready = ({k: sem(f"{n}{k}") for k in "AB"} for n in
                                                      ("rinv_ready", "rT_ready", "rexp_ready", "oT_ready"))
        var_ready, rstd_ready, z_ready = ({k: sem(f"{n}{k}") for k in "AB"} for n in
                                          ("var_ready", "rstd_ready", "z_ready"))
        x1_ready, x1res_ready, x2_ready, rows_ready = sem("x1_ready"), sem("x1res_ready"), sem("x2_ready"), sem("rows_ready")
        x2_stored = sem("x2_stored")
        rmax_ready, rexps_ready, pdif_ready, pexp_ready = sem("rmax_ready"), sem("rexps_ready"), sem("pdif_ready"), sem("pexp_ready")
        held = {k: sem(f"held_{k}") for k in ("pool", "dve")}
        sum_ready = {k: sem(f"sum_ready{k}") for k in "AB"}
        logits_ready, places_ready = sem("logits_ready"), sem("places_ready")
        member_ready, slots_ready = sem("member_ready"), sem("slots_ready")
        dispatched = sem("dispatched_rows")
        dummies_written, pads_written, tables_ready = sem("dummies_written"), sem("pads_written"), sem("tables_ready")
        blk_loaded = [sem(f"blk_loaded{k}") for k in range(RING)]
        y_written = [sem(f"y_written{k}") for k in range(RING)]
        xbT_filled, xbT_ready = sem("xbT_filled"), sem("xbT_ready")
        h_filled, h_ready = sem("h_filled"), sem("h_ready")
        hT_filled, gelu_ready = sem("hT_filled"), sem("gelu_ready")
        yb_filled, y_ready = sem("yb_filled"), sem("y_ready")
        parts_loaded = [sem(f"parts_loaded{k}") for k in range(2)]
        tail_var, tail_rstd, tail_z, tail_out = sem("tail_var"), sem("tail_rstd"), sem("tail_z"), sem("tail_out")
        out_written = [sem(f"out_written{k}") for k in range(2)]

        w1_flat = w1[:, :, :, :].rearrange("p k e f -> p (k e f)")
        G = QT_N * D
        tail_y = [w1_flat[:, 3 * G * s:3 * G * s + 2 * G].rearrange("p (k t d) -> p k t d", k=TOPK, t=QT_N) for s in range(2)]
        tail_x = [w1_flat[:, 3 * G * s + 2 * G:3 * G * s + 3 * G].rearrange("p (t d) -> p t d", t=QT_N) for s in range(2)]

        taken = {"xT": xT_ready, "q": q_ready, "k": kT_ready, "v": vz_ready, "cT": cT_ready, "k2": k2T_ready, "v2": v2z_ready, "x1T": x1T_ready,
                 "q2": q2_ready, "x2T": x2T_ready, "route": logits_ready, "rank": places_ready}
        for k in "AB":
            taken.update({"rT" + k: rT_ready[k], "R" + k: rexp_ready[k], "wo" + k: sum_ready[k]})

        block = ctx.enter_context(nc.Block())

        def u_at(what):
            kind, b, m = what
            return kind, b, m, m if kind == "A" else UA + m

        def turns_on(kind, m):
            return "act" if kind == "B" or m % 3 == 2 else "dve"

        NL = B - 1

        @block.sync
        def _(sp):
            def load_x(b):
                sp.dma_start(x_in, t["x"][bass.ds(b, 1), :, :].rearrange("a (t p) d -> p (a t) d", p=P)).then_inc(x_loaded, 16)

            def load_ctx(b):
                sp.dma_start(ctx_in[:, :], t["ctx"][bass.ds(b, 1), :, :].rearrange("a s d -> s (a d)")).then_inc(ctx_loaded, 16)

            load_x(0)
            for k in ("wq", "wk", "wv", "wo"):
                sp.dma_start(wA[k], t[f"sa_{k}"].rearrange("(k p) n -> p k n", p=P)).then_inc(wA_loaded, 16)
                if k == "wq":
                    for n, v in enumerate(("sa_bq", "sa_bk", "ca_bq", "ca_bk")):
                        sp.dma_start(bias_rows[DC * n:DC * n + DC, :], t[v].rearrange("(c p) -> c p", p=P)).then_inc(rows_loaded, 16)
                    sp.dma_start(b1_rows[:, :], t["e_b1"].rearrange("e (f p) -> (e f) p", p=P)).then_inc(rows_loaded, 16)
            for k, v in (("bvA", "sa_bv"), ("boA", "sa_bo"), ("g1", "ln1_g"), ("be1", "ln1_b"), ("bvB", "ca_bv"), ("boB", "ca_bo"),
                         ("g2", "ln2_g"), ("be2", "ln2_b"), ("g3", "ln3_g"), ("be3", "ln3_b")):
                sp.dma_start(vecs[k][:, :], t[v].rearrange("(a n) -> a n", a=1).to_broadcast([P, D])).then_inc(vec_loaded, 16)
            sp.dma_start(rb[:, :], t["router_b"].rearrange("(a n) -> a n", a=1).to_broadcast([P, E])).then_inc(vec_loaded, 16)
            load_ctx(0)
            for k in ("wq", "wk", "wv", "wo"):
                sp.dma_start(wB[k][:, :, :], t[f"ca_{k}"].rearrange("(k p) n -> p k n", p=P)).then_inc(wB_loaded, 16)
            sp.dma_start(rw[:, :, :], t["router_w"].rearrange("(k p) n -> p k n", p=P)).then_inc(wB_loaded, 16)
            sp.wait_ge(consts_pool, 1)
            sp.wait_ge(consts_dve, 1)
            dummy = xs_dram[E * REGION:XS_ROWS, :].rearrange("(n p) d -> p n d", p=P)
            for n in range(NDUMMY):
                sp.dma_start(dummy[:, n, 0:D], zrow[:, :]).then_inc(dummies_written, 16)
            sp.dma_start(dummy[:, :, D:ROW], padmeta[:, E:E + NDUMMY, :]).then_inc(dummies_written, 16)

            sp.wait_ge(xT_ready, 1)
            sp.wait_ge(xres_ready, 1)
            load_x(1)
            with sp.Fori(0, NL - 1) as i:
                sp.wait_ge(xT_ready, i + 2)
                sp.wait_ge(xres_ready, i + 2)
                load_x(i + 2)
                sp.wait_ge(cT_ready, i + 1)
                load_ctx(i + 1)
                sp.wait_ge(x2_ready, i + 1)
                sp.dma_start(x2_dram[bass.ds(i * S, S), :].rearrange("(t p) d -> p t d", p=P), rows[:, 0, :, 0:D]).then_inc(x2_stored, 16)
            sp.wait_ge(cT_ready, NL)
            load_ctx(NL)
            sp.wait_ge(x2_ready, NL)
            sp.dma_start(x2_dram[(NL - 1) * S:NL * S, :].rearrange("(t p) d -> p t d", p=P), rows[:, 0, :, 0:D]).then_inc(x2_stored, 16)
            sp.wait_ge(scores_ready, UNITS * NL + UA)
            for e in (E - 2, E - 1):
                sp.dma_start(w2[:, e, :, :], t["e_w2"][e, :, :].rearrange("(f p) n -> p f n", p=P)).then_inc(late_loaded, 16)
            sp.wait_ge(x2_ready, B)
            sp.dma_start(x2_dram[NL * S:B * S, :].rearrange("(t p) d -> p t d", p=P), rows[:, 0, :, 0:D]).then_inc(x2_stored, 16)

            sp.wait_ge(tables_ready, 1)
            for e in range(E):
                r = sp.value_load(pad_row[0:1, e:e + 1], min_val=e * REGION, max_val=e * REGION + T)
                sp.dma_start(xs_dram[bass.ds(r, P), 0:D], zrow[:, :]).then_inc(pads_written, 16)
                sp.dma_start(xs_dram[bass.ds(r, P), D:ROW], padmeta[:, e, :]).then_inc(pads_written, 16)
            sp.wait_ge(dummies_written, 16 * (NDUMMY + 1))
            sp.wait_ge(pads_written, 16 * 2 * E)
            sp.wait_ge(dispatched, 16 * QT_N * TOPK * B)

            def load_block(j, slot_):
                r = sp.value_load(blk_row[0:1, bass.ds(j, 1)], min_val=0, max_val=XS_ROWS - P)
                e = sp.value_load(blk_e[0:1, bass.ds(j, 1)], min_val=0, max_val=E - 1)
                sp.dma_start(xb[slot_], xs_dram[bass.ds(r, P), :]).then_inc(blk_loaded[slot_], 16)
                sp.dma_start(b2b[slot_], t["e_b2"][bass.ds(e, 1), :].to_broadcast([P, D])).then_inc(blk_loaded[slot_], 16)

            for j in range(RING):
                load_block(j, j)
            with sp.Fori(0, (NBLK - RING) // RING) as i:
                for s in range(RING):
                    sp.wait_ge(y_written[s], 16 * i + 16)
                    load_block(i * RING + RING + s, s)
            for j in range(NBLK // RING * RING, NBLK):
                sp.wait_ge(y_written[j % RING], 16 * (j // RING))
                load_block(j, j % RING)

            for s in range(RING):
                sp.wait_ge(y_written[s], 16 * len(range(s, NBLK, RING)))
            sp.wait_ge(x2_stored, 16 * B)

            def load_parts(g, s):
                for k in range(TOPK):
                    sp.dma_start(tail_y[s][:, k, :, :], y_dram[bass.ds(g * S + k * T, S), :].rearrange("(t p) d -> p t d", p=P)).then_inc(parts_loaded[s], 16)
                sp.dma_start(tail_x[s], x2_dram[bass.ds(g * S, S), :].rearrange("(t p) d -> p t d", p=P)).then_inc(parts_loaded[s], 16)

            def store(g, s):
                sp.dma_start(out[bass.ds(g, 1), :, :].rearrange("a (t p) d -> p (a t) d", p=P), tail_x[s]).then_inc(out_written[s], 16)

            load_parts(0, 0)
            load_parts(1, 1)
            with sp.Fori(0, B // 2 - 1) as i:
                for s in range(2):
                    sp.wait_ge(tail_out, 2 * i + s + 1)
                    store(2 * i + s, s)
                    sp.wait_ge(out_written[s], 16 * i + 16)
                    load_parts(2 * i + s + 2, s)
            for s in range(2):
                sp.wait_ge(tail_out, B - 2 + s + 1)
                store(B - 2 + s, s)
            for s in range(2):
                sp.wait_ge(out_written[s], 16 * (B // 2))

        @block.tensor
        def _(pe):
            def open_bank(w):
                if w.had is not None:
                    name, b = w.had
                    pe.wait_ge(taken[name], b + 1)
                return w_bank[w.bank]

            def turn4(w, src):
                o = open_bank(w)
                for c in range(DC):
                    for tt in range(QT_N):
                        last = nc.tensor.transpose(o[:, c * S + tt * P:c * S + tt * P + P], src[:, tt, c * P:c * P + P], ident[:, :])
                last.then_inc(work_filled, 1)

            def across(w, wt, src, n):
                o = open_bank(w)
                for c in range(DC):
                    for k in range(DC):
                        last = nc.tensor.matmul(o[:, c * n:c * n + n], wt[:, k, c * P:c * P + P], src[:, k, :], start=k == 0, stop=k == DC - 1)
                last.then_inc(work_filled, 1)

            def along(w, wt, src):
                o = open_bank(w)
                for tt in range(QT_N):
                    for k in range(DC):
                        last = nc.tensor.matmul(o[:, tt * D:tt * D + D], src[:, k, tt * P:tt * P + P], wt[:, k, :], start=k == 0, stop=k == DC - 1)
                last.then_inc(work_filled, 1)

            def scores(what):
                kind, b, m, first = u_at(what)
                if not (isinstance(b, int) and UNITS * b + first < 2):
                    pe.wait_ge(probs_ready, b * UNITS + (first - 1))
                o = s_bank[first % 2]
                if kind == "A":
                    c, q, heads, keys = a_unit(m)
                    if m == 0:
                        pe.wait_ge(q_ready, b + 1)
                        pe.wait_ge(kz_ready, b + 1)
                    n = len(heads)
                    o3 = o[:, :].rearrange("p (h k) -> p h k", h=n)
                    nc.tensor.matmul(o3, qT[:, c, q * P:q * P + P], kz[:, c, heads[0]:heads[0] + n, 0:keys], start=True, stop=False)
                    nc.tensor.matmul(o3[:, :, keys - P:keys], identb[:, :], causal[:, None, :].to_broadcast([P, n, P]),
                                     start=False, stop=True).then_inc(scores_ready, 1)
                else:
                    c, q, heads = b_unit(m)
                    if m == 0:
                        pe.wait_ge(q2_ready, b + 1)
                        pe.wait_ge(k2z_ready, b + 1)
                    nc.tensor.matmul(o[:, 0:4 * SE].rearrange("p (h k) -> p h k", h=4), q2T[:, c, q * P:q * P + P],
                                     k2z[:, c, heads[0]:heads[0] + 4, :], start=True, stop=True).then_inc(scores_ready, 1)

            def turn(what):
                kind, b, m, first = u_at(what)
                pe.wait_ge(probs_ready, b * UNITS + (first + 1))
                o, p = t_bank[first % 2], probs[first % 2]
                for j in range(4):
                    if kind == "A":
                        last = nc.tensor.transpose(o[:, j * P:j * P + P], p[:, j * P:j * P + P], ident[:, :])
                    else:
                        last = nc.tensor.transpose(o[0:SE, j * P:j * P + P], p[:, j * SE:j * SE + SE], ident[:, :])
                last.then_inc(turned, 1)

            def values(what):
                kind, b, m, first = u_at(what)
                pe.wait_ge(probsT_ready[first % 2], b * (UNITS // 2) + (first // 2 + 1))
                p, o = probsT[first % 2], o_bank[kind]
                if m == 0:
                    pe.wait_ge(vz_ready if kind == "A" else v2z_ready, b + 1)
                    if not (isinstance(b, int) and b == 0):
                        pe.wait_ge(oT_ready[kind], b)
                if kind == "A":
                    c, q, heads, keys = a_unit(m)
                    n = keys // P
                    for kt in range(n):
                        for a, s_ in enumerate(heads):
                            par, strip, h = s_ // STRIPS, s_ % STRIPS, head_of(c, s_)
                            last = nc.tensor.matmul(o[32 * strip:32 * strip + 32, c * S + q * P:c * S + q * P + P],
                                                    vz[:, kt, 32 * h:32 * h + 32], p[:, (a * n + kt) * P:(a * n + kt) * P + P],
                                                    start=par == 0 and kt == 0, stop=par == 1 and kt == n - 1)
                else:
                    c, q, heads = b_unit(m)
                    for a, s_ in enumerate(heads):
                        par, strip, h = s_ // STRIPS, s_ % STRIPS, head_of(c, s_)
                        last = nc.tensor.matmul(o[32 * strip:32 * strip + 32, c * S + q * P:c * S + q * P + P],
                                                v2z[:, 32 * h:32 * h + 32], p[0:SE, a * P:a * P + P], start=par == 0, stop=par == 1)
                last.then_inc(values_done, 1)

            def rows_of_rinv(w, k, b):
                o = open_bank(w)
                pe.wait_ge(rinv_ready[k], b + 1)
                for q in range(QT_N):
                    last = nc.tensor.transpose(o[0:H, q * P:q * P + P], rinv[k][:, q, :], ident[:, :])
                last.then_inc(work_filled, 1)

            def spread_rinv(w, k, b):
                o = open_bank(w)
                pe.wait_ge(rT_ready[k], b + 1)
                for c in range(DC):
                    last = nc.tensor.matmul(o[:, c * S:c * S + S], spread[:, c, :], rT[:, :], start=True, stop=True)
                last.then_inc(work_filled, 1)

            pe.wait_ge(consts_pool, 1)
            pe.wait_ge(consts_dve, 1)
            pe.wait_ge(rows_loaded, 16 * 5)
            nc.tensor.transpose(o_bank["A"][:, 0:4 * DC], bias_rows[:, :], ident[0:4 * DC, 0:4 * DC])
            nc.tensor.transpose(o_bank["B"][:, 0:E * FC], b1_rows[:, :], ident[0:E * FC, 0:E * FC]).then_inc(bias_turned, 1)

            scope = ExitStack()
            for name, what, w in batch_script(lambda: scope.enter_context(pe.Fori(0, NL))):
                if name == "enter":
                    pe.wait_ge(wB_loaded, 16 * 5)
                elif name == "leave":
                    scope.close()
                elif name == "xT":
                    pe.wait_ge(x_loaded, what * 16 + 16)
                    turn4(w, x_in)
                elif name in ("q", "k"):
                    if w.filled is not None and isinstance(what, int) and what == 0 and name == "q":
                        pe.wait_ge(wA_loaded, 16 * 4)
                    pe.wait_ge(xT_ready, what + 1)
                    across(w, wA["w" + name], xT, S)
                elif name == "v":
                    along(w, wA["wv"], xT)
                elif name == "cT":
                    o = open_bank(w)
                    pe.wait_ge(ctx_loaded, what * 16 + 16)
                    for c in range(DC):
                        last = nc.tensor.transpose(o[:, c * SE:c * SE + SE], ctx_in[:, c * P:c * P + P], ident[0:SE, 0:SE])
                    last.then_inc(work_filled, 1)
                elif name == "k2":
                    pe.wait_ge(cT_ready, what + 1)
                    across(w, wB["wk"], cT, SE)
                elif name == "v2":
                    o = open_bank(w)
                    for k in range(DC):
                        last = nc.tensor.matmul(o[0:SE, 0:D], cT[:, k, :], wB["wv"][:, k, :], start=k == 0, stop=k == DC - 1)
                    last.then_inc(work_filled, 1)
                elif name == "x1T":
                    pe.wait_ge(x1_ready, what + 1)
                    turn4(w, x1)
                elif name == "q2":
                    pe.wait_ge(x1T_ready, what + 1)
                    across(w, wB["wq"], xT, S)
                elif name == "x2T":
                    pe.wait_ge(x2_ready, what + 1)
                    turn4(w, rows[:, 0, :, :])
                elif name == "route":
                    o = open_bank(w)
                    pe.wait_ge(x2T_ready, what + 1)
                    for tt in range(QT_N):
                        for k in range(DC):
                            last = nc.tensor.matmul(o[:, tt * E:tt * E + E], xT[:, k, tt * P:tt * P + P], rw[:, k, :], start=k == 0, stop=k == DC - 1)
                    last.then_inc(work_filled, 1)
                elif name == "rank":
                    o = open_bank(w)
                    pe.wait_ge(member_ready, what + 1)
                    m = member[:, :, :].rearrange("p t e -> p (t e)")
                    nc.tensor.matmul(o[:, 0:QT_N * E], before[:, :], m, start=True, stop=True)
                    nc.tensor.matmul(o[:, QT_N * E:2 * QT_N * E], onesb[:, :], m, start=True, stop=True).then_inc(work_filled, 1)
                elif name in ("rTA", "rTB"):
                    rows_of_rinv(w, name[-1], what)
                elif name in ("RA", "RB"):
                    spread_rinv(w, name[-1], what)
                elif name in ("woA", "woB"):
                    pe.wait_ge(oT_ready[name[-1]], what + 1)
                    along(w, (wA if name == "woA" else wB)["wo"], oT)
                elif name == "scores":
                    scores(what)
                elif name == "turn":
                    turn(what)
                elif name == "values":
                    values(what)

            h_bank, g_bank, x_bank, y_bank = bank[0:2], bank[2:4], bank[4], bank[6:8]

            def block_T(j, s):
                pe.wait_ge(blk_loaded[s], 32 * (j // RING) + 32 if isinstance(j, int) else j[1] * 32 + j[2] // RING * 32 + 32)

            def jval(j, add):
                return j + add if isinstance(j, int) else j[1] * RING + (j[2] + add)

            def turn_x(j):
                n = j if isinstance(j, int) else j[2]
                s = n % RING
                block_T(j, s)
                if n > 0:
                    pe.wait_ge(xbT_ready, jval(j, 0))
                for c in range(DC):
                    last = nc.tensor.transpose(x_bank[:, c * P:c * P + P], xb[s][:, c * P:c * P + P], ident[:, :])
                last.then_inc(xbT_filled, 1)

            def load_e(j):
                return pe.value_load(blk_e[0:1, bass.ds(jval(j, 0), 1)], min_val=0, max_val=E - 1)

            def up(j, half_, e):
                n = j if isinstance(j, int) else j[2]
                if half_ == 0:
                    pe.wait_ge(xbT_ready, jval(j, 1))
                if n > 0:
                    pe.wait_ge(h_ready, 2 * jval(j, -1) + half_ + 1)
                for k in range(DC):
                    last = nc.tensor.matmul(h_bank[half_][:, :], xbT[:, k, :], w1[:, k, bass.ds(e, 1), half_ * 512:half_ * 512 + 512],
                                            start=k == 0, stop=k == DC - 1)
                last.then_inc(h_filled, 1)

            def turn_h(j):
                n = j if isinstance(j, int) else j[2]
                pe.wait_ge(h_ready, 2 * jval(j, 1))
                if n > 0:
                    pe.wait_ge(gelu_ready, jval(j, 0))
                for f in range(FC):
                    last = nc.tensor.transpose(g_bank[f // 4][:, f % 4 * P:f % 4 * P + P], hid[:, f * P:f * P + P], ident[:, :])
                last.then_inc(hT_filled, 1)

            def down(j, e):
                n = j if isinstance(j, int) else j[2]
                pe.wait_ge(gelu_ready, jval(j, 1))
                if n > 1:
                    pe.wait_ge(y_ready, jval(j, -1))
                for f in range(FC):
                    last = nc.tensor.matmul(y_bank[n % 2][:, 0:D], gT[:, f, :], w2[:, bass.ds(e, 1), f, :], start=f == 0, stop=f == FC - 1)
                last.then_inc(yb_filled, 1)

            def step(j, prev, nxt):
                turn_h(prev)
                e = load_e(j)
                up(j, 0, e)
                up(j, 1, e)
                if nxt is not None:
                    turn_x(nxt)
                down(prev, load_e(prev))

            pe.wait_ge(tables_ready, 1)
            pe.wait_ge(experts_loaded, 16 * (2 * E - 2))
            pe.wait_ge(late_loaded, 16 * 2)
            turn_x(0)
            e0 = load_e(0)
            up(0, 0, e0)
            up(0, 1, e0)
            turn_x(1)
            turns = (NBLK - 2) // RING
            with pe.Fori(0, turns) as i:
                for s in range(RING):
                    step(("loop", i, s + 1), ("loop", i, s), ("loop", i, s + 2))
            for j in range(turns * RING + 1, NBLK):
                step(j, j - 1, j + 1 if j + 1 < NBLK else None)
            turn_h(NBLK - 1)
            down(NBLK - 1, load_e(NBLK - 1))

        @block.scalar
        def _(act):
            for e in range(E):
                act.dma_start(w1[:, :, e, :], t["e_w1"][e, :, :].rearrange("(k p) n -> p k n", p=P)).then_inc(experts_loaded, 16)
                if e < E - 2:
                    act.dma_start(w2[:, e, :, :], t["e_w2"][e, :, :].rearrange("(f p) n -> p f n", p=P)).then_inc(experts_loaded, 16)
            act.wait_ge(bias_turned, 1)
            nc.scalar.copy(bias[:, :], o_bank["A"][:, 0:4 * DC])
            nc.scalar.copy(b1[:, :], o_bank["B"][:, 0:E * FC]).then_inc(bias_ready, 1)
            act.wait_ge(bias_ready, 1)

            def shifted(w, dst, n, col):
                act.wait_ge(work_filled, w.filled)
                for c in range(DC):
                    last = nc.scalar.activation(dst[:, c, :], w_bank[w.bank][:, c * n:c * n + n], ACT.Identity, bias=bias[:, col + c:col + c + 1])
                return last

            flat = lambda x: x[:, :, :].rearrange("p c n -> p (c n)")
            scope = ExitStack()
            for name, what, w in batch_script(lambda: scope.enter_context(act.Fori(0, NL))):
                b = what
                if name == "leave":
                    scope.close()
                elif name in ("xT", "x1T", "x2T"):
                    ready = {"xT": xT_ready, "x1T": x1T_ready, "x2T": x2T_ready}[name]
                    act.wait_ge(work_filled, w.filled)
                    ins = nc.scalar.copy(flat(xT), w_bank[w.bank][:, :])
                    ins.then_inc(ready, 1)
                elif name == "k":
                    if not (isinstance(b, int) and b == 0):
                        act.wait_ge(kz_ready, b)
                    ins = shifted(w, kT, S, DC)
                    ins.then_inc(kT_ready, 1)
                elif name == "cT":
                    act.wait_ge(work_filled, w.filled)
                    ins = nc.scalar.copy(flat(cT), w_bank[w.bank][:, 0:DC * SE])
                    ins.then_inc(cT_ready, 1)
                elif name == "k2":
                    if not (isinstance(b, int) and b == 0):
                        act.wait_ge(k2z_ready, b)
                    ins = shifted(w, k2T, SE, 3 * DC)
                    ins.then_inc(k2T_ready, 1)
                elif name in ("rTA", "rTB"):
                    act.wait_ge(work_filled, w.filled)
                    ins = nc.scalar.copy(rT[:, :], w_bank[w.bank][0:H, 0:S])
                    ins.then_inc(rT_ready[name[-1]], 1)
                elif name in ("RA", "RB"):
                    act.wait_ge(work_filled, w.filled)
                    ins = nc.scalar.copy(flat(rexp), w_bank[w.bank][:, :])
                    ins.then_inc(rexp_ready[name[-1]], 1)
                elif name == "scores":
                    kind, b, m, first = u_at(what)
                    act.wait_ge(max_ready, b * UNITS + (first + 1))
                    p = probs[first % 2]
                    if kind == "A":
                        c, q, heads, keys = a_unit(m)
                        for a, s_ in enumerate(heads):
                            h = head_of(c, s_)
                            last = nc.scalar.activation(p[:, a * keys:a * keys + keys], s_bank[first % 2][:, a * keys:a * keys + keys], ACT.Exp,
                                                        bias=nmax[first % 2][:, a:a + 1], accum_out=sums["A"][:, q, h:h + 1])
                        last.then_inc(probs_ready, 1)
                    else:
                        nc.scalar.activation(p[:, 0:4 * SE], p[:, 0:4 * SE], ACT.Exp).then_inc(probs_ready, 1)
                elif name == "turn":
                    kind, b, m, first = u_at(what)
                    if turns_on(kind, m) == "act":
                        act.wait_ge(turned, b * UNITS + (first + 1))
                        n = P if kind == "A" else SE
                        nc.scalar.copy(probsT[first % 2][0:n, :], t_bank[first % 2][0:n, :]).then_inc(probsT_ready[first % 2], 1)
                elif name == "route":
                    act.wait_ge(rmax_ready, b + 1)
                    for tt in range(QT_N):
                        last = nc.scalar.activation(etop[:, tt, :], top[:, tt, :], ACT.Exp, bias=ntop[:, tt:tt + 1], accum_out=esum[:, tt:tt + 1])
                    last.then_inc(rexps_ready, 1)
                    act.wait_ge(pdif_ready, b + 1)
                    nc.scalar.activation(pexp[:, :], pdif[:, :], ACT.Exp).then_inc(pexp_ready, 1)

            h_bank, g_bank, x_bank, y_bank = bank[0:2], bank[2:4], bank[4], bank[6:8]

            def jv(j, add):
                return j + add if isinstance(j, int) else j[1] * RING + (j[2] + add)

            def take_x(j):
                act.wait_ge(xbT_filled, jv(j, 1))
                nc.scalar.copy(xbT.rearrange("p c n -> p (c n)"), x_bank[:, 0:D]).then_inc(xbT_ready, 1)

            def gelu(j):
                e = act.value_load(blk_e[0:1, bass.ds(jv(j, 0), 1)], min_val=0, max_val=E - 1)
                act.wait_ge(hT_filled, jv(j, 1))
                for f in range(FC):
                    last = nc.scalar.activation(gT[:, f, :], g_bank[f // 4][:, f % 4 * P:f % 4 * P + P], ACT.Gelu, bias=b1[:, bass.ds(e * FC + f, 1)])
                last.then_inc(gelu_ready, 1)

            act.wait_ge(tables_ready, 1)
            take_x(0)
            take_x(1)
            turns = (NBLK - 2) // RING
            with act.Fori(0, turns) as i:
                for s in range(RING):
                    gelu(("loop", i, s))
                    take_x(("loop", i, s + 2))
            for j in range(turns * RING, NBLK):
                gelu(j)
                if j + 2 < NBLK:
                    take_x(j + 2)

        @block.gpsimd
        def _(pool):
            own = Chain(pool, pool_own, POOL_LINKS, NL)
            gp = nc.gpsimd
            own.link(gp.memset(ident[:, :], 0.0))
            own.link(gp.affine_select(out=ident[:, :], in_=ident[:, :], compare_op=ALU.not_equal, fill=1.0, base=0, pattern=[[-1, P]], channel_multiplier=1))
            own.link(gp.memset(identb[:, :], 0.0))
            own.link(gp.affine_select(out=identb[:, :], in_=identb[:, :], compare_op=ALU.not_equal, fill=1.0, base=0, pattern=[[-1, P]], channel_multiplier=1))
            own.link(gp.memset(causal[:, :], 0.0))
            own.link(gp.affine_select(out=causal[:, :], in_=causal[:, :], compare_op=ALU.is_ge, fill=MASKED, base=0, pattern=[[-1, P]], channel_multiplier=1))
            own.link(gp.memset(before[:, :], 1.0))
            own.link(gp.affine_select(out=before[:, :], in_=before[:, :], compare_op=ALU.is_gt, fill=0.0, base=0, pattern=[[1, P]], channel_multiplier=-1))
            hm = hmask[:, :].rearrange("p (a s) -> p a s", a=2)
            own.link(gp.memset(hmask[:, :], 1.0))
            own.link(gp.affine_select(out=hm, in_=hm, compare_op=ALU.is_ge, fill=0.0, base=0, pattern=[[-HD, 2], [-2 * HD, STRIPS]], channel_multiplier=1))
            own.link(gp.affine_select(out=hm, in_=hm, compare_op=ALU.is_ge, fill=0.0, base=HD - 1, pattern=[[HD, 2], [2 * HD, STRIPS]], channel_multiplier=-1))
            own.link(gp.memset(spread[:, :, :], 1.0))
            own.link(gp.affine_select(out=spread[:, :, :], in_=spread[:, :, :], compare_op=ALU.is_ge, fill=0.0, base=0, pattern=[[P, DC], [1, P]], channel_multiplier=-HD))
            own.link(gp.affine_select(out=spread[:, :, :], in_=spread[:, :, :], compare_op=ALU.is_ge, fill=0.0, base=HD - 1, pattern=[[-P, DC], [-1, P]], channel_multiplier=HD))
            own.link(gp.iota(iota8[:, :], pattern=[[1, E]], base=0, channel_multiplier=0, allow_small_or_imprecise_dtypes=True))
            own.link(gp.iota(base[:, :], pattern=[[REGION, E]], base=0, channel_multiplier=0, allow_small_or_imprecise_dtypes=True))
            own.link(gp.iota(run[:, :], pattern=[[REGION, E]], base=0, channel_multiplier=0, allow_small_or_imprecise_dtypes=True))
            own.link(gp.iota(idf[:, :, :], pattern=[[T, TOPK], [P, QT_N]], base=0, channel_multiplier=1, allow_small_or_imprecise_dtypes=True))
            own.link(gp.iota(jgrid[:, :], pattern=[[1, NBLK]], base=0, channel_multiplier=0, allow_small_or_imprecise_dtypes=True))
            own.link(gp.memset(padmeta[:, :, :], 0.0))
            gp.iota(padmeta[:, :, 0:1].bitcast(I32), pattern=[[P, E + NDUMMY], [0, 1]], base=Y_PAD, channel_multiplier=1).then_inc(consts_pool, 1)

            def two(x):
                return x[:, None, :].to_broadcast([P, QT_N, D])

            pool.wait_ge(vec_loaded, 16 * 11)
            scope = ExitStack()
            inside = []

            def loop():
                i = scope.enter_context(pool.Fori(0, NL))
                own.enter(i)
                return i

            for name, what, w in batch_script(loop):
                b = what
                first = isinstance(b, int) and b == 0
                if name == "leave":
                    own.leave()
                    scope.close()
                elif name == "xT":
                    pool.wait_ge(x_loaded, b * 16 + 16)
                    if not first:
                        pool.wait_ge(var_ready["A"], b)
                    gp.tensor_tensor(xres, x_in, two(vecs["boA"]), ALU.add).then_inc(xres_ready, 1)
                elif name in ("k", "k2"):
                    src, dst, n, got, put = (kT, kz, S, kT_ready, kz_ready) if name == "k" else (k2T, k2z, SE, k2T_ready, k2z_ready)
                    pool.wait_ge(got, b + 1)
                    for c in range(DC):
                        last = gp.tensor_tensor(dst[:, c, :, :], src[:, c, None, :].to_broadcast([P, HC, n]), hmask[:, :, None].to_broadcast([P, HC, n]), ALU.mult)
                    last.then_inc(put, 1)
                elif name in ("woA", "woB"):
                    k = name[-1]
                    pool.wait_ge(var_ready[k], b + 1)
                    gp.tensor_tensor(rstd[k][:, :], var[k][:, :], half[:, :], ALU.pow).then_inc(rstd_ready[k], 1)
                    y, g, be = (y_a, "g1", "be1") if k == "A" else (y_b, "g2", "be2")
                    pool.wait_ge(z_ready[k], b + 1)
                    own.link(gp.tensor_tensor(y if k == "A" else y[:, :, :], y if k == "A" else y[:, :, :], two(vecs[g]), ALU.mult))
                    if k == "A":
                        ins = gp.tensor_tensor(x1[:, :, :], y_a, two(vecs["be1"]), ALU.add)
                        ins.then_inc(x1_ready, 1)
                        pool.wait_ge(x1_ready, b + 1)
                        gp.tensor_tensor(x1res[:, :, :], x1[:, :, :], two(vecs["boB"]), ALU.add).then_inc(x1res_ready, 1)
                    else:
                        if not first:
                            pool.wait_ge(dispatched, b * (16 * QT_N * TOPK))
                            pool.wait_ge(x2_stored, b * 16)
                        gp.tensor_tensor(rows[:, 0, :, 0:D], y_b[:, :, :], two(vecs["be2"]), ALU.add).then_inc(x2_ready, 1)
                        gp.tensor_tensor(rows[:, 1, :, 0:D], y_b[:, :, :], two(vecs["be2"]), ALU.add).then_inc(rows_ready, 1)
                elif name == "rank":
                    pool.wait_ge(slots_ready, b + 1)
                    pool.wait_ge(rows_ready, b + 1)
                    pool.sem_inc(held["pool"], 1)
                    for k in range(TOPK):
                        for tt in range(QT_N):
                            gp.indirect_dma_start(out=xs_dram, out_offset=bass.IndirectOffsetOnAxis(ap=slot[:, k, tt:tt + 1], axis=0),
                                                  in_=rows[:, k, tt, :], in_offset=None).then_inc(dispatched, 16)

            def put(j):
                n = j if isinstance(j, int) else j[2]
                s = n % RING
                pool.wait_ge(y_ready, j + 1 if isinstance(j, int) else j[1] * RING + (j[2] + 1))
                pool.sem_inc(held["pool"], 1)
                gp.indirect_dma_start(out=y_dram, out_offset=bass.IndirectOffsetOnAxis(ap=xb[s][:, D:D + 1].bitcast(U32), axis=0),
                                      in_=xb[s][:, 0:D], in_offset=None).then_inc(y_written[s], 16)

            turns = NBLK // RING
            with pool.Fori(0, turns) as i:
                for s in range(RING):
                    put(("loop", i, s))
            for j in range(turns * RING, NBLK):
                put(j)

            late = Chain(pool, pool_late, 2, B // 2)

            def finish(n, g, s):
                pool.wait_ge(tail_var, n)
                gp.tensor_tensor(rstd["A"][:, :], var["A"][:, :], half[:, :], ALU.pow).then_inc(tail_rstd, 1)
                pool.wait_ge(tail_z, n)
                late.link(gp.tensor_tensor(tail_x[s], tail_x[s], two(vecs["g3"]), ALU.mult))
                gp.tensor_tensor(tail_x[s], tail_x[s], two(vecs["be3"]), ALU.add).then_inc(tail_out, 1)

            with pool.Fori(0, B // 2) as i:
                late.enter(i)
                for s in range(2):
                    finish(2 * i + s + 1, None, s)
                late.leave()

        @block.vector
        def _(dve):
            v = nc.vector
            own = Chain(dve, dve_own, DVE_LINKS, NL)
            v.memset(onesb[:, :], 1.0)
            v.memset(half[:, :], -0.5)
            v.memset(ones8[:, :], 1.0)
            v.memset(vz, 0.0)
            v.memset(v2z[:, :], 0.0)
            v.memset(zrow[:, :], 0.0).then_inc(consts_dve, 1)
            dve.wait_ge(consts_dve, 1)
            dve.wait_ge(consts_pool, 1)
            dve.wait_ge(vec_loaded, 16 * 11)
            dve.wait_ge(bias_ready, 1)

            def norm(k, y, src, res, resem, b, first, w):
                dve.wait_ge(work_filled, w.filled)
                dve.wait_ge(resem, b + 1)
                if not first:
                    dve.wait_ge(x1_ready if k == "A" else x2_ready, b)
                ins = v.tensor_tensor(y, w_bank[w.bank][:, :].rearrange("p (t d) -> p t d", t=QT_N), res, ALU.add)
                ins.then_inc(sum_ready[k], 1)
                dve.wait_ge(sum_ready[k], b + 1)
                for tt in range(QT_N):
                    ins = v.bn_stats(stats[k][:, tt, :], y[:, tt, :])
                own.link(ins)
                dve.sem_inc(held["dve"], 1)
                for tt in range(QT_N):
                    ins = v.bn_aggr(mv[k][:, tt, :], stats[k][:, tt, :])
                own.link(ins)
                v.tensor_scalar(var[k][:, :], mv[k][:, :, 1], EPS, None, ALU.add).then_inc(var_ready[k], 1)
                dve.wait_ge(rstd_ready[k], b + 1)
                for tt in range(QT_N):
                    ins = v.tensor_scalar(y[:, tt, :], y[:, tt, :], mv[k][:, tt, 0:1], rstd[k][:, tt:tt + 1], ALU.subtract, ALU.mult)
                ins.then_inc(z_ready[k], 1)

            def scaled_q(w, dst, col, ready):
                dve.wait_ge(work_filled, w.filled)
                for c in range(DC):
                    ins = v.tensor_scalar(dst[:, c, :], w_bank[w.bank][:, c * S:c * S + S], bias[:, col + c:col + c + 1], HD ** -0.5, ALU.add, ALU.mult)
                ins.then_inc(ready, 1)

            def spread_v(dst, src, bv, n):
                d4 = dst.rearrange("p (s a x) -> p s a x", s=H // 2, a=2)
                s4 = src.rearrange("p (s a x) -> p s a x", s=H // 2, a=2)
                b4 = bv[0:n, :].rearrange("p (s a x) -> p s a x", s=H // 2, a=2)
                for par in range(2):
                    ins = v.tensor_tensor(d4[:, :, par, par * HD:par * HD + HD], s4[:, :, par, :], b4[:, :, par, :], ALU.add)
                return ins

            scope = ExitStack()

            def loop():
                i = scope.enter_context(dve.Fori(0, NL))
                own.enter(i)
                return i

            late_sum = []
            for name, what, w in batch_script(loop):
                b = what
                first = isinstance(b, int) and b == 0
                if name == "leave":
                    own.leave()
                    scope.close()
                elif name == "q":
                    scaled_q(w, qT, 0, q_ready)
                elif name == "q2":
                    scaled_q(w, q2T, 2 * DC, q2_ready)
                elif name == "v":
                    dve.wait_ge(work_filled, w.filled)
                    for tt in range(QT_N):
                        ins = spread_v(vz[:, tt, :], w_bank[w.bank][:, tt * D:tt * D + D], vecs["bvA"], P)
                    ins.then_inc(vz_ready, 1)
                elif name == "v2":
                    dve.wait_ge(work_filled, w.filled)
                    ins = spread_v(v2z[:, :], w_bank[w.bank][0:SE, 0:D], vecs["bvB"], SE)
                    ins.then_inc(v2z_ready, 1)
                elif name == "scores":
                    kind, b, m, start = u_at(what)
                    dve.wait_ge(scores_ready, b * UNITS + (start + 1))
                    nm = nmax[start % 2]
                    if kind == "A":
                        c, q, heads, keys = a_unit(m)
                        n = len(heads)
                        v.tensor_reduce(nm[:, 0:n], s_bank[start % 2][:, :].rearrange("p (h k) -> p h k", h=n), AX, ALU.max, negate=True).then_inc(max_ready, 1)
                    else:
                        s3 = s_bank[start % 2][:, 0:4 * SE].rearrange("p (h k) -> p h k", h=4)
                        own.link(v.tensor_reduce(nm[:, 0:4], s3, AX, ALU.max, negate=True))
                        v.tensor_tensor(probs[start % 2][:, 0:4 * SE].rearrange("p (h k) -> p h k", h=4), s3,
                                        nm[:, 0:4, None].to_broadcast([P, 4, SE]), ALU.add).then_inc(max_ready, 1)
                elif name == "turn":
                    kind, b, m, start = u_at(what)
                    if kind == "B":
                        c, q, heads = b_unit(m)
                        dve.wait_ge(probs_ready, b * UNITS + (start + 1))
                        lo = c * HC + heads[0] // STRIPS
                        own.link(v.tensor_reduce(sums["B"][:, q, lo:c * HC + HC:2], probs[start % 2][:, 0:4 * SE].rearrange("p (h k) -> p h k", h=4), AX, ALU.add))
                    if turns_on(kind, m) == "dve":
                        dve.wait_ge(turned, b * UNITS + (start + 1))
                        v.tensor_copy(probsT[start % 2][:, :], t_bank[start % 2][:, :]).then_inc(probsT_ready[start % 2], 1)
                elif name in ("rTA", "rTB"):
                    k = name[-1]
                    dve.wait_ge(probs_ready, b * UNITS + (UA if k == "A" else UNITS))
                    if not first:
                        dve.wait_ge(rT_ready[k], b)
                    v.reciprocal(rinv[k][:, :, :], sums[k][:, :, :]).then_inc(rinv_ready[k], 1)
                elif name in ("oTA", "oTB"):
                    k = name[-1]
                    dve.wait_ge(rexp_ready[k], b + 1)
                    dve.wait_ge(values_done, b * UNITS + (UA if k == "A" else UNITS))
                    v.tensor_tensor(oT[:, :, :].rearrange("p c n -> p (c n)"), o_bank[k][:, :], rexp[:, :, :].rearrange("p c n -> p (c n)"), ALU.mult).then_inc(oT_ready[k], 1)
                elif name == "woA":
                    norm("A", y_a, None, xres, xres_ready, b, first, w)
                elif name == "woB":
                    norm("B", y_b[:, :, :], None, x1res[:, :, :], x1res_ready, b, first, w)
                elif name == "route":
                    dve.wait_ge(work_filled, w.filled)
                    ins = v.tensor_tensor(lg[:, :, :], w_bank[w.bank][:, 0:QT_N * E].rearrange("p (t e) -> p t e", t=QT_N), rb[:, None, :].to_broadcast([P, QT_N, E]), ALU.add)
                    ins.then_inc(logits_ready, 1)
                    dve.wait_ge(logits_ready, b + 1)
                    dve.sem_inc(held["dve"], 1)
                    for tt in range(QT_N):
                        ins = v.max(top[:, tt, :], lg[:, tt, :])
                    own.link(ins)
                    v.tensor_scalar(ntop[:, :], top[:, :, 0], -1.0, None, ALU.mult).then_inc(rmax_ready, 1)
                    for tt in range(QT_N):
                        ins = v.max_index(topi[:, tt, :], top[:, tt, :], lg[:, tt, :])
                    own.link(ins)
                    own.link(v.tensor_copy(topf[:, :, :], topi[:, :, 0:TOPK]))
                    for k in range(TOPK):
                        for tt in range(QT_N):
                            ins = v.tensor_scalar(hot[k][:, tt, :], iota8[:, :], topf[:, tt, k:k + 1], None, ALU.is_equal)
                    own.link(ins)
                    v.tensor_tensor(member[:, :, :], hot[0][:, :, :], hot[1][:, :, :], ALU.add).then_inc(member_ready, 1)
                    dve.wait_ge(rexps_ready, b + 1)
                    own.link(v.reciprocal(erec[:, :], esum[:, :]))
                    own.link(v.tensor_tensor(pdif[:, :], etop[:, :, 1], etop[:, :, 0], ALU.subtract))
                    ins = v.tensor_tensor(pdif[:, :], pdif[:, :], erec[:, :], ALU.mult)
                    ins.then_inc(pdif_ready, 1)
                    dve.wait_ge(pexp_ready, b + 1)
                    own.link(v.tensor_scalar(den[:, :], pexp[:, :], 1.0, None, ALU.add))
                    own.link(v.reciprocal(cw[:, 0, :], den[:, :]))
                    own.link(v.tensor_tensor(cw[:, 1, :], pexp[:, :], cw[:, 0, :], ALU.mult))
                elif name == "rank":
                    dve.wait_ge(work_filled, w.filled)
                    o = w_bank[w.bank]
                    own.link(v.tensor_tensor(run1[:, :], run[:, :], o[:, 2 * E:3 * E], ALU.add))
                    v.tensor_tensor(place[:, 0, :], o[:, 0:E], run[:, :], ALU.add)
                    own.link(v.tensor_tensor(place[:, 1, :], o[:, E:2 * E], run1[:, :], ALU.add))
                    v.tensor_tensor(run[:, :], run1[:, :], o[:, 3 * E:4 * E], ALU.add).then_inc(places_ready, 1)
                    for k in range(TOPK):
                        for tt in range(QT_N):
                            own.link(v.tensor_tensor(picked[:, :], hot[k][:, tt, :], place[:, tt, :], ALU.mult))
                            own.link(v.tensor_reduce(slotf[:, k, tt:tt + 1], picked[:, :], AX, ALU.add))
                    if not first:
                        dve.wait_ge(dispatched, b * (16 * QT_N * TOPK))
                    v.tensor_copy(slot[:, :, :], slotf[:, :, :])
                    v.tensor_copy(rows[:, :, :, D:D + 1].bitcast(I32), idf[:, :, :, None])
                    own.link(v.tensor_copy(rows[:, :, :, D + 1:D + 2], cw[:, :, :, None]))
                    v.tensor_scalar(idf[:, :, :], idf[:, :, :], float(S), None, ALU.add).then_inc(slots_ready, 1)

            own.link(v.tensor_copy(pad_row[:, :], run[:, :]))
            own.link(v.tensor_tensor(nb[:, :], run[:, :], base[:, :], ALU.subtract))
            own.link(v.tensor_scalar(nb[:, :], nb[:, :], float(P - 1), None, ALU.add))
            own.link(v.tensor_copy(nbi[:, :], nb[:, :]))
            own.link(v.tensor_single_scalar(nbi[:, :], nbi[:, :], P.bit_length() - 1, ALU.arith_shift_right))
            own.link(v.tensor_copy(nb[:, :], nbi[:, :]))
            own.link(v.tensor_tensor_scan(cum[:, :], ones8[:, :], nb[:, :], 0.0, ALU.mult, ALU.add))
            wide = lambda x: x[:, None, :].to_broadcast([P, NBLK, E])
            own.link(v.tensor_tensor(ge, jgrid[:, :, None].to_broadcast([P, NBLK, E]), wide(cum), ALU.is_ge))
            own.link(v.tensor_reduce(blkf, ge, AX, ALU.add))
            own.link(v.tensor_tensor(ge, ge, wide(nb), ALU.mult))
            own.link(v.tensor_reduce(skipped, ge, AX, ALU.add))
            own.link(v.tensor_tensor(skipped, jgrid[:, :], skipped, ALU.subtract))
            own.link(v.tensor_scalar(skipped, skipped, float(P), None, ALU.mult))
            own.link(v.scalar_tensor_tensor(out=blk_row[:, :], in0=blkf, scalar=float(REGION), in1=skipped, op0=ALU.mult, op1=ALU.add))
            v.tensor_scalar(blk_e[:, :], blkf, float(E - 1), None, ALU.min).then_inc(tables_ready, 1)

            h_bank, y_bank = bank[0:2], bank[6:8]
            moe = Chain(dve, dve_moe, RING, (NBLK - 2) // RING)

            def jv(j, add):
                return j + add if isinstance(j, int) else j[1] * RING + (j[2] + add)

            def take_h(j):
                n = j if isinstance(j, int) else j[2]
                for h in range(2):
                    dve.wait_ge(h_filled, 2 * jv(j, 0) + h + 1)
                    if n > 0 and h == 0:
                        dve.wait_ge(hT_filled, jv(j, 0))
                    v.tensor_copy(hid[:, h * 512:h * 512 + 512], h_bank[h][:, :]).then_inc(h_ready, 1)

            def take_y(j):
                n = j if isinstance(j, int) else j[2]
                s = n % RING
                dve.wait_ge(yb_filled, jv(j, 1))
                moe.link(v.tensor_tensor(xb[s][:, 0:D], y_bank[n % 2][:, 0:D], b2b[s], ALU.add))
                v.tensor_scalar(xb[s][:, 0:D], xb[s][:, 0:D], xb[s][:, D + 1:D + 2], None, ALU.mult).then_inc(y_ready, 1)

            take_h(0)
            turns = (NBLK - 2) // RING
            with dve.Fori(0, turns) as i:
                moe.enter(i)
                for s in range(RING):
                    take_h(("loop", i, s + 1))
                    take_y(("loop", i, s))
                moe.leave()
            for j in range(turns * RING + 1, NBLK):
                take_h(j)
                take_y(j - 1)
            take_y(NBLK - 1)

            tail = Chain(dve, dve_tail, 8, B // 2)

            def total(i, s):
                dve.wait_ge(parts_loaded[s], i * 48 + 48)
                x = tail_x[s]
                tail.link(v.tensor_tensor(tail_y[s][:, 0, :, :], tail_y[s][:, 0, :, :], tail_y[s][:, 1, :, :], ALU.add))
                tail.link(v.tensor_tensor(x, x, tail_y[s][:, 0, :, :], ALU.add))
                for tt in range(QT_N):
                    ins = v.bn_stats(stats["A"][:, tt, :], x[:, tt, :])
                tail.link(ins)
                dve.sem_inc(held["dve"], 1)
                for tt in range(QT_N):
                    ins = v.bn_aggr(mv["A"][:, tt, :], stats["A"][:, tt, :])
                tail.link(ins)
                ins = v.tensor_scalar(var["A"][:, :], mv["A"][:, :, 1], EPS, None, ALU.add)
                ins.then_inc(tail_var, 1)
                dve.wait_ge(tail_rstd, 2 * i + s + 1)
                for tt in range(QT_N):
                    ins = v.tensor_scalar(x[:, tt, :], x[:, tt, :], mv["A"][:, tt, 0:1], rstd["A"][:, tt:tt + 1], ALU.subtract, ALU.mult)
                ins.then_inc(tail_z, 1)

            with dve.Fori(0, B // 2) as i:
                tail.enter(i)
                for s in range(2):
                    total(i, s)
                tail.leave()


DVE_LINKS = 40
POOL_LINKS = 2

_SHORT = {"ctx": "ctx_1024", "x": "x"}
_LAYER = ["sa_wq", "sa_bq", "sa_wk", "sa_bk", "sa_wv", "sa_bv", "sa_wo", "sa_bo", "ca_wq", "ca_bq", "ca_wk", "ca_bk", "ca_wv", "ca_bv",
          "ca_wo", "ca_bo", "ln1_g", "ln1_b", "ln2_g", "ln2_b", "ln3_g", "ln3_b", "router_w", "router_b", "e_w1", "e_b1", "e_w2", "e_b2"]


def kernel(**inputs):
    import numpy as np
    import concourse.bacc as bacc
    from concourse.bass_utils import run_bass_kernel_spmd

    nc = bacc.Bacc("TRN2", target_bir_lowering=False, num_devices=1)
    names = {**_SHORT, **{k: f"L0_xattn_{k}" for k in _LAYER}}
    arrays, aps = {}, {}
    for short, name in names.items():
        a = np.ascontiguousarray(inputs[name])
        arrays[f"in_{short}"] = a
        aps[short] = nc.dram_tensor(f"in_{short}", a.shape, mybir.dt.from_np(a.dtype), kind="ExternalInput").ap()
    out = nc.dram_tensor("layer_out", (B, S, D), F32, kind="ExternalOutput").ap()
    decoder_layer(nc, aps, out)
    r = run_bass_kernel_spmd(nc, [arrays], core_ids=[0])
    return r.results[0]["layer_out"]
```

```python
from contextlib import ExitStack

import concourse.bass as bass
from concourse import mybir

ALU = mybir.AluOpType
ACT = mybir.ActivationFunctionType
AX = mybir.AxisListType.X
F32 = mybir.dt.float32
BF16 = mybir.dt.bfloat16
I32 = mybir.dt.int32
U32 = mybir.dt.uint32

P = 128
B, S, D = 8, 256, 256
H = 16
HD = D // H
SE = 77
E, FF, TOPK = 8, 1024, 2
T = B * S
QT_N = S // P
DC = D // P
FC = FF // P
HC = H // DC
STRIPS = 4
EPS = 1e-5
MASKED = -1e30

ROW = D + 2
REGION = T + P
NBLK = T * TOPK // P + E - 1
NDUMMY = NBLK - T * TOPK // P
XS_ROWS = E * REGION + NDUMMY * P
Y_PAD = T * TOPK
Y_ROWS = Y_PAD + (E + NDUMMY) * P

UA, UB = 12, 8
UNITS = UA + UB
SB = 3
TB = 3
LAG = 4
TURN0, TURN1 = 1, B - 2
NL = TURN1 - TURN0
RING = 4
TAIL = 4


def a_unit(m):
    c, r = divmod(m, 6)
    return (c, 0, range(4 * r, 4 * r + 4), P) if r < 2 else (c, 1, range(2 * r - 4, 2 * r - 2), S)


def b_unit(m):
    q, c, par = m // 4, m // 2 % 2, m % 2
    return c, q, range(4 * par, 4 * par + 4), SE


def head_of(c, slot):
    return c * HC + 2 * (slot % STRIPS) + slot // STRIPS


class WorkUse:

    def __init__(self, n, at, had):
        self.bank, self.filled, self.had = n % 2, at(n + 1), had


class Unit:

    def __init__(self, what, n, pos, at, at_half, freed, after):
        self.kind, self.b, self.m = what
        self.bank, self.turn = pos % SB, n % 2
        self.done, self.turn_done, self.freed, self.after = at(n + 1), at_half(n // 2 + 1), freed, after
        self.turn_freed = at_half(n // 2) if n >= 2 else None


def turn_steps(a, f, b, p):

    def pipeline(units, hooks):
        n = len(units)
        for k in range(n + LAG + 1 if n else max(hooks) + 1):
            if k < n:
                yield ("scores", units[k])
            if 0 <= k - 2 < n:
                yield ("turn", units[k - 2])
            if 0 <= k - LAG < n:
                yield ("values", units[k - LAG])
            yield from hooks.get(k, ())
        assert max(hooks) <= k

    def have(what, *names):
        return [(name, what) for name in names] if what is not None else []

    yield from pipeline([("A", a, m) for m in range(UA)] if a is not None else [],
                        {1: have(p, "zB"), 5: have(p, "x2T"), 6: have(p, "route"), 7: have(p, "gate"), 9: have(f, "xT"), 10: have(p, "rank"),
                         12: have(f, "k"), 14: have(a, "rTA"), 15: have(f, "q"), 16: have(a, "RA", "oTA")})
    yield from have(f, "v") + have(a, "woA")
    if b is None:
        yield from have(a, "nA", "zA") + have(f, "xres")
    else:
        yield from pipeline([("B", b, m) for m in range(UB)], {1: have(a, "nA"), 4: have(a, "zA") + have(f, "xres"), 10: have(b, "rTB")})
    yield from have(a, "cT") + have(b, "RB") + have(a, "k2") + have(b, "oTB") + have(a, "v2")
    yield from have(b, "woB", "nB") + have(a, "x1res", "x1T", "q2")


def batch_script(loop):
    no_bank = {"nA", "nB", "zA", "zB", "oTA", "oTB", "gate", "xres", "x1res"}
    bank_n, unit_n = 0, 0
    had, s_had, o_had = [None, None], [None] * SB, None

    def numbered(steps, i, bank_step, unit_step):
        nonlocal bank_n, unit_n, o_had
        at_bank = lambda n: n if i is None else i * bank_step + n
        at_unit = lambda n: n if i is None else i * unit_step + n
        at_half = lambda n: n if i is None else i * (unit_step // 2) + n
        units, pos, upto = {}, 0, None
        for name, what in steps:
            if name == "scores":
                kind, b, m = what
                k = pos % SB
                units[what[0], m] = Unit(what, unit_n, pos, at_unit, at_half, None if s_had[k] is None else at_unit(s_had[k] + 1),
                                         o_had if m == 0 else None)
                s_had[k] = unit_n
                if m == 0:
                    o_had = (kind, b)
                unit_n, pos = unit_n + 1, pos + 1
                upto = at_unit(unit_n)
            if name in ("scores", "turn", "values"):
                yield name, units[what[0], what[2]], None
            elif name in no_bank:
                yield name, what, upto
            else:
                w = WorkUse(bank_n, at_bank, had[bank_n % 2])
                w.upto = upto
                had[bank_n % 2] = name, what
                bank_n += 1
                yield name, what, w

    def batches(t):
        return [x if 0 <= x < B else None for x in (t + 1, t + 2, t, t - 1)]

    for t in range(-2, TURN0):
        yield from numbered(turn_steps(*batches(t)), None, 0, 0)
    steady = list(turn_steps(*batches(TURN0)))
    per_bank = sum(name not in no_bank | {"scores", "turn", "values"} for name, _ in steady)
    assert per_bank % 2 == 0 and unit_n % 2 == 0
    yield "enter", None, None
    i = loop()
    t = i + TURN0
    bank_0, unit_0 = bank_n, unit_n
    had[:] = [(name, what - TURN0 + t) for name, what in had]
    o_had = o_had[0], o_had[1] - TURN0 + t
    s_0, had_0 = [n - unit_n for n in s_had], [name for name, _ in had]
    yield from numbered(turn_steps(t + 1, t + 2, t, t - 1), i, per_bank, UNITS)
    assert bank_n - bank_0 == per_bank and unit_n - unit_0 == UNITS
    assert s_0 == [n - unit_n for n in s_had] and had_0 == [name for name, _ in had]
    bank_n, unit_n = bank_0 + per_bank * NL, unit_0 + UNITS * NL
    s_had[:] = [n + UNITS * (NL - 1) for n in s_had]
    last = [(name, what) for name, what in turn_steps(*batches(TURN1 - 1)) if name not in no_bank | {"scores", "turn", "values"}][-2:]
    had[bank_n % 2], had[(bank_n + 1) % 2] = last
    o_had = "B", TURN1 - 1
    yield "leave", None, None
    for t in range(TURN1, B + 1):
        yield from numbered(turn_steps(*batches(t)), None, 0, 0)


class Chain:

    def __init__(self, eng, sem, per, turns):
        self.eng, self.sem, self.per, self.turns, self.n, self.i = eng, sem, per, turns, 0, None

    def enter(self, i):
        self.i, self.before = i, self.n

    def leave(self):
        assert self.n - self.before == self.per, ("links in the loop", self.n - self.before)
        self.n, self.i = self.before + self.per * self.turns, None

    def link(self, ins):
        self.n += 1
        ins.then_inc(self.sem, 1)
        self.eng.wait_ge(self.sem, self.n if self.i is None else self.n + self.per * self.i)


def decoder_layer(nc, t, out):
    ctx = ExitStack()
    with ctx:
        def sb(name, shape, dt=F32):
            return ctx.enter_context(nc.sbuf_tensor(name, shape, dt))

        def sem(name):
            return ctx.enter_context(nc.semaphore(name))

        xs_dram = nc.dram_tensor("dispatched", (XS_ROWS, ROW), F32, kind="Internal").ap()
        y_dram = nc.dram_tensor("expert_rows", (Y_ROWS, D), F32, kind="Internal").ap()

        w1 = sb("w1", [P, DC, E, FF])
        w2 = sb("w2", [P, E, FC, D])
        kz = w2[:, E - 2:E, :, :]
        SHARED = 5120
        shared = sb("shared", [P, SHARED])
        at = [0]

        def part(n):
            at[0] += n
            assert at[0] <= SHARED, at[0]
            return shared[:, at[0] - n:at[0]]
        wA = {k: part(DC * D).rearrange("p (k n) -> p k n", k=DC) for k in ("wq", "wk", "wv", "wo")}
        x_in = part(QT_N * D).rearrange("p (t d) -> p t d", t=QT_N)
        xres = part(QT_N * D).rearrange("p (t d) -> p t d", t=QT_N)
        qT = part(DC * S).rearrange("p (c n) -> p c n", c=DC)
        kT = part(DC * S).rearrange("p (c n) -> p c n", c=DC)
        vz = part(QT_N * H * 32).rearrange("p (t n) -> p t n", t=QT_N)
        at[0] = 0
        xb = [part(ROW) for _ in range(RING)]
        b2b = [part(D) for _ in range(RING)]
        xbT = part(DC * P).rearrange("p (c n) -> p c n", c=DC)
        hid = part(FF)
        gT = part(FF).rearrange("p (f n) -> p f n", f=FC)
        pad_rows = shared[:, at[0] - 2 * FF - DC * P:at[0] - 2 * FF - DC * P + E * ROW].rearrange("p (e d) -> p e d", e=E)
        y_sum = part(D)
        ge = part(NBLK * E).rearrange("p (j e) -> p j e", j=NBLK)
        skipped, blkf = part(NBLK), part(NBLK)
        y_a = xres

        wB = {k: sb(f"{k}_cross", [P, DC, D]) for k in ("wq", "wk", "wv", "wo")}
        vecs = {k: sb(k, [P, D]) for k in ("bvA", "boA", "bvB", "boB", "g1", "be1", "g2", "be2", "g3", "be3")}
        rw = sb("router_w", [P, DC, E])
        rb = sb("router_b", [P, E])
        bias_rows, b1_rows = w2[0:4 * DC, E - 1, 0, 0:P], w2[0:E * FC, E - 1, 1, 0:P]
        bias = sb("bias", [P, 4 * DC])
        b1 = sb("b1", [P, E * FC])

        xT = sb("xT", [P, DC, S])
        q2T = sb("q2T", [P, DC, S])
        x1 = sb("x1", [P, QT_N, D])
        x1res = sb("x1res", [P, QT_N, D])
        ctx_in = sb("ctx_in", [SE, D])
        cT = sb("cT", [P, DC, SE])
        k2T = sb("k2T", [P, DC, SE])
        k2z = sb("k2z", [P, DC, HC, SE])
        v2z = sb("v2z", [SE, H * 32])
        probs = [sb(f"probs{k}", [P, 512]) for k in range(SB)]
        probsT = [w2[:, E - 3, 2 * k:2 * k + 2, :].rearrange("p f d -> p (f d)") for k in range(TB)]
        nmax = [sb(f"nmax{k}", [P, 4]) for k in range(SB)]
        sums = {k: sb(f"sums{k}", [P, QT_N, H]) for k in "AB"}
        rinv = {k: sb(f"rinv{k}", [P, QT_N, H]) for k in "AB"}
        rT = sb("rT", [H, S])
        rexp = sb("rexp", [P, DC, S])
        oT = sb("oT", [P, DC, S])
        rows = sb("rows", [P, TOPK, QT_N, ROW])
        y_b = rows[:, 1, :, 0:D]
        stats = {k: sb(f"stats{k}", [P, QT_N, 6]) for k in "AB"}
        mv = {k: sb(f"mv{k}", [P, QT_N, 2]) for k in "AB"}
        var = {k: sb(f"var{k}", [P, QT_N]) for k in "AB"}
        rstd = {k: sb(f"rstd{k}", [P, QT_N]) for k in "AB"}
        lg = sb("logits", [P, QT_N, E])
        top = sb("top", [P, QT_N, 8])
        topi = sb("topi", [P, QT_N, 8], U32)
        topf = sb("topf", [P, QT_N, TOPK])
        ntop = sb("ntop", [P, QT_N])
        etop = sb("etop", [P, QT_N, 8])
        esum = sb("esum", [P, QT_N])
        erec = sb("erec", [P, QT_N])
        pdif = sb("pdif", [P, QT_N])
        pexp = sb("pexp", [P, QT_N])
        den = sb("den", [P, QT_N])
        cw = sb("cw", [P, TOPK, QT_N])
        hot = [sb(f"hot{k}", [P, QT_N, E]) for k in range(TOPK)]
        member = sb("member", [P, QT_N, E], BF16)
        run = sb("run", [P, E])
        run1 = sb("run1", [P, E])
        base = sb("base", [P, E])
        place = sb("place", [P, QT_N, E])
        picked = sb("picked", [P, E])
        slotf = sb("slotf", [P, TOPK, QT_N])
        slot = sb("slot", [P, TOPK, QT_N], U32)
        idf = sb("idf", [P, TOPK, QT_N])

        ident = sb("ident", [P, P])
        identb = sb("identb", [P, P], BF16)
        causal = sb("causal", [P, P], BF16)
        before = sb("before", [P, P], BF16)
        onesb = sb("onesb", [P, P], BF16)
        hmask = sb("hmask", [P, HC])
        spread = sb("spread", [H, DC, P])
        iota8 = sb("iota8", [P, E])
        half = sb("half", [P, QT_N])
        dummy_meta = sb("dummy_meta", [P, NDUMMY, 2])
        jgrid = sb("jgrid", [P, NBLK])
        nb = sb("nb", [P, E])
        nbi = sb("nbi", [P, E], I32)
        ones8 = sb("ones8", [P, E])
        cum = sb("cum", [P, E])
        blk_row = sb("blk_row", [P, NBLK], I32)
        blk_e = sb("blk_e", [P, NBLK], I32)
        pad_row = sb("pad_row", [P, E], I32)

        bank = [ctx.enter_context(nc.psum_tensor(f"bank{k}", [P, 512], F32)) for k in range(8)]
        s_bank, t_bank, w_bank, o_bank = bank[0:SB], bank[SB:5], bank[5:7], bank[7]

        consts_dve = sem("consts_dve")
        consts_pool = sem("consts_pool")
        pool_own = sem("pool_own")
        pool_late = sem("pool_late")
        dve_own = sem("dve_own")
        dve_moe = sem("dve_moe")
        dve_tail = sem("dve_tail")
        act_own = sem("act_own")
        wqk_loaded, wvo_loaded, wB_loaded = sem("wqk_loaded"), sem("wvo_loaded"), sem("wB_loaded")
        vecA_loaded, vec_loaded = sem("vecA_loaded"), sem("vec_loaded")
        rows_loaded = sem("rows_loaded")
        bias_turned, bias_ready = sem("bias_turned"), sem("bias_ready")
        experts_loaded, late_loaded = sem("experts_loaded"), sem("late_loaded")
        x_loaded, ctx_loaded = sem("x_loaded"), sem("ctx_loaded")
        work_filled = sem("work_filled")
        xT_ready, xres_ready = sem("xT_ready"), sem("xres_ready")
        q_ready, kT_ready, kz_ready, vz_ready = sem("q_ready"), sem("kT_ready"), sem("kz_ready"), sem("vz_ready")
        cT_ready, k2T_ready, k2z_ready, v2z_ready = sem("cT_ready"), sem("k2T_ready"), sem("k2z_ready"), sem("v2z_ready")
        x1T_ready, q2_ready, x2T_ready = sem("x1T_ready"), sem("q2_ready"), sem("x2T_ready")
        scores_ready, max_ready, probs_ready = sem("scores_ready"), sem("max_ready"), sem("probs_ready")
        turned = sem("turned")
        probsT_ready = [sem(f"probsT_ready{k}") for k in range(2)]
        values_done = sem("values_done")
        rinv_ready, rT_ready, rexp_ready, oT_ready = ({k: sem(f"{n}{k}") for k in "AB"} for n in
                                                      ("rinv_ready", "rT_ready", "rexp_ready", "oT_ready"))
        var_ready, rstd_ready, z_ready = ({k: sem(f"{n}{k}") for k in "AB"} for n in
                                          ("var_ready", "rstd_ready", "z_ready"))
        x1_ready, x1res_ready, x2_ready, rows_ready = sem("x1_ready"), sem("x1res_ready"), sem("x2_ready"), sem("rows_ready")
        rmax_ready, rexps_ready, pdif_ready, pexp_ready = sem("rmax_ready"), sem("rexps_ready"), sem("pdif_ready"), sem("pexp_ready")
        held = {k: sem(f"held_{k}") for k in ("pool", "dve")}
        sum_ready = {k: sem(f"sum_ready{k}") for k in "AB"}
        logits_ready, places_ready = sem("logits_ready"), sem("places_ready")
        member_ready, slots_ready = sem("member_ready"), sem("slots_ready")
        dispatched = sem("dispatched_rows")
        dummies_written, pads_written, tables_ready = sem("dummies_written"), sem("pads_written"), sem("tables_ready")
        pad_rows_ready, ends_ready = sem("pad_rows_ready"), sem("ends_ready")
        blk_loaded = [sem(f"blk_loaded{k}") for k in range(RING)]
        y_written = [sem(f"y_written{k}") for k in range(RING)]
        xbT_filled, xbT_ready = sem("xbT_filled"), sem("xbT_ready")
        h_filled, h_ready = sem("h_filled"), sem("h_ready")
        hT_filled, gelu_ready = sem("hT_filled"), sem("gelu_ready")
        yb_filled, y_ready = sem("yb_filled"), sem("y_ready")
        parts_loaded = [sem(f"parts_loaded{k}") for k in range(TAIL)]
        tail_var, tail_rstd, tail_z, tail_out = sem("tail_var"), sem("tail_rstd"), sem("tail_z"), sem("tail_out")
        out_written = [sem(f"out_written{k}") for k in range(TAIL)]

        w1_flat = w1[:, :, :, :].rearrange("p k e f -> p (k e f)")
        G = QT_N * D
        tail_y = [w1_flat[:, TOPK * G * s:TOPK * G * (s + 1)].rearrange("p (k t d) -> p k t d", k=TOPK, t=QT_N) for s in range(TAIL)]
        tail_x = [y[:, 0, :, :] for y in tail_y]

        taken = {"xT": xT_ready, "q": q_ready, "k": kT_ready, "v": vz_ready, "cT": cT_ready, "k2": k2T_ready, "v2": v2z_ready, "x1T": x1T_ready,
                 "q2": q2_ready, "x2T": x2T_ready, "route": logits_ready, "rank": places_ready}
        for k in "AB":
            taken.update({"rT" + k: rT_ready[k], "R" + k: rexp_ready[k], "wo" + k: sum_ready[k]})

        block = ctx.enter_context(nc.Block())

        def turns_on(kind, m):
            return "act" if kind == "A" and len(a_unit(m)[2]) == 2 else "dve"

        def write_pads(eng, experts):
            eng.wait_ge(pad_rows_ready, 1)
            eng.wait_ge(ends_ready, 1)
            for e in experts:
                r = eng.value_load(pad_row[0:1, e:e + 1], min_val=e * REGION, max_val=e * REGION + T)
                eng.dma_start(xs_dram[bass.ds(r, P), :], pad_rows[:, e, :]).then_inc(pads_written, 16)

        @block.sync
        def _(sp):
            def load_x(b):
                sp.dma_start(x_in, t["x"][bass.ds(b, 1), :, :].rearrange("a (t p) d -> p (a t) d", p=P)).then_inc(x_loaded, 16)

            def load_ctx(b):
                sp.dma_start(ctx_in[:, :], t["ctx"][bass.ds(b, 1), :, :].rearrange("a s d -> s (a d)")).then_inc(ctx_loaded, 16)

            load_x(0)
            for n, v in enumerate(("sa_bq", "sa_bk", "ca_bq", "ca_bk")):
                sp.dma_start(w2[DC * n:DC * n + DC, E - 1, 0, 0:P], t[v].rearrange("(c p) -> c p", p=P)).then_inc(rows_loaded, 16)
            sp.dma_start(b1_rows, t["e_b1"].rearrange("e (f p) -> (e f) p", p=P)).then_inc(rows_loaded, 16)
            for k, loaded in (("wk", wqk_loaded), ("wq", wqk_loaded), ("wv", wvo_loaded), ("wo", wvo_loaded)):
                sp.dma_start(wA[k], t[f"sa_{k}"].rearrange("(k p) n -> p k n", p=P)).then_inc(loaded, 16)
            for k, v in (("bvA", "sa_bv"), ("boA", "sa_bo"), ("g1", "ln1_g"), ("be1", "ln1_b"), ("bvB", "ca_bv"), ("boB", "ca_bo"),
                         ("g2", "ln2_g"), ("be2", "ln2_b"), ("g3", "ln3_g"), ("be3", "ln3_b")):
                sp.dma_start(vecs[k][:, :], t[v].rearrange("(a n) -> a n", a=1).to_broadcast([P, D])).then_inc(vecA_loaded if k[-1] == "A" else vec_loaded, 16)
            sp.dma_start(rb[:, :], t["router_b"].rearrange("(a n) -> a n", a=1).to_broadcast([P, E])).then_inc(vec_loaded, 16)
            load_ctx(0)
            for k in ("wk", "wv", "wq", "wo"):
                sp.dma_start(wB[k][:, :, :], t[f"ca_{k}"].rearrange("(k p) n -> p k n", p=P)).then_inc(wB_loaded, 16)
            sp.dma_start(rw[:, :, :], t["router_w"].rearrange("(k p) n -> p k n", p=P)).then_inc(wB_loaded, 16)

            def next_x(b):
                sp.wait_ge(xT_ready, b)
                sp.wait_ge(xres_ready, b)
                load_x(b)

            def next_ctx(b):
                sp.wait_ge(cT_ready, b)
                load_ctx(b)

            next_x(1)
            for e in range(E):
                sp.dma_start(w1[:, :, e, :], t["e_w1"][e, :, :].rearrange("(k p) n -> p k n", p=P)).then_inc(experts_loaded, 16)
                if e < E - 3:
                    sp.dma_start(w2[:, e, :, :], t["e_w2"][e, :, :].rearrange("(f p) n -> p f n", p=P)).then_inc(experts_loaded, 16)
            sp.wait_ge(consts_pool, 1)
            sp.wait_ge(vecA_loaded, 16 * 2)
            dummy = xs_dram[E * REGION:XS_ROWS, :].rearrange("(n p) d -> p n d", p=P)
            for n in range(NDUMMY):
                sp.dma_start(dummy[:, n, 0:D], vecs["boA"][:, :]).then_inc(dummies_written, 16)
            sp.dma_start(dummy[:, :, D:ROW], dummy_meta[:, :, :]).then_inc(dummies_written, 16)
            next_x(2)
            next_ctx(1)
            next_x(3)
            next_ctx(2)
            with sp.Fori(0, NL - 1) as i:
                next_x(i + 4)
                next_ctx(i + 3)
            next_ctx(B - 1)
            sp.wait_ge(rT_ready["A"], B)
            for e in (E - 2, E - 1):
                sp.dma_start(w2[:, e, :, :], t["e_w2"][e, :, :].rearrange("(f p) n -> p f n", p=P)).then_inc(late_loaded, 16)
            sp.wait_ge(oT_ready["B"], B)
            sp.dma_start(w2[:, E - 3, :, :], t["e_w2"][E - 3, :, :].rearrange("(f p) n -> p f n", p=P)).then_inc(late_loaded, 16)

            write_pads(sp, range(0, E // 2))
            sp.wait_ge(tables_ready, 1)
            sp.wait_ge(dummies_written, 16 * (NDUMMY + 1))
            sp.wait_ge(pads_written, 16 * E)
            sp.wait_ge(dispatched, 16 * QT_N * TOPK * B)

            def load_block(j, slot_):
                r = sp.value_load(blk_row[0:1, bass.ds(j, 1)], min_val=0, max_val=XS_ROWS - P)
                e = sp.value_load(blk_e[0:1, bass.ds(j, 1)], min_val=0, max_val=E - 1)
                sp.dma_start(xb[slot_], xs_dram[bass.ds(r, P), :]).then_inc(blk_loaded[slot_], 16)
                sp.dma_start(b2b[slot_], t["e_b2"][bass.ds(e, 1), :].to_broadcast([P, D])).then_inc(blk_loaded[slot_], 16)

            for j in range(RING):
                load_block(j, j)
            with sp.Fori(0, (NBLK - RING) // RING) as i:
                for s in range(RING):
                    sp.wait_ge(y_written[s], 16 * i + 16)
                    load_block(i * RING + RING + s, s)
            for j in range(NBLK // RING * RING, NBLK):
                sp.wait_ge(y_written[j % RING], 16 * (j // RING))
                load_block(j, j % RING)

            for s in range(RING):
                sp.wait_ge(y_written[s], 16 * len(range(s, NBLK, RING)))

            def load_parts(g, s):
                for k in range(TOPK):
                    sp.dma_start(tail_y[s][:, k, :, :], y_dram[bass.ds(g * S + k * T, S), :].rearrange("(t p) d -> p t d", p=P)).then_inc(parts_loaded[s], 16)

            def store(g, s):
                sp.dma_start(out[bass.ds(g, 1), :, :].rearrange("a (t p) d -> p (a t) d", p=P), tail_x[s]).then_inc(out_written[s], 16)

            for s in range(TAIL):
                load_parts(s, s)
            with sp.Fori(0, B // TAIL - 1) as i:
                for s in range(TAIL):
                    sp.wait_ge(tail_out, TAIL * i + (s + 1))
                    store(TAIL * i + s, s)
                for s in range(TAIL):
                    sp.wait_ge(out_written[s], 16 * i + 16)
                    load_parts(TAIL * i + (s + TAIL), s)
            for s in range(TAIL):
                sp.wait_ge(tail_out, B - TAIL + s + 1)
                store(B - TAIL + s, s)
            for s in range(TAIL):
                sp.wait_ge(out_written[s], 16 * (B // TAIL))

        @block.tensor
        def _(pe):
            def open_bank(w):
                if w.had is not None:
                    name, b = w.had
                    pe.wait_ge(taken[name], b + 1)
                return w_bank[w.bank]

            def turn4(w, src):
                o = open_bank(w)
                for c in range(DC):
                    for tt in range(QT_N):
                        last = nc.tensor.transpose(o[:, c * S + tt * P:c * S + tt * P + P], src[:, tt, c * P:c * P + P], ident[:, :])
                last.then_inc(work_filled, 1)

            def across(w, wt, src, n):
                o = open_bank(w)
                for c in range(DC):
                    for k in range(DC):
                        last = nc.tensor.matmul(o[:, c * n:c * n + n], wt[:, k, c * P:c * P + P], src[:, k, :], start=k == 0, stop=k == DC - 1)
                last.then_inc(work_filled, 1)

            def along(w, wt, src):
                o = open_bank(w)
                for tt in range(QT_N):
                    for k in range(DC):
                        last = nc.tensor.matmul(o[:, tt * D:tt * D + D], src[:, k, tt * P:tt * P + P], wt[:, k, :], start=k == 0, stop=k == DC - 1)
                last.then_inc(work_filled, 1)

            def scores(u):
                if u.freed is not None:
                    pe.wait_ge(probs_ready, u.freed)
                o = s_bank[u.bank]
                if u.kind == "A":
                    c, q, heads, keys = a_unit(u.m)
                    if u.m == 0:
                        pe.wait_ge(q_ready, u.b + 1)
                    if u.m % (UA // DC) == 0:
                        pe.wait_ge(kz_ready, DC * u.b + (c + 1))
                    n = len(heads)
                    o3 = o[:, :].rearrange("p (h k) -> p h k", h=n)
                    nc.tensor.matmul(o3, qT[:, c, q * P:q * P + P], kz[:, c, heads[0]:heads[0] + n, 0:keys], start=True, stop=False)
                    nc.tensor.matmul(o3[:, :, keys - P:keys], identb[:, :], causal[:, None, :].to_broadcast([P, n, P]),
                                     start=False, stop=True).then_inc(scores_ready, 1)
                else:
                    c, q, heads, keys = b_unit(u.m)
                    if u.m == 0:
                        pe.wait_ge(q2_ready, u.b + 1)
                        pe.wait_ge(k2z_ready, DC * u.b + DC)
                    nc.tensor.matmul(o[:, 0:4 * SE].rearrange("p (h k) -> p h k", h=4), q2T[:, c, q * P:q * P + P],
                                     k2z[:, c, heads[0]:heads[0] + 4, :], start=True, stop=True).then_inc(scores_ready, 1)

            def turn(u):
                pe.wait_ge(probs_ready, u.done)
                if u.turn_freed is not None:
                    pe.wait_ge(probsT_ready[u.turn], u.turn_freed)
                o, p = t_bank[u.turn], probs[u.bank]
                for j in range(4):
                    if u.kind == "A":
                        last = nc.tensor.transpose(o[:, j * P:j * P + P], p[:, j * P:j * P + P], ident[:, :])
                    else:
                        last = nc.tensor.transpose(o[0:SE, j * P:j * P + P], p[:, j * SE:j * SE + SE], ident[:, :])
                last.then_inc(turned, 1)

            def values(u):
                pe.wait_ge(probsT_ready[u.turn], u.turn_done)
                p = probsT[u.bank]
                if u.m == 0:
                    pe.wait_ge(vz_ready if u.kind == "A" else v2z_ready, u.b + 1)
                    if u.after is not None:
                        pe.wait_ge(oT_ready[u.after[0]], u.after[1] + 1)
                if u.kind == "A":
                    c, q, heads, keys = a_unit(u.m)
                    n = keys // P
                    for kt in range(n):
                        for a, s_ in enumerate(heads):
                            par, strip, h = s_ // STRIPS, s_ % STRIPS, head_of(c, s_)
                            last = nc.tensor.matmul(o_bank[32 * strip:32 * strip + 32, c * S + q * P:c * S + q * P + P],
                                                    vz[:, kt, 32 * h:32 * h + 32], p[:, (a * n + kt) * P:(a * n + kt) * P + P],
                                                    start=par == 0 and kt == 0, stop=par == 1 and kt == n - 1)
                else:
                    c, q, heads, keys = b_unit(u.m)
                    for a, s_ in enumerate(heads):
                        par, strip, h = s_ // STRIPS, s_ % STRIPS, head_of(c, s_)
                        last = nc.tensor.matmul(o_bank[32 * strip:32 * strip + 32, c * S + q * P:c * S + q * P + P],
                                                v2z[:, 32 * h:32 * h + 32], p[0:SE, a * P:a * P + P], start=par == 0, stop=par == 1)
                last.then_inc(values_done, 1)

            def rows_of_rinv(w, k, b):
                o = open_bank(w)
                pe.wait_ge(rinv_ready[k], b + 1)
                for q in range(QT_N):
                    last = nc.tensor.transpose(o[0:H, q * P:q * P + P], rinv[k][:, q, :], ident[:, :])
                last.then_inc(work_filled, 1)

            def spread_rinv(w, k, b):
                o = open_bank(w)
                pe.wait_ge(rT_ready[k], b + 1)
                for c in range(DC):
                    last = nc.tensor.matmul(o[:, c * S:c * S + S], spread[:, c, :], rT[:, :], start=True, stop=True)
                last.then_inc(work_filled, 1)

            pe.wait_ge(consts_pool, 1)
            pe.wait_ge(consts_dve, 1)
            pe.wait_ge(rows_loaded, 16 * 5)
            nc.tensor.transpose(t_bank[0][:, 0:4 * DC], bias_rows, ident[0:4 * DC, 0:4 * DC])
            nc.tensor.transpose(t_bank[1][:, 0:E * FC], b1_rows, ident[0:E * FC, 0:E * FC]).then_inc(bias_turned, 1)

            scope = ExitStack()
            for name, what, w in batch_script(lambda: scope.enter_context(pe.Fori(0, NL))):
                if name == "leave":
                    scope.close()
                elif name == "xT":
                    pe.wait_ge(x_loaded, what * 16 + 16)
                    turn4(w, x_in)
                elif name in ("q", "k"):
                    if isinstance(what, int) and what == 0 and name == "k":
                        pe.wait_ge(wqk_loaded, 16 * 2)
                    pe.wait_ge(xT_ready, what + 1)
                    across(w, wA["w" + name], xT, S)
                elif name == "v":
                    if isinstance(what, int) and what == 0:
                        pe.wait_ge(wvo_loaded, 16 * 2)
                    along(w, wA["wv"], xT)
                elif name == "cT":
                    o = open_bank(w)
                    if isinstance(what, int) and what == 0:
                        pe.wait_ge(wB_loaded, 16 * 5)
                    pe.wait_ge(ctx_loaded, what * 16 + 16)
                    for c in range(DC):
                        last = nc.tensor.transpose(o[:, c * SE:c * SE + SE], ctx_in[:, c * P:c * P + P], ident[0:SE, 0:SE])
                    last.then_inc(work_filled, 1)
                elif name == "k2":
                    pe.wait_ge(cT_ready, what + 1)
                    across(w, wB["wk"], cT, SE)
                elif name == "v2":
                    o = open_bank(w)
                    for k in range(DC):
                        last = nc.tensor.matmul(o[0:SE, 0:D], cT[:, k, :], wB["wv"][:, k, :], start=k == 0, stop=k == DC - 1)
                    last.then_inc(work_filled, 1)
                elif name == "x1T":
                    pe.wait_ge(x1_ready, what + 1)
                    turn4(w, x1)
                elif name == "q2":
                    pe.wait_ge(x1T_ready, what + 1)
                    across(w, wB["wq"], xT, S)
                elif name == "x2T":
                    pe.wait_ge(x2_ready, what + 1)
                    turn4(w, rows[:, 0, :, :])
                elif name == "route":
                    o = open_bank(w)
                    pe.wait_ge(x2T_ready, what + 1)
                    for tt in range(QT_N):
                        for k in range(DC):
                            last = nc.tensor.matmul(o[:, tt * E:tt * E + E], xT[:, k, tt * P:tt * P + P], rw[:, k, :], start=k == 0, stop=k == DC - 1)
                    last.then_inc(work_filled, 1)
                elif name == "rank":
                    o = open_bank(w)
                    pe.wait_ge(member_ready, what + 1)
                    m = member[:, :, :].rearrange("p t e -> p (t e)")
                    nc.tensor.matmul(o[:, 0:QT_N * E], before[:, :], m, start=True, stop=True)
                    nc.tensor.matmul(o[:, QT_N * E:2 * QT_N * E], onesb[:, :], m, start=True, stop=True).then_inc(work_filled, 1)
                elif name in ("rTA", "rTB"):
                    rows_of_rinv(w, name[-1], what)
                elif name in ("RA", "RB"):
                    spread_rinv(w, name[-1], what)
                elif name in ("woA", "woB"):
                    pe.wait_ge(oT_ready[name[-1]], what + 1)
                    along(w, (wA if name == "woA" else wB)["wo"], oT)
                elif name == "scores":
                    scores(what)
                elif name == "turn":
                    turn(what)
                elif name == "values":
                    values(what)

            h_bank, g_bank, x_bank, y_bank = bank[0:2], bank[2:4], bank[4], bank[6:8]

            def block_T(j, s):
                pe.wait_ge(blk_loaded[s], 32 * (j // RING) + 32 if isinstance(j, int) else j[1] * 32 + j[2] // RING * 32 + 32)

            def jval(j, add):
                return j + add if isinstance(j, int) else j[1] * RING + (j[2] + add)

            def turn_x(j):
                n = j if isinstance(j, int) else j[2]
                s = n % RING
                block_T(j, s)
                if n > 0:
                    pe.wait_ge(xbT_ready, jval(j, 0))
                for c in range(DC):
                    last = nc.tensor.transpose(x_bank[:, c * P:c * P + P], xb[s][:, c * P:c * P + P], ident[:, :])
                last.then_inc(xbT_filled, 1)

            def load_e(j):
                return pe.value_load(blk_e[0:1, bass.ds(jval(j, 0), 1)], min_val=0, max_val=E - 1)

            def up(j, half_, e):
                n = j if isinstance(j, int) else j[2]
                if half_ == 0:
                    pe.wait_ge(xbT_ready, jval(j, 1))
                if n > 0:
                    pe.wait_ge(h_ready, 2 * jval(j, -1) + half_ + 1)
                for k in range(DC):
                    last = nc.tensor.matmul(h_bank[half_][:, :], xbT[:, k, :], w1[:, k, bass.ds(e, 1), half_ * 512:half_ * 512 + 512],
                                            start=k == 0, stop=k == DC - 1)
                last.then_inc(h_filled, 1)

            def turn_h(j):
                n = j if isinstance(j, int) else j[2]
                pe.wait_ge(h_ready, 2 * jval(j, 1))
                if n > 0:
                    pe.wait_ge(gelu_ready, jval(j, 0))
                for f in range(FC):
                    last = nc.tensor.transpose(g_bank[f // 4][:, f % 4 * P:f % 4 * P + P], hid[:, f * P:f * P + P], ident[:, :])
                last.then_inc(hT_filled, 1)

            def down(j, e):
                n = j if isinstance(j, int) else j[2]
                pe.wait_ge(gelu_ready, jval(j, 1))
                if n > 1:
                    pe.wait_ge(y_ready, jval(j, -1))
                for f in range(FC):
                    last = nc.tensor.matmul(y_bank[n % 2][:, 0:D], gT[:, f, :], w2[:, bass.ds(e, 1), f, :], start=f == 0, stop=f == FC - 1)
                last.then_inc(yb_filled, 1)

            def step(j, prev, nxt):
                turn_h(prev)
                e = load_e(j)
                up(j, 0, e)
                up(j, 1, e)
                if nxt is not None:
                    turn_x(nxt)
                down(prev, load_e(prev))

            pe.wait_ge(tables_ready, 1)
            pe.wait_ge(experts_loaded, 16 * (2 * E - 3))
            pe.wait_ge(late_loaded, 16 * 3)
            turn_x(0)
            e0 = load_e(0)
            up(0, 0, e0)
            up(0, 1, e0)
            turn_x(1)
            turns = (NBLK - 2) // RING
            with pe.Fori(0, turns) as i:
                for s in range(RING):
                    step(("loop", i, s + 1), ("loop", i, s), ("loop", i, s + 2))
            for j in range(turns * RING + 1, NBLK):
                step(j, j - 1, j + 1 if j + 1 < NBLK else None)
            turn_h(NBLK - 1)
            down(NBLK - 1, load_e(NBLK - 1))

        @block.scalar
        def _(act):
            act.wait_ge(bias_turned, 1)
            nc.scalar.copy(bias[:, :], t_bank[0][:, 0:4 * DC])
            nc.scalar.copy(b1[:, :], t_bank[1][:, 0:E * FC]).then_inc(bias_ready, 1)
            act.wait_ge(bias_ready, 1)

            def shifted(w, dst, n, col):
                act.wait_ge(work_filled, w.filled)
                for c in range(DC):
                    last = nc.scalar.activation(dst[:, c, :], w_bank[w.bank][:, c * n:c * n + n], ACT.Identity, bias=bias[:, col + c:col + c + 1])
                return last

            flat = lambda x: x[:, :, :].rearrange("p c n -> p (c n)")
            scope = ExitStack()
            for name, what, w in batch_script(lambda: scope.enter_context(act.Fori(0, NL))):
                b = what
                if name == "leave":
                    scope.close()
                elif name in ("xT", "x1T", "x2T"):
                    ready = {"xT": xT_ready, "x1T": x1T_ready, "x2T": x2T_ready}[name]
                    act.wait_ge(work_filled, w.filled)
                    ins = nc.scalar.copy(flat(xT), w_bank[w.bank][:, :])
                    ins.then_inc(ready, 1)
                elif name == "k":
                    if not (isinstance(b, int) and b == 0):
                        act.wait_ge(kz_ready, DC * b)
                    ins = shifted(w, kT, S, DC)
                    ins.then_inc(kT_ready, 1)
                elif name == "cT":
                    act.wait_ge(work_filled, w.filled)
                    ins = nc.scalar.copy(flat(cT), w_bank[w.bank][:, 0:DC * SE])
                    ins.then_inc(cT_ready, 1)
                elif name == "k2":
                    if not (isinstance(b, int) and b == 0):
                        act.wait_ge(k2z_ready, DC * b)
                    ins = shifted(w, k2T, SE, 3 * DC)
                    ins.then_inc(k2T_ready, 1)
                elif name in ("rTA", "rTB"):
                    act.wait_ge(work_filled, w.filled)
                    ins = nc.scalar.copy(rT[:, :], w_bank[w.bank][0:H, 0:S])
                    ins.then_inc(rT_ready[name[-1]], 1)
                elif name in ("RA", "RB"):
                    act.wait_ge(work_filled, w.filled)
                    ins = nc.scalar.copy(flat(rexp), w_bank[w.bank][:, :])
                    ins.then_inc(rexp_ready[name[-1]], 1)
                elif name == "scores":
                    u = what
                    act.wait_ge(max_ready, u.done)
                    p = probs[u.bank]
                    c, q, heads, keys = a_unit(u.m) if u.kind == "A" else b_unit(u.m)
                    for a, s_ in enumerate(heads):
                        h = head_of(c, s_)
                        last = nc.scalar.activation(p[:, a * keys:a * keys + keys], s_bank[u.bank][:, a * keys:a * keys + keys], ACT.Exp,
                                                    bias=nmax[u.bank][:, a:a + 1], accum_out=sums[u.kind][:, q, h:h + 1])
                    last.then_inc(probs_ready, 1)
                elif name == "turn":
                    u = what
                    if turns_on(u.kind, u.m) == "act":
                        act.wait_ge(turned, u.done)
                        n = P if u.kind == "A" else SE
                        nc.scalar.copy(probsT[u.bank][0:n, :], t_bank[u.turn][0:n, :]).then_inc(probsT_ready[u.turn], 1)
                elif name == "route":
                    act.wait_ge(rmax_ready, b + 1)
                    for tt in range(QT_N):
                        last = nc.scalar.activation(etop[:, tt, :], top[:, tt, :], ACT.Exp, bias=ntop[:, tt:tt + 1], accum_out=esum[:, tt:tt + 1])
                    last.then_inc(rexps_ready, 1)
                elif name == "gate":
                    act.wait_ge(pdif_ready, b + 1)
                    nc.scalar.activation(pexp[:, :], pdif[:, :], ACT.Exp).then_inc(pexp_ready, 1)

            write_pads(act, range(E // 2, E))

            h_bank, g_bank, x_bank, y_bank = bank[0:2], bank[2:4], bank[4], bank[6:8]

            def jv(j, add):
                return j + add if isinstance(j, int) else j[1] * RING + (j[2] + add)

            def take_x(j):
                act.wait_ge(xbT_filled, jv(j, 1))
                nc.scalar.copy(xbT.rearrange("p c n -> p (c n)"), x_bank[:, 0:D]).then_inc(xbT_ready, 1)

            def gelu(j):
                e = act.value_load(blk_e[0:1, bass.ds(jv(j, 0), 1)], min_val=0, max_val=E - 1)
                act.wait_ge(hT_filled, jv(j, 1))
                for f in range(FC):
                    last = nc.scalar.activation(gT[:, f, :], g_bank[f // 4][:, f % 4 * P:f % 4 * P + P], ACT.Gelu, bias=b1[:, bass.ds(e * FC + f, 1)])
                last.then_inc(gelu_ready, 1)

            act.wait_ge(tables_ready, 1)
            take_x(0)
            take_x(1)
            turns = (NBLK - 2) // RING
            with act.Fori(0, turns) as i:
                for s in range(RING):
                    gelu(("loop", i, s))
                    take_x(("loop", i, s + 2))
            for j in range(turns * RING, NBLK):
                gelu(j)
                if j + 2 < NBLK:
                    take_x(j + 2)

        @block.gpsimd
        def _(pool):
            own = Chain(pool, pool_own, POOL_LINKS, NL)
            gp = nc.gpsimd
            own.link(gp.memset(ident[:, :], 0.0))
            own.link(gp.affine_select(out=ident[:, :], in_=ident[:, :], compare_op=ALU.not_equal, fill=1.0, base=0, pattern=[[-1, P]], channel_multiplier=1))
            own.link(gp.memset(identb[:, :], 0.0))
            own.link(gp.affine_select(out=identb[:, :], in_=identb[:, :], compare_op=ALU.not_equal, fill=1.0, base=0, pattern=[[-1, P]], channel_multiplier=1))
            own.link(gp.memset(causal[:, :], 0.0))
            own.link(gp.affine_select(out=causal[:, :], in_=causal[:, :], compare_op=ALU.is_ge, fill=MASKED, base=0, pattern=[[-1, P]], channel_multiplier=1))
            own.link(gp.memset(before[:, :], 1.0))
            own.link(gp.affine_select(out=before[:, :], in_=before[:, :], compare_op=ALU.is_gt, fill=0.0, base=0, pattern=[[1, P]], channel_multiplier=-1))
            hm = hmask[:, :].rearrange("p (a s) -> p a s", a=2)
            own.link(gp.memset(hmask[:, :], 1.0))
            own.link(gp.affine_select(out=hm, in_=hm, compare_op=ALU.is_ge, fill=0.0, base=0, pattern=[[-HD, 2], [-2 * HD, STRIPS]], channel_multiplier=1))
            own.link(gp.affine_select(out=hm, in_=hm, compare_op=ALU.is_ge, fill=0.0, base=HD - 1, pattern=[[HD, 2], [2 * HD, STRIPS]], channel_multiplier=-1))
            own.link(gp.memset(spread[:, :, :], 1.0))
            own.link(gp.affine_select(out=spread[:, :, :], in_=spread[:, :, :], compare_op=ALU.is_ge, fill=0.0, base=0, pattern=[[P, DC], [1, P]], channel_multiplier=-HD))
            own.link(gp.affine_select(out=spread[:, :, :], in_=spread[:, :, :], compare_op=ALU.is_ge, fill=0.0, base=HD - 1, pattern=[[-P, DC], [-1, P]], channel_multiplier=HD))
            own.link(gp.iota(iota8[:, :], pattern=[[1, E]], base=0, channel_multiplier=0, allow_small_or_imprecise_dtypes=True))
            own.link(gp.iota(base[:, :], pattern=[[REGION, E]], base=0, channel_multiplier=0, allow_small_or_imprecise_dtypes=True))
            own.link(gp.iota(run[:, :], pattern=[[REGION, E]], base=0, channel_multiplier=0, allow_small_or_imprecise_dtypes=True))
            own.link(gp.iota(idf[:, :, :], pattern=[[T, TOPK], [P, QT_N]], base=0, channel_multiplier=1, allow_small_or_imprecise_dtypes=True))
            own.link(gp.iota(jgrid[:, :], pattern=[[1, NBLK]], base=0, channel_multiplier=0, allow_small_or_imprecise_dtypes=True))
            own.link(gp.memset(dummy_meta[:, :, :], 0.0))
            gp.iota(dummy_meta[:, :, 0:1].bitcast(I32), pattern=[[P, NDUMMY], [0, 1]], base=Y_PAD + E * P, channel_multiplier=1).then_inc(consts_pool, 1)

            def two(x):
                return x[:, None, :].to_broadcast([P, QT_N, D])

            scope = ExitStack()

            def loop():
                i = scope.enter_context(pool.Fori(0, NL))
                own.enter(i)
                return i

            for name, what, w in batch_script(loop):
                b = what
                first = isinstance(b, int) and b == 0
                if name == "leave":
                    own.leave()
                    scope.close()
                elif name == "xres":
                    if first:
                        pool.wait_ge(vecA_loaded, 16 * 2)
                    pool.wait_ge(x_loaded, b * 16 + 16)
                    if not first:
                        pool.wait_ge(x1_ready, b)
                    gp.tensor_tensor(xres, x_in, two(vecs["boA"]), ALU.add).then_inc(xres_ready, 1)
                elif name in ("k", "k2"):
                    src, dst, n, got, put = (kT, kz, S, kT_ready, kz_ready) if name == "k" else (k2T, k2z, SE, k2T_ready, k2z_ready)
                    pool.wait_ge(got, b + 1)
                    for c in range(DC):
                        gp.tensor_tensor(dst[:, c, :, :], src[:, c, None, :].to_broadcast([P, HC, n]), hmask[:, :, None].to_broadcast([P, HC, n]), ALU.mult).then_inc(put, 1)
                elif name in ("nA", "nB"):
                    k = name[-1]
                    pool.wait_ge(var_ready[k], b + 1)
                    gp.tensor_tensor(rstd[k][:, :], var[k][:, :], half[:, :], ALU.pow).then_inc(rstd_ready[k], 1)
                elif name == "zA":
                    pool.wait_ge(z_ready["A"], b + 1)
                    if first:
                        pool.wait_ge(vec_loaded, 16 * 9)
                    own.link(gp.tensor_tensor(y_a, y_a, two(vecs["g1"]), ALU.mult))
                    gp.tensor_tensor(x1[:, :, :], y_a, two(vecs["be1"]), ALU.add).then_inc(x1_ready, 1)
                elif name == "x1res":
                    pool.wait_ge(x1_ready, b + 1)
                    if not first:
                        pool.wait_ge(sum_ready["B"], b)
                    gp.tensor_tensor(x1res[:, :, :], x1[:, :, :], two(vecs["boB"]), ALU.add).then_inc(x1res_ready, 1)
                elif name == "zB":
                    pool.wait_ge(z_ready["B"], b + 1)
                    own.link(gp.tensor_tensor(y_b, y_b, two(vecs["g2"]), ALU.mult))
                    if not first:
                        pool.wait_ge(dispatched, b * (16 * QT_N * TOPK))
                    gp.tensor_tensor(rows[:, 0, :, 0:D], y_b, two(vecs["be2"]), ALU.add).then_inc(x2_ready, 1)
                    pool.wait_ge(x2_ready, b + 1)
                    gp.tensor_tensor(y_b, y_b, two(vecs["be2"]), ALU.add).then_inc(rows_ready, 1)
                    if isinstance(b, int) and b == B - 2:
                        pool.wait_ge(oT_ready["A"], B)
                        own.link(gp.memset(pad_rows, 0.0))
                        gp.iota(pad_rows[:, :, D:D + 1].bitcast(I32), pattern=[[P, E], [0, 1]], base=Y_PAD, channel_multiplier=1).then_inc(pad_rows_ready, 1)
                elif name == "rank":
                    pool.wait_ge(slots_ready, b + 1)
                    pool.wait_ge(rows_ready, b + 1)
                    pool.sem_inc(held["pool"], 1)
                    for k in range(TOPK):
                        for tt in range(QT_N):
                            gp.indirect_dma_start(out=xs_dram, out_offset=bass.IndirectOffsetOnAxis(ap=slot[:, k, tt:tt + 1], axis=0),
                                                  in_=rows[:, k, tt, :], in_offset=None).then_inc(dispatched, 16)

            def put(j):
                n = j if isinstance(j, int) else j[2]
                s = n % RING
                pool.wait_ge(y_ready, j + 1 if isinstance(j, int) else j[1] * RING + (j[2] + 1))
                pool.sem_inc(held["pool"], 1)
                gp.indirect_dma_start(out=y_dram, out_offset=bass.IndirectOffsetOnAxis(ap=xb[s][:, D:D + 1].bitcast(U32), axis=0),
                                      in_=xb[s][:, 0:D], in_offset=None).then_inc(y_written[s], 16)

            turns = NBLK // RING
            with pool.Fori(0, turns) as i:
                for s in range(RING):
                    put(("loop", i, s))
            for j in range(turns * RING, NBLK):
                put(j)

            late = Chain(pool, pool_late, TAIL, B // TAIL)

            def raised(n, s):
                k = "AB"[s % 2]
                pool.wait_ge(tail_var, n)
                gp.tensor_tensor(rstd[k][:, :], var[k][:, :], half[:, :], ALU.pow).then_inc(tail_rstd, 1)

            def finish(n, s):
                pool.wait_ge(tail_z, n)
                late.link(gp.tensor_tensor(tail_x[s], tail_x[s], two(vecs["g3"]), ALU.mult))
                gp.tensor_tensor(tail_x[s], tail_x[s], two(vecs["be3"]), ALU.add).then_inc(tail_out, 1)

            with pool.Fori(0, B // TAIL) as i:
                late.enter(i)
                for s in range(TAIL + 1):
                    if s < TAIL:
                        raised(TAIL * i + (s + 1), s)
                    if s > 0:
                        finish(TAIL * i + s, s - 1)
                late.leave()

        @block.vector
        def _(dve):
            v = nc.vector
            own = Chain(dve, dve_own, DVE_LINKS, NL)
            v.memset(onesb[:, :], 1.0)
            v.memset(half[:, :], -0.5)
            v.memset(ones8[:, :], 1.0)
            v.memset(vz, 0.0)
            v.memset(v2z[:, :], 0.0).then_inc(consts_dve, 1)
            dve.wait_ge(consts_dve, 1)
            dve.wait_ge(consts_pool, 1)
            dve.wait_ge(bias_ready, 1)

            def norm(k, y, res, resem, b, first, w):
                dve.wait_ge(work_filled, w.filled)
                dve.wait_ge(resem, b + 1)
                if k == "B" and not first:
                    dve.wait_ge(dispatched, b * (16 * QT_N * TOPK))
                ins = v.tensor_tensor(y, w_bank[w.bank][:, :].rearrange("p (t d) -> p t d", t=QT_N), res, ALU.add)
                ins.then_inc(sum_ready[k], 1)
                dve.wait_ge(sum_ready[k], b + 1)
                for tt in range(QT_N):
                    ins = v.bn_stats(stats[k][:, tt, :], y[:, tt, :])
                own.link(ins)
                dve.sem_inc(held["dve"], 1)
                for tt in range(QT_N):
                    ins = v.bn_aggr(mv[k][:, tt, :], stats[k][:, tt, :])
                own.link(ins)
                v.tensor_scalar(var[k][:, :], mv[k][:, :, 1], EPS, None, ALU.add).then_inc(var_ready[k], 1)

            def normalised(k, y, b):
                dve.wait_ge(rstd_ready[k], b + 1)
                for tt in range(QT_N):
                    ins = v.tensor_scalar(y[:, tt, :], y[:, tt, :], mv[k][:, tt, 0:1], rstd[k][:, tt:tt + 1], ALU.subtract, ALU.mult)
                ins.then_inc(z_ready[k], 1)

            def scaled_q(w, dst, col, ready):
                dve.wait_ge(work_filled, w.filled)
                for c in range(DC):
                    ins = v.tensor_scalar(dst[:, c, :], w_bank[w.bank][:, c * S:c * S + S], bias[:, col + c:col + c + 1], HD ** -0.5, ALU.add, ALU.mult)
                ins.then_inc(ready, 1)

            def spread_v(dst, src, bv, n):
                d4 = dst.rearrange("p (s a x) -> p s a x", s=H // 2, a=2)
                s4 = src.rearrange("p (s a x) -> p s a x", s=H // 2, a=2)
                b4 = bv[0:n, :].rearrange("p (s a x) -> p s a x", s=H // 2, a=2)
                for par in range(2):
                    ins = v.tensor_tensor(d4[:, :, par, par * HD:par * HD + HD], s4[:, :, par, :], b4[:, :, par, :], ALU.add)
                return ins

            scope = ExitStack()

            def loop():
                i = scope.enter_context(dve.Fori(0, NL))
                own.enter(i)
                return i

            for name, what, w in batch_script(loop):
                b = what
                first = isinstance(b, int) and b == 0
                if name == "leave":
                    own.leave()
                    scope.close()
                elif name == "q":
                    scaled_q(w, qT, 0, q_ready)
                elif name == "q2":
                    scaled_q(w, q2T, 2 * DC, q2_ready)
                elif name == "v":
                    dve.wait_ge(work_filled, w.filled)
                    if first:
                        dve.wait_ge(vecA_loaded, 16 * 2)
                    for tt in range(QT_N):
                        ins = spread_v(vz[:, tt, :], w_bank[w.bank][:, tt * D:tt * D + D], vecs["bvA"], P)
                    ins.then_inc(vz_ready, 1)
                elif name == "v2":
                    dve.wait_ge(work_filled, w.filled)
                    if first:
                        dve.wait_ge(vec_loaded, 16 * 9)
                    ins = spread_v(v2z[:, :], w_bank[w.bank][0:SE, 0:D], vecs["bvB"], SE)
                    ins.then_inc(v2z_ready, 1)
                elif name == "scores":
                    u = what
                    dve.wait_ge(scores_ready, u.done)
                    c, q, heads, keys = a_unit(u.m) if u.kind == "A" else b_unit(u.m)
                    n = len(heads)
                    v.tensor_reduce(nmax[u.bank][:, 0:n], s_bank[u.bank][:, 0:n * keys].rearrange("p (h k) -> p h k", h=n), AX, ALU.max, negate=True).then_inc(max_ready, 1)
                elif name == "turn":
                    u = what
                    if turns_on(u.kind, u.m) == "dve":
                        dve.wait_ge(turned, u.done)
                        n = P if u.kind == "A" else SE
                        v.tensor_copy(probsT[u.bank][0:n, :], t_bank[u.turn][0:n, :]).then_inc(probsT_ready[u.turn], 1)
                elif name in ("rTA", "rTB"):
                    k = name[-1]
                    dve.wait_ge(probs_ready, w.upto)
                    if not first:
                        dve.wait_ge(rT_ready[k], b)
                    v.reciprocal(rinv[k][:, :, :], sums[k][:, :, :]).then_inc(rinv_ready[k], 1)
                elif name in ("oTA", "oTB"):
                    k, upto = name[-1], w
                    dve.wait_ge(rexp_ready[k], b + 1)
                    dve.wait_ge(values_done, upto)
                    v.tensor_tensor(oT[:, :, :].rearrange("p c n -> p (c n)"), o_bank[:, :], rexp[:, :, :].rearrange("p c n -> p (c n)"), ALU.mult).then_inc(oT_ready[k], 1)
                elif name in ("woA", "woB"):
                    w_norm = w
                elif name == "nA":
                    norm("A", y_a, xres, xres_ready, b, first, w_norm)
                elif name in ("zA", "zB"):
                    normalised(name[-1], y_a if name == "zA" else y_b, b)
                elif name == "nB":
                    norm("B", y_b, x1res[:, :, :], x1res_ready, b, first, w_norm)
                elif name == "route":
                    dve.wait_ge(work_filled, w.filled)
                    ins = v.tensor_tensor(lg[:, :, :], w_bank[w.bank][:, 0:QT_N * E].rearrange("p (t e) -> p t e", t=QT_N), rb[:, None, :].to_broadcast([P, QT_N, E]), ALU.add)
                    ins.then_inc(logits_ready, 1)
                    dve.wait_ge(logits_ready, b + 1)
                    dve.sem_inc(held["dve"], 1)
                    for tt in range(QT_N):
                        ins = v.max(top[:, tt, :], lg[:, tt, :])
                    own.link(ins)
                    v.tensor_scalar(ntop[:, :], top[:, :, 0], -1.0, None, ALU.mult).then_inc(rmax_ready, 1)
                    for tt in range(QT_N):
                        ins = v.max_index(topi[:, tt, :], top[:, tt, :], lg[:, tt, :])
                    own.link(ins)
                    own.link(v.tensor_copy(topf[:, :, :], topi[:, :, 0:TOPK]))
                    for k in range(TOPK):
                        for tt in range(QT_N):
                            ins = v.tensor_scalar(hot[k][:, tt, :], iota8[:, :], topf[:, tt, k:k + 1], None, ALU.is_equal)
                    own.link(ins)
                    v.tensor_tensor(member[:, :, :], hot[0][:, :, :], hot[1][:, :, :], ALU.add).then_inc(member_ready, 1)
                elif name == "gate":
                    dve.wait_ge(rexps_ready, b + 1)
                    own.link(v.reciprocal(erec[:, :], esum[:, :]))
                    own.link(v.tensor_tensor(pdif[:, :], etop[:, :, 1], etop[:, :, 0], ALU.subtract))
                    ins = v.tensor_tensor(pdif[:, :], pdif[:, :], erec[:, :], ALU.mult)
                    ins.then_inc(pdif_ready, 1)
                    dve.wait_ge(pexp_ready, b + 1)
                    own.link(v.tensor_scalar(den[:, :], pexp[:, :], 1.0, None, ALU.add))
                    own.link(v.reciprocal(cw[:, 0, :], den[:, :]))
                    own.link(v.tensor_tensor(cw[:, 1, :], pexp[:, :], cw[:, 0, :], ALU.mult))
                elif name == "rank":
                    dve.wait_ge(work_filled, w.filled)
                    o = w_bank[w.bank]
                    own.link(v.tensor_tensor(run1[:, :], run[:, :], o[:, 2 * E:3 * E], ALU.add))
                    v.tensor_tensor(place[:, 0, :], o[:, 0:E], run[:, :], ALU.add)
                    own.link(v.tensor_tensor(place[:, 1, :], o[:, E:2 * E], run1[:, :], ALU.add))
                    v.tensor_tensor(run[:, :], run1[:, :], o[:, 3 * E:4 * E], ALU.add).then_inc(places_ready, 1)
                    for k in range(TOPK):
                        for tt in range(QT_N):
                            own.link(v.tensor_tensor(picked[:, :], hot[k][:, tt, :], place[:, tt, :], ALU.mult))
                            own.link(v.tensor_reduce(slotf[:, k, tt:tt + 1], picked[:, :], AX, ALU.add))
                    if not first:
                        dve.wait_ge(dispatched, b * (16 * QT_N * TOPK))
                    v.tensor_copy(slot[:, :, :], slotf[:, :, :])
                    v.tensor_copy(rows[:, :, :, D:D + 1].bitcast(I32), idf[:, :, :, None])
                    own.link(v.tensor_copy(rows[:, :, :, D + 1:D + 2], cw[:, :, :, None]))
                    v.tensor_scalar(idf[:, :, :], idf[:, :, :], float(S), None, ALU.add).then_inc(slots_ready, 1)

            v.tensor_copy(pad_row[:, :], run[:, :]).then_inc(ends_ready, 1)
            own.link(v.tensor_tensor(nb[:, :], run[:, :], base[:, :], ALU.subtract))
            own.link(v.tensor_scalar(nb[:, :], nb[:, :], float(P - 1), None, ALU.add))
            own.link(v.tensor_copy(nbi[:, :], nb[:, :]))
            own.link(v.tensor_single_scalar(nbi[:, :], nbi[:, :], P.bit_length() - 1, ALU.arith_shift_right))
            own.link(v.tensor_copy(nb[:, :], nbi[:, :]))
            own.link(v.tensor_tensor_scan(cum[:, :], ones8[:, :], nb[:, :], 0.0, ALU.mult, ALU.add))
            wide = lambda x: x[:, None, :].to_broadcast([P, NBLK, E])
            own.link(v.tensor_tensor(ge, jgrid[:, :, None].to_broadcast([P, NBLK, E]), wide(cum), ALU.is_ge))
            own.link(v.tensor_reduce(blkf, ge, AX, ALU.add))
            own.link(v.tensor_tensor(ge, ge, wide(nb), ALU.mult))
            own.link(v.tensor_reduce(skipped, ge, AX, ALU.add))
            own.link(v.tensor_tensor(skipped, jgrid[:, :], skipped, ALU.subtract))
            own.link(v.tensor_scalar(skipped, skipped, float(P), None, ALU.mult))
            own.link(v.scalar_tensor_tensor(out=blk_row[:, :], in0=blkf, scalar=float(REGION), in1=skipped, op0=ALU.mult, op1=ALU.add))
            v.tensor_scalar(blk_e[:, :], blkf, float(E - 1), None, ALU.min).then_inc(tables_ready, 1)

            h_bank, y_bank = bank[0:2], bank[6:8]
            moe = Chain(dve, dve_moe, 2 * RING, (NBLK - 2) // RING)

            def jv(j, add):
                return j + add if isinstance(j, int) else j[1] * RING + (j[2] + add)

            def take_h(j):
                n = j if isinstance(j, int) else j[2]
                for h in range(2):
                    dve.wait_ge(h_filled, 2 * jv(j, 0) + h + 1)
                    if n > 0 and h == 0:
                        dve.wait_ge(hT_filled, jv(j, 0))
                    v.tensor_copy(hid[:, h * 512:h * 512 + 512], h_bank[h][:, :]).then_inc(h_ready, 1)

            def take_y(j):
                n = j if isinstance(j, int) else j[2]
                s = n % RING
                dve.wait_ge(yb_filled, jv(j, 1))
                moe.link(v.tensor_tensor(y_sum, y_bank[n % 2][:, 0:D], b2b[s], ALU.add))
                moe.link(v.tensor_scalar(y_sum, y_sum, xb[s][:, D + 1:D + 2], None, ALU.mult))
                v.scalar_tensor_tensor(out=xb[s][:, 0:D], in0=xb[s][:, 0:D], scalar=1.0 / TOPK, in1=y_sum, op0=ALU.mult, op1=ALU.add).then_inc(y_ready, 1)
                dve.wait_ge(y_ready, jv(j, 1))

            take_h(0)
            turns = (NBLK - 2) // RING
            with dve.Fori(0, turns) as i:
                moe.enter(i)
                for s in range(RING):
                    take_h(("loop", i, s + 1))
                    take_y(("loop", i, s))
                moe.leave()
            for j in range(turns * RING + 1, NBLK):
                take_h(j)
                take_y(j - 1)
            take_y(NBLK - 1)

            tail = Chain(dve, dve_tail, 3 * TAIL, B // TAIL)

            def total(i, s):
                k = "AB"[s % 2]
                dve.wait_ge(parts_loaded[s], i * 32 + 32)
                x = tail_x[s]
                tail.link(v.tensor_tensor(x, x, tail_y[s][:, 1, :, :], ALU.add))
                for tt in range(QT_N):
                    ins = v.bn_stats(stats[k][:, tt, :], x[:, tt, :])
                tail.link(ins)
                dve.sem_inc(held["dve"], 1)
                for tt in range(QT_N):
                    ins = v.bn_aggr(mv[k][:, tt, :], stats[k][:, tt, :])
                tail.link(ins)
                v.tensor_scalar(var[k][:, :], mv[k][:, :, 1], EPS, None, ALU.add).then_inc(tail_var, 1)

            def scaled(i, s):
                k, x = "AB"[s % 2], tail_x[s]
                dve.wait_ge(tail_rstd, TAIL * i + (s + 1))
                for tt in range(QT_N):
                    ins = v.tensor_scalar(x[:, tt, :], x[:, tt, :], mv[k][:, tt, 0:1], rstd[k][:, tt:tt + 1], ALU.subtract, ALU.mult)
                ins.then_inc(tail_z, 1)

            with dve.Fori(0, B // TAIL) as i:
                tail.enter(i)
                for s in range(TAIL + 1):
                    if s < TAIL:
                        total(i, s)
                    if s > 0:
                        scaled(i, s - 1)
                tail.leave()


DVE_LINKS = 24
POOL_LINKS = 2

_SHORT = {"ctx": "ctx_1024", "x": "x"}
_LAYER = ["sa_wq", "sa_bq", "sa_wk", "sa_bk", "sa_wv", "sa_bv", "sa_wo", "sa_bo", "ca_wq", "ca_bq", "ca_wk", "ca_bk", "ca_wv", "ca_bv",
          "ca_wo", "ca_bo", "ln1_g", "ln1_b", "ln2_g", "ln2_b", "ln3_g", "ln3_b", "router_w", "router_b", "e_w1", "e_b1", "e_w2", "e_b2"]


def kernel(**inputs):
    import numpy as np
    import concourse.bacc as bacc
    from concourse.bass_utils import run_bass_kernel_spmd

    nc = bacc.Bacc("TRN2", target_bir_lowering=False, num_devices=1)
    names = {**_SHORT, **{k: f"L0_xattn_{k}" for k in _LAYER}}
    arrays, aps = {}, {}
    for short, name in names.items():
        a = np.ascontiguousarray(inputs[name])
        arrays[f"in_{short}"] = a
        aps[short] = nc.dram_tensor(f"in_{short}", a.shape, mybir.dt.from_np(a.dtype), kind="ExternalInput").ap()
    out = nc.dram_tensor("layer_out", (B, S, D), F32, kind="ExternalOutput").ap()
    decoder_layer(nc, aps, out)
    r = run_bass_kernel_spmd(nc, [arrays], core_ids=[0])
    return r.results[0]["layer_out"]
```

```python
from contextlib import ExitStack

import concourse.bass as bass
from concourse import mybir

ALU = mybir.AluOpType
ACT = mybir.ActivationFunctionType
AX = mybir.AxisListType.X
F32 = mybir.dt.float32
BF16 = mybir.dt.bfloat16
I32 = mybir.dt.int32
U32 = mybir.dt.uint32

P = 128
B, S, D = 8, 256, 256
H = 16
HD = D // H
SE = 77
E, FF, TOPK = 8, 1024, 2
T = B * S
QT_N = S // P
DC = D // P
FC = FF // P
HC = H // DC
STRIPS = 4
EPS = 1e-5
MASKED = -1e30

ROW = D + 2
REGION = T + P
NBLK = T * TOPK // P + E - 1
NDUMMY = NBLK - T * TOPK // P
XS_ROWS = E * REGION + NDUMMY * P
Y_PAD = T * TOPK
Y_ROWS = Y_PAD + (E + NDUMMY) * P

UA, UB = 12, 8
UNITS = UA + UB
PARTS = 3
OTHER_PAIRS = ((0, 1), (1, 2), (0, 2))
KROWS = (PARTS + len(OTHER_PAIRS)) * HD
STACKS = 16 * (1 + len(OTHER_PAIRS))
LATE = 5
SB = 3
PB = 4
TURN_LAG, LAG = 3, 5
TURN0, TURN1 = 1, B - 2
NL = TURN1 - TURN0
SUMMED_BY_DVE = (0,)
SHIFTED_BY_DVE = (4, 6, 7)
RING = 4
EARLY = 2 * RING
EARLY_BATCHES = B - 2
EARLY_BEFORE = 2
LATER = NBLK - EARLY
assert EARLY_BATCHES * S * TOPK - E * (P - 1) > (EARLY - 1) * P


def a_unit(m):
    c, r = divmod(m, 6)
    return (c, 0, range(4 * r, 4 * r + 4), P) if r < 2 else (c, 1, range(2 * r - 4, 2 * r - 2), S)


def b_unit(m):
    q, c, par = m // 4, m // 2 % 2, m % 2
    return c, q, range(4 * par, 4 * par + 4), SE


def head_of(c, slot):
    return c * HC + 2 * (slot % STRIPS) + slot // STRIPS


class WorkUse:

    def __init__(self, n, at, had):
        self.bank, self.filled, self.had = n % 2, at(n + 1), had


class Unit:

    def __init__(self, what, n, pos, at, at_half, freed, after):
        self.kind, self.b, self.m = what
        self.bank, self.buf, self.turn = pos % SB, pos % PB, n % 2
        self.done, self.turn_done, self.freed, self.after = at(n + 1), at_half(n // 2 + 1), freed, after
        self.turn_freed = at_half(n // 2) if n >= 2 else None


def counted(j, add):
    return j + add if isinstance(j, int) else j[1] * RING + (j[2] + add)


def units_to(kind, b):
    if kind == "A":
        return UA if isinstance(b, int) and b == 0 else b * UNITS + (2 * UA - UNITS)
    return UNITS * B if isinstance(b, int) and b == B - 1 else b * UNITS + (UNITS + UA)


BESIDE = (
    (0, "p", "rTB"), (1, "a", "xres"), (2, "p", "RB"), (2, "b", "zA"), (3, "p", "oTB"), (3, "b", "x1T"), (4, "b", "q2"), (4, "b", "q2m"),
    (5, "b", "v2"), (6, "a", "cT"), (7, "p", "woB"), (8, "p", "nB"), (8, "b", "x1res"), (8, "f", "xT"), (8, "p", "zB"), (9, "a", "k2"),
    (11, "f", "k"), (11, "f", "km"), (11, "f", "q"), (11, "p", "x2T"), (13, "p", "route"), (13, "a", "k2m"), (14, "f", "qm"), (14, "a", "rTA"),
    (14, "p", "gate"), (16, "p", "rank"), (16, "a", "oTA"), (16, "a", "RA"), (16, "f", "v"), (17, "a", "woA"), (19, "a", "nA"))


EARLY_STEPS = (
    ((0, "table", 0), (3, "eW", 0), (3, "eT", 0), (4, "eU", 0), (4, "eT", 1), (5, "eW", 1), (7, "eU", 1), (8, "eW", 2), (8, "eD", 0)),
    ((4, "eT", 2), (5, "eU", 2), (5, "eW", 3), (6, "eT", 3), (9, "eD", 1), (9, "eU", 3), (9, "eT", 4), (9, "eW", 4), (9, "eD", 2), (9, "eW", 5),
     (11, "eU", 4), (11, "eT", 5), (14, "eD", 3), (16, "eU", 5), (16, "eT", 6), (16, "pads", 0), (16, "eW", 6), (16, "later", 0), (16, "eD", 4), (17, "eU", 6),
     (17, "eW", 7), (17, "eT", 7), (17, "eD", 5), (17, "eU", 7), (19, "eW", 8), (19, "eT", 8), (19, "eD", 6)))
EARLY_W2 = [E - 2 if j < EARLY_BEFORE or j % 2 else E - 4 for j in range(EARLY)]


def turn_steps(a, f, b, p):
    units = {}
    if a is not None:
        units.update({m: ("A", a, m) for m in range(UA)})
    if b is not None:
        units.update({UA + m: ("B", b, m) for m in range(UB)})
    if p is not None:
        units.update({UA + m - UNITS: ("B", p, m) for m in range(UB)})

    roles = {"a": a, "f": f, "b": b, "p": p}
    beside = [(step, name, roles[role]) for step, role, name in BESIDE if roles[role] is not None]
    if f is None and a is None:
        beside += EARLY_STEPS[p - (B - 2)]
    for k in range(UNITS):
        for name, at in (("scores", k), ("turn", k - TURN_LAG), ("values", k - LAG)):
            if at in units and (name != "scores" or at >= 0):
                yield name, units[at]
        for step, name, batch in beside:
            if step == k:
                yield name, batch


def batch_script(loop):
    no_bank = {"nA", "nB", "zA", "zB", "oTA", "oTB", "gate", "xres", "x1res", "km", "qm", "k2m", "q2m", "eW", "eT", "eU", "eD", "pads", "table", "later"}
    bank_n, unit_n = 0, 0
    had, s_had, o_had = [None, None], [None] * SB, None
    seen = {}

    def numbered(t, i, bank_step, unit_step):
        nonlocal bank_n, unit_n, o_had
        steps, p = turn_steps(*batches(t)), t - 1
        at_bank = lambda n: n if i is None else i * bank_step + n
        at_unit = lambda n: n if i is None else i * unit_step + n
        at_half = lambda n: n if i is None else i * (unit_step // 2) + n
        pos = 0
        units = {("B", m): Unit(("B", p, m), n, pos_, at_unit, at_half, None, None) for m, (n, pos_) in seen.items()}
        for name, what in steps:
            if name == "scores":
                kind, b, m = what
                k = pos % SB
                units[what[0], m] = Unit(what, unit_n, pos, at_unit, at_half, None if s_had[k] is None else at_unit(s_had[k] + 1),
                                         o_had if m == 0 else None)
                if kind == "B":
                    seen[m] = unit_n, pos
                s_had[k] = unit_n
                if m == 0:
                    o_had = (kind, b)
                unit_n, pos = unit_n + 1, pos + 1
            if name in ("scores", "turn", "values"):
                yield name, units[what[0], what[2]], None
            elif name in no_bank:
                yield name, what, None
            else:
                w = WorkUse(bank_n, at_bank, had[bank_n % 2])
                had[bank_n % 2] = name, what
                bank_n += 1
                yield name, what, w

    def batches(t):
        return [x if not isinstance(x, int) or 0 <= x < B else None for x in (t + 1, t + 2, t, t - 1)]

    for t in range(-2, TURN0):
        yield from numbered(t, None, 0, 0)
    steady = list(turn_steps(*batches(TURN0)))
    per_bank = sum(name not in no_bank | {"scores", "turn", "values"} for name, _ in steady)
    assert per_bank % 2 == 0 and unit_n % 2 == 0
    yield "enter", None, None
    i = loop()
    t = i + TURN0
    bank_0, unit_0 = bank_n, unit_n
    had[:] = [(name, what - TURN0 + t) for name, what in had]
    o_had = o_had[0], o_had[1] - TURN0 + t
    s_0, had_0 = [n - unit_n for n in s_had], [name for name, _ in had]
    yield from numbered(t, i, per_bank, UNITS)
    assert bank_n - bank_0 == per_bank and unit_n - unit_0 == UNITS
    assert s_0 == [n - unit_n for n in s_had] and had_0 == [name for name, _ in had]
    bank_n, unit_n = bank_0 + per_bank * NL, unit_0 + UNITS * NL
    s_had[:] = [n + UNITS * (NL - 1) for n in s_had]
    seen.update({m: (n + UNITS * (NL - 1), pos) for m, (n, pos) in seen.items()})
    last = [(name, what) for name, what in turn_steps(*batches(TURN1 - 1)) if name not in no_bank | {"scores", "turn", "values"}][-2:]
    had[bank_n % 2], had[(bank_n + 1) % 2] = last
    o_had = "B", TURN1 - 1
    yield "leave", None, None
    for t in range(TURN1, B + 1):
        yield from numbered(t, None, 0, 0)


class Chain:

    def __init__(self, eng, sem, per, turns):
        self.eng, self.sem, self.per, self.turns, self.n, self.i = eng, sem, per, turns, 0, None

    def enter(self, i):
        self.i, self.before = i, self.n

    def leave(self):
        assert self.n - self.before == self.per, ("links in the loop", self.n - self.before)
        self.n, self.i = self.before + self.per * self.turns, None

    def link(self, ins):
        self.n += 1
        ins.then_inc(self.sem, 1)
        self.eng.wait_ge(self.sem, self.n if self.i is None else self.n + self.per * self.i)


def decoder_layer(nc, t, out):
    ctx = ExitStack()
    with ctx:
        def sb(name, shape, dt=F32):
            return ctx.enter_context(nc.sbuf_tensor(name, shape, dt))

        def sem(name):
            return ctx.enter_context(nc.semaphore(name))

        xs_dram = nc.dram_tensor("dispatched", (XS_ROWS, ROW), F32, kind="Internal").ap()
        parts_dram = {k: nc.dram_tensor(f"{k}_parts", (DC, P, PARTS, S if k != "k2" else SE), BF16, kind="Internal").ap() for k in ("q", "k", "q2", "k2")}
        y_dram = nc.dram_tensor("expert_rows", (Y_ROWS, D), F32, kind="Internal").ap()

        w1 = sb("w1", [P, DC, E, FF])
        w2 = sb("w2", [P, E, FC, D])
        place_of = lambda e: w2[:, e, :, :].rearrange("p f d -> p (f d)")
        qS = place_of(E - 1).bitcast(BF16).rearrange("p (h n) -> p h n", h=H)
        kS = place_of(E - 2).bitcast(BF16).rearrange("p (h n) -> p h n", h=H)
        q2S = place_of(E - 4).bitcast(BF16).rearrange("p (h n) -> p h n", h=H)
        probsT = [place_of(E - 3)[:, 512 * k:512 * k + 512] for k in range(PB)]
        in_parts = place_of(E - LATE).bitcast(BF16)
        q_parts, k_parts = (in_parts[:, PARTS * DC * S * k:PARTS * DC * S * (k + 1)].rearrange("p (a c n) -> p a c n", a=PARTS, c=DC) for k in range(2))
        k2_parts = sb("k2_split", [P, PARTS, DC, SE], BF16)
        rexp = place_of(E - LATE)[:, PARTS * DC * S:PARTS * DC * S + DC * S].rearrange("p (c n) -> p c n", c=DC)
        SHARED = 5120
        shared = sb("shared", [P, SHARED])
        at = [0]

        def part(n):
            at[0] += n
            assert at[0] <= SHARED, at[0]
            return shared[:, at[0] - n:at[0]]
        wA = {k: part(DC * D).rearrange("p (k n) -> p k n", k=DC) for k in ("wq", "wk", "wv", "wo")}
        x_in = part(QT_N * D).rearrange("p (t d) -> p t d", t=QT_N)
        xres = part(QT_N * D).rearrange("p (t d) -> p t d", t=QT_N)
        qT = part(DC * S).rearrange("p (c n) -> p c n", c=DC)
        kT = part(DC * S).rearrange("p (c n) -> p c n", c=DC)
        vz = part(QT_N * H * 32).rearrange("p (t n) -> p t n", t=QT_N)
        at[0] = 0
        xb = [part(ROW) for _ in range(RING)]
        b2b = [part(D) for _ in range(RING)]
        xbT = part(DC * P).rearrange("p (c n) -> p c n", c=DC)
        gT = [part(FF).rearrange("p (f n) -> p f n", f=FC) for _ in range(2)]
        y_sum = part(D)
        ge = part(LATER * E).rearrange("p (j e) -> p j e", j=LATER)
        skipped, blkf = part(LATER), part(LATER)
        y_a = xres

        wB_all = sb("w_cross", [P, 4, DC, D])
        wB = {k: wB_all[:, n, :, :] for n, k in enumerate(("wq", "wk", "wv", "wo"))}
        w1_later = wB_all[:, :, :, :].rearrange("p a k n -> p (a k n)").rearrange("p (k f) -> p k f", k=DC)
        w1_early = place_of(E - 1).rearrange("p (k f) -> p k f", k=DC)
        vecs = {k: sb(k, [P, D]) for k in ("bvA", "boA", "bvB", "boB", "g1", "be1", "g2", "be2", "g3", "be3")}
        rw = sb("router_w", [P, DC, E])
        rb = sb("router_b", [P, E])
        bias_rows, b1_rows = w2[0:4 * DC, E - 1, 0, 0:P], w2[0:E * FC, E - 1, 1, 0:P]
        bias = sb("bias", [P, 4 * DC])
        b1 = sb("b1", [P, E * FC])

        xT = sb("xT", [P, DC, S])
        q2T = sb("q2T", [P, DC, S])
        x12T = sb("x12T", [P, DC, S])
        x1 = sb("x1", [P, QT_N, D])
        x1res = sb("x1res", [P, QT_N, D])
        ctx_in = sb("ctx_in", [SE, D])
        cT = sb("cT", [P, DC, SE])
        k2T = sb("k2T", [P, DC, SE])
        k2S = sb("k2S", [P, H, SE], BF16)
        v2z = sb("v2z", [SE, H * 32])
        probs = [sb(f"probs{k}", [P, 512]) for k in range(PB)]
        nmax = [sb(f"nmax{k}", [P, 4]) for k in range(SB)]
        sums = {k: sb(f"sums{k}", [P, QT_N, H]) for k in "AB"}
        rinv = {k: sb(f"rinv{k}", [P, QT_N, H]) for k in "AB"}
        rT = sb("rT", [H, S])
        oT = sb("oT", [P, DC, S])
        rows = sb("rows", [P, TOPK, QT_N, ROW])
        y_b = rows[:, 1, :, 0:D]
        stats = {k: sb(f"stats{k}", [P, QT_N, 6]) for k in "AB"}
        mv = {k: sb(f"mv{k}", [P, QT_N, 2]) for k in "AB"}
        var = {k: sb(f"var{k}", [P, QT_N]) for k in "AB"}
        rstd = {k: sb(f"rstd{k}", [P, QT_N]) for k in "AB"}
        lg = sb("logits", [P, QT_N, E])
        top = sb("top", [P, QT_N, 8])
        topi = sb("topi", [P, QT_N, 8], U32)
        topf = sb("topf", [P, QT_N, TOPK])
        ntop = sb("ntop", [P, QT_N])
        etop = sb("etop", [P, QT_N, 8])
        esum = sb("esum", [P, QT_N])
        erec = sb("erec", [P, QT_N])
        pdif = sb("pdif", [P, QT_N])
        pexp = sb("pexp", [P, QT_N])
        den = sb("den", [P, QT_N])
        cw = sb("cw", [P, TOPK, QT_N])
        hot = sb("hot", [P, TOPK, QT_N, E])
        member = sb("member", [P, QT_N, E], BF16)
        run = sb("run", [P, E])
        run1 = sb("run1", [P, E])
        base = sb("base", [P, E])
        place = sb("place", [P, QT_N, E])
        picked = sb("picked", [P, TOPK, QT_N, E])
        slotf = sb("slotf", [P, TOPK, QT_N])
        slot = sb("slot", [P, TOPK, QT_N], U32)
        idf = sb("idf", [P, TOPK, QT_N])

        ident = sb("ident", [P, P])
        identb = sb("identb", [P, P], BF16)
        causal = sb("causal", [P, S], BF16)
        before = sb("before", [P, P], BF16)
        onesb = sb("onesb", [P, P], BF16)
        spread = sb("spread", [H, DC, P])
        iota8 = sb("iota8", [P, E])
        half = sb("half", [P, QT_N])
        dummy_meta = sb("dummy_meta", [P, NDUMMY, 2])
        jgrid = sb("jgrid", [P, LATER])
        jlater = sb("jlater", [P, LATER])
        ge_early = sb("ge_early", [P, EARLY, E])
        skipped_early, blkf_early = sb("skipped_early", [P, EARLY]), sb("blkf_early", [P, EARLY])
        early_of = sb("early_of", [P, E])
        early_next = sb("early_next", [P, E])
        pad_rows = sb("pad_rows", [P, D + 2 * E])
        nb = sb("nb", [P, E])
        weighed = sb("weighed", [P, E])
        nbi = sb("nbi", [P, E], I32)
        ones8 = sb("ones8", [P, E])
        cum = sb("cum", [P, E])
        blk_row = sb("blk_row", [P, NBLK], I32)
        blk_e = sb("blk_e", [P, NBLK], I32)
        pad_row = sb("pad_row", [P, E], I32)

        bank = [ctx.enter_context(nc.psum_tensor(f"bank{k}", [P, 512], F32)) for k in range(8)]
        s_bank, t_bank, w_bank, o_bank = bank[0:SB], bank[SB:5], bank[5:7], bank[7]

        consts_dve = sem("consts_dve")
        consts_pool = sem("consts_pool")
        ident_ready = sem("ident_ready")
        pool_own = sem("pool_own")
        pool_late = sem("pool_late")
        dve_own = sem("dve_own")
        dve_moe = sem("dve_moe")
        dve_tail = sem("dve_tail")
        wqk_loaded, wvo_loaded, wB_loaded = sem("wqk_loaded"), sem("wvo_loaded"), sem("wB_loaded")
        vecA_loaded, vec_loaded = sem("vecA_loaded"), sem("vec_loaded")
        rows_loaded = sem("rows_loaded")
        bias_turned, bias_ready = sem("bias_turned"), sem("bias_ready")
        experts_loaded, late_loaded = sem("experts_loaded"), sem("late_loaded")
        x_loaded, ctx_loaded = sem("x_loaded"), sem("ctx_loaded")
        work_filled = sem("work_filled")
        xT_ready, xres_ready = sem("xT_ready"), sem("xres_ready")
        q_ready, kT_ready, vz_ready = sem("q_ready"), sem("kT_ready"), sem("vz_ready")
        high_ready, left_ready, middle_ready, parts_ready, parts_written, stacked = (
            {k: sem(f"{n}_{k}") for k in ("q", "k", "q2", "k2")} for n in
            ("high_ready", "left_ready", "middle_ready", "parts_ready", "parts_written", "stacked"))
        cT_ready, k2T_ready, v2z_ready = sem("cT_ready"), sem("k2T_ready"), sem("v2z_ready")
        x1T_ready, q2_ready, x2T_ready = sem("x1T_ready"), sem("q2_ready"), sem("x2T_ready")
        scores_ready, max_ready, probs_ready = sem("scores_ready"), sem("max_ready"), sem("probs_ready")
        turned = sem("turned")
        probsT_ready = [sem(f"probsT_ready{k}") for k in range(2)]
        values_done = sem("values_done")
        rinv_ready, rT_ready, rexp_ready, oT_ready = ({k: sem(f"{n}{k}") for k in "AB"} for n in
                                                      ("rinv_ready", "rT_ready", "rexp_ready", "oT_ready"))
        var_ready, rstd_ready, z_ready = ({k: sem(f"{n}{k}") for k in "AB"} for n in
                                          ("var_ready", "rstd_ready", "z_ready"))
        x1_ready, x1res_ready, x2_ready, rows_ready = sem("x1_ready"), sem("x1res_ready"), sem("x2_ready"), sem("rows_ready")
        rmax_ready, rexps_ready, pdif_ready, pexp_ready = sem("rmax_ready"), sem("rexps_ready"), sem("pdif_ready"), sem("pexp_ready")
        held = {k: sem(f"held_{k}") for k in ("pool", "dve", "sp")}
        sum_ready = {k: sem(f"sum_ready{k}") for k in "AB"}
        logits_ready, places_ready = sem("logits_ready"), sem("places_ready")
        member_ready, slots_ready = sem("member_ready"), sem("slots_ready")
        dispatched = sem("dispatched_rows")
        dummies_written, pads_written, tables_ready = sem("dummies_written"), sem("pads_written"), sem("tables_ready")
        pad_rows_ready, ends_ready = sem("pad_rows_ready"), sem("ends_ready")
        early_tables_ready = sem("early_tables_ready")
        early_w2_loaded = {e: sem(f"early_w2_loaded{e}") for e in sorted(set(EARLY_W2))}
        blk_loaded = [sem(f"blk_loaded{k}") for k in range(RING)]
        y_written = [sem(f"y_written{k}") for k in range(RING)]
        xbT_filled, xbT_ready = sem("xbT_filled"), sem("xbT_ready")
        w1_now_ready, hT_filled, gelu_ready = sem("w1_now_ready"), sem("hT_filled"), sem("gelu_ready")
        yb_filled, y_ready = sem("yb_filled"), sem("y_ready")
        parts_loaded = [sem(f"parts_loaded{k}") for k in range(B)]
        sum_filled, stats_ready, tail_var_ready, tail_rstd_ready = sem("sum_filled"), sem("stats_ready"), sem("tail_var_ready"), sem("tail_rstd_ready")
        tail_z_ready, tail_g_ready, tail_out = sem("tail_z_ready"), sem("tail_g_ready"), [sem(f"tail_out{k}") for k in range(B)]
        out_written = sem("out_written")

        w1_flat = w1[:, :, :, :].rearrange("p k e f -> p (k e f)")
        G = QT_N * D
        tail_y = [w1_flat[:, TOPK * G * s:TOPK * G * (s + 1)].rearrange("p (k t d) -> p k t d", k=TOPK, t=QT_N) for s in range(B)]
        tail_x = [y[:, 0, :, :] for y in tail_y]
        tail_sum = [(tail_x[s] if s in SUMMED_BY_DVE else bank[s][:, :].rearrange("p (t d) -> p t d", t=QT_N)) for s in range(B)]
        at[0] = TOPK * G * B

        def tail_part(n):
            at[0] += n
            return w1_flat[:, at[0] - n:at[0]]
        tail_stats = [tail_part(QT_N * 6).rearrange("p (t n) -> p t n", t=QT_N) for _ in range(B)]
        tail_mv = [tail_part(QT_N * 2).rearrange("p (t n) -> p t n", t=QT_N) for _ in range(B)]
        tail_var, tail_rstd, tail_shift = ([tail_part(QT_N) for _ in range(B)] for _ in range(3))

        taken = {"xT": xT_ready, "q": q_ready, "k": kT_ready, "v": vz_ready, "cT": cT_ready, "k2": k2T_ready, "v2": v2z_ready, "x1T": x1T_ready,
                 "q2": q2_ready, "x2T": x2T_ready, "route": logits_ready, "rank": places_ready}
        for k in "AB":
            taken.update({"rT" + k: rT_ready[k], "R" + k: rexp_ready[k], "wo" + k: sum_ready[k]})

        def y_of(n):
            return bank[7 if n < EARLY else 6 + n % 2][:, 0:D]

        operand = {"k": (kT, k_parts), "q": (qT, q_parts), "k2": (k2T, k2_parts), "q2": (q2T, q_parts)}

        high_at = lambda k: 0 if k[0] == "q" else PARTS - 1

        def leave_high(eng, k, b):
            src, parts = operand[k]
            eng.wait_ge(high_ready[k], b + 1)
            eng.tensor_tensor(src[:, :, :], src[:, :, :], parts[:, high_at(k), :, :], ALU.subtract).then_inc(left_ready[k], 1)

        def leave_middle(eng, k, b):
            src, parts = operand[k]
            eng.wait_ge(middle_ready[k], b + 1)
            eng.tensor_tensor(parts[:, PARTS - 1 - high_at(k), :, :], src[:, :, :], parts[:, 1, :, :], ALU.subtract).then_inc(parts_ready[k], 1)

        def splits(name, b):
            return "dve" if isinstance(b, int) and b == 0 and name[:2] not in ("q2", "k2") else "pool"

        block = ctx.enter_context(nc.Block())

        def turns_on(kind, m):
            return "act" if (kind, m) in [('A', 5), ('B', 1), ('B', 2), ('B', 4), ('B', 5), ('B', 6)] else "dve"

        def write_pads(eng, experts):
            eng.wait_ge(pad_rows_ready, 1)
            eng.wait_ge(ends_ready, 1)
            for e in experts:
                r = eng.value_load(pad_row[0:1, e:e + 1], min_val=e * REGION, max_val=e * REGION + T)
                eng.dma_start(xs_dram[bass.ds(r, P), :], pad_rows[:, 2 * e:2 * e + ROW]).then_inc(pads_written, 16)

        @block.sync
        def _(sp):
            def load_x(b):
                sp.dma_start(x_in, t["x"][bass.ds(b, 1), :, :].rearrange("a (t p) d -> p (a t) d", p=P)).then_inc(x_loaded, 16)

            def load_ctx(b):
                sp.dma_start(ctx_in[:, :], t["ctx"][bass.ds(b, 1), :, :].rearrange("a s d -> s (a d)")).then_inc(ctx_loaded, 16)

            load_x(0)
            for k in ("wk", "wq"):
                sp.dma_start(wA[k], t[f"sa_{k}"].rearrange("(k p) n -> p k n", p=P)).then_inc(wqk_loaded, 16)
            for n, v in enumerate(("sa_bq", "sa_bk", "ca_bq", "ca_bk")):
                sp.dma_start(w2[DC * n:DC * n + DC, E - 1, 0, 0:P], t[v].rearrange("(c p) -> c p", p=P)).then_inc(rows_loaded, 16)
            sp.dma_start(b1_rows, t["e_b1"].rearrange("e (f p) -> (e f) p", p=P)).then_inc(rows_loaded, 16)
            for k in ("wv", "wo"):
                sp.dma_start(wA[k], t[f"sa_{k}"].rearrange("(k p) n -> p k n", p=P)).then_inc(wvo_loaded, 16)
            def load_row(k, v, loaded):
                sp.dma_start(vecs[k][:, :], t[v].rearrange("(a n) -> a n", a=1).to_broadcast([P, D])).then_inc(loaded, 16)

            load_row("bvA", "sa_bv", vecA_loaded)
            load_row("boA", "sa_bo", vecA_loaded)

            def wait(ready, n):
                sp.wait_ge(ready, n)
                if not isinstance(n, int):
                    sp.sem_inc(held["sp"], 1)

            def next_x(b):
                wait(xT_ready, b)
                wait(xres_ready, b)
                load_x(b)

            def next_ctx(b):
                wait(cT_ready, b)
                load_ctx(b)

            def stack(b, *names):
                forms = {"q": (q_parts, qS), "k": (k_parts, kS), "q2": (q_parts, q2S), "k2": (k2_parts[:, :, :, :], k2S)}
                first = isinstance(b, int) and b == 0
                for k in names:
                    wait(parts_ready[k], b + 1)
                    if not first:
                        wait(stacked[k], b * STACKS)
                    sp.dma_start(parts_dram[k].rearrange("c p a n -> p a c n"), forms[k][0]).then_inc(parts_written[k], 16)
                for k in names:
                    wait(parts_written[k], b * 16 + 16)
                    if not first:
                        wait(scores_ready, units_to("B" if k[-1] == "2" else "A", b - 1))
                    sp.dma_start(forms[k][1][0:PARTS * HD, :, :], parts_dram[k].rearrange("c (h x) a n -> (x a) (c h) n", x=HD)).then_inc(stacked[k], 16)
                    for n, pair in enumerate(OTHER_PAIRS):
                        part_ = parts_dram[k][:, :, pair[0 if k[0] == "q" else 1], :].rearrange("c (h x) n -> x (c h) n", x=HD)
                        sp.dma_start(forms[k][1][HD * (PARTS + n):HD * (PARTS + n + 1), :, :], part_).then_inc(stacked[k], 16)

            def turn_of_loads(a, f, b):
                if f is not None and not (isinstance(f, int) and f == 0):
                    next_x(f)
                if a is not None and not (isinstance(a, int) and a == 0):
                    next_ctx(a)
                if b is not None:
                    stack(b, "q2")
                if f is not None:
                    stack(f, "k", "q")
                if a is not None:
                    stack(a, "k2")

            def load_w1(e):
                sp.dma_start(w1[:, :, bass.ds(e, 1), :].rearrange("p k a f -> p k (a f)"), t["e_w1"][bass.ds(e, 1), :, :].rearrange("a (k p) n -> p (a k) n", p=P)).then_inc(experts_loaded, 16)

            turn_of_loads(None, 0, None)
            next_x(1)
            load_ctx(0)
            for k in ("wk", "wv", "wq", "wo"):
                sp.dma_start(wB[k], t[f"ca_{k}"].rearrange("(k p) n -> p k n", p=P)).then_inc(wB_loaded, 16)
            sp.dma_start(rw[:, :, :], t["router_w"].rearrange("(k p) n -> p k n", p=P)).then_inc(wB_loaded, 16)
            for k, v in (("g1", "ln1_g"), ("be1", "ln1_b"), ("bvB", "ca_bv"), ("boB", "ca_bo"), ("g2", "ln2_g"), ("be2", "ln2_b"), ("g3", "ln3_g"), ("be3", "ln3_b")):
                load_row(k, v, vec_loaded)
            sp.dma_start(rb[:, :], t["router_b"].rearrange("(a n) -> a n", a=1).to_broadcast([P, E])).then_inc(vec_loaded, 16)
            for e in range(E - LATE):
                sp.dma_start(w2[:, e, :, :], t["e_w2"][e, :, :].rearrange("(f p) n -> p f n", p=P)).then_inc(experts_loaded, 16)
            sp.wait_ge(vecA_loaded, 16 * 2)
            sp.wait_ge(consts_pool, 1)
            dummy = xs_dram[E * REGION:XS_ROWS, :].rearrange("(n p) d -> p n d", p=P)
            for n in range(NDUMMY):
                sp.dma_start(dummy[:, n, 0:D], vecs["boA"][:, :]).then_inc(dummies_written, 16)
            sp.dma_start(dummy[:, :, D:ROW], dummy_meta[:, :, :]).then_inc(dummies_written, 16)
            stack(1, "k", "q")
            stack(0, "k2")
            for e in range(0, E - NL - 1):
                load_w1(e)
            for turn in range(0, TURN0):
                turn_of_loads(turn + 1, turn + 2, turn)
            load_w1(E - NL - 1)
            with sp.Fori(0, NL) as i:
                turn_of_loads(i + (TURN0 + 1), i + (TURN0 + 2), i + TURN0)
                load_w1(i + (E - NL))
            turn_of_loads(TURN1 + 1, None, TURN1)

            def load_block(j, slot_, left):
                r = sp.value_load(blk_row[0:1, bass.ds(j, 1)], min_val=0, max_val=XS_ROWS - P)
                e = sp.value_load(blk_e[0:1, bass.ds(j, 1)], min_val=0, max_val=E - 1)
                if not isinstance(left, int) or left > 0:
                    sp.wait_ge(y_written[slot_], 16 * left)
                sp.dma_start(xb[slot_], xs_dram[bass.ds(r, P), :]).then_inc(blk_loaded[slot_], 16)
                sp.dma_start(b2b[slot_], t["e_b2"][bass.ds(e, 1), :].to_broadcast([P, D])).then_inc(blk_loaded[slot_], 16)

            def load_early_w2(j):
                e = sp.value_load(blk_e[0:1, j:j + 1], min_val=0, max_val=E - 1)
                sp.dma_start(w2[:, EARLY_W2[j], :, :], t["e_w2"][bass.ds(e, 1), :, :].rearrange("a (f p) n -> p (a f) n", p=P)).then_inc(early_w2_loaded[EARLY_W2[j]], 16)

            def load_late_w2(e):
                sp.dma_start(w2[:, e, :, :], t["e_w2"][e, :, :].rearrange("(f p) n -> p f n", p=P)).then_inc(late_loaded, 16)

            sp.wait_ge(early_tables_ready, 1)
            sp.wait_ge(sum_ready["A"], B)
            sp.wait_ge(dispatched, 16 * QT_N * TOPK * EARLY_BATCHES)
            load_block(0, 0, 0)
            load_early_w2(0)
            for j in range(1, RING):
                load_block(j, j, 0)
            turn_of_loads(None, None, B - 1)
            sp.wait_ge(yb_filled, 1)
            load_early_w2(1)
            sp.wait_ge(scores_ready, units_to("B", B - 1))
            load_early_w2(2)
            sp.wait_ge(oT_ready["B"], B)
            for e in (E - LATE, E - 3):
                load_late_w2(e)
            for j in range(RING, EARLY):
                load_block(j, j % RING, j // RING)
                sp.wait_ge(yb_filled, j - 2)
                load_early_w2(j - 1)
            write_pads(sp, range(0, E // 2))
            sp.wait_ge(tables_ready, 1)
            sp.wait_ge(dummies_written, 16 * (NDUMMY + 1))
            sp.wait_ge(pads_written, 16 * E)
            sp.wait_ge(dispatched, 16 * QT_N * TOPK * B)
            load_block(EARLY, EARLY % RING, EARLY // RING)
            sp.wait_ge(yb_filled, EARLY - 2)
            load_early_w2(EARLY - 1)
            load_block(EARLY + 1, (EARLY + 1) % RING, (EARLY + 1) // RING)
            sp.wait_ge(hT_filled, EARLY)
            load_late_w2(E - 1)
            for n in (2, 1):
                sp.wait_ge(yb_filled, EARLY + 1 - n)
                load_late_w2(EARLY_W2[EARLY - n])
            for j in range(EARLY + 2, EARLY + RING):
                load_block(j, j % RING, j // RING)
            with sp.Fori(0, (LATER - RING) // RING) as i:
                for s in range(RING):
                    load_block(i * RING + EARLY + RING + s, s, i + (EARLY // RING + 1))
            for j in range(NBLK // RING * RING, NBLK):
                load_block(j, j % RING, j // RING)

            for s in range(RING):
                sp.wait_ge(y_written[s], 16 * len(range(s, NBLK, RING)))

            for s in range(B):
                for k in range(TOPK):
                    sp.dma_start(tail_y[s][:, k, :, :], y_dram[s * S + k * T:s * S + k * T + S, :].rearrange("(t p) d -> p t d", p=P)).then_inc(parts_loaded[s], 16)
            for s in range(B):
                sp.wait_ge(tail_out[s], 1)
                sp.dma_start(out[s:s + 1, :, :].rearrange("a (t p) d -> p (a t) d", p=P), tail_x[s]).then_inc(out_written, 16)
            sp.wait_ge(out_written, 16 * B)

        @block.tensor
        def _(pe):
            def open_bank(w):
                if w.had is not None:
                    name, b = w.had
                    pe.wait_ge(taken[name], b + 1)
                return w_bank[w.bank]

            def turn4(w, src):
                o = open_bank(w)
                for c in range(DC):
                    for tt in range(QT_N):
                        last = nc.tensor.transpose(o[:, c * S + tt * P:c * S + tt * P + P], src[:, tt, c * P:c * P + P], ident[:, :])
                last.then_inc(work_filled, 1)

            def across(w, wt, src, n):
                o = open_bank(w)
                for c in range(DC):
                    for k in range(DC):
                        last = nc.tensor.matmul(o[:, c * n:c * n + n], wt[:, k, c * P:c * P + P], src[:, k, :], start=k == 0, stop=k == DC - 1)
                last.then_inc(work_filled, 1)

            def along(w, wt, src):
                o = open_bank(w)
                for tt in range(QT_N):
                    for k in range(DC):
                        last = nc.tensor.matmul(o[:, tt * D:tt * D + D], src[:, k, tt * P:tt * P + P], wt[:, k, :], start=k == 0, stop=k == DC - 1)
                last.then_inc(work_filled, 1)

            def scores(u):
                if u.freed is not None:
                    pe.wait_ge(probs_ready, u.freed)
                o = s_bank[u.bank]
                if u.m == 0:
                    if isinstance(u.b, int) and u.kind == "B" and u.b == B - 1:
                        pe.wait_ge(gelu_ready, EARLY_BEFORE)
                    for k in ("q", "k") if u.kind == "A" else ("q2", "k2"):
                        pe.wait_ge(stacked[k], u.b * STACKS + STACKS)
                if u.kind == "A":
                    c, q, heads, keys = a_unit(u.m)
                    n = len(heads)
                    if isinstance(u.b, int) and u.b == 0 and u.m == 0:
                        pe.wait_ge(consts_pool, 1)
                    nc.tensor.matmul(o[:, :].rearrange("p (h k) -> p h k", h=n), identb[:, :], causal[:, None, S - keys:S].to_broadcast([P, n, keys]), start=True, stop=False)
                    q_, k_ = qS, kS
                else:
                    c, q, heads, keys = b_unit(u.m)
                    q_, k_ = q2S, k2S
                for a, s_ in enumerate(heads):
                    h = head_of(c, s_)
                    last = nc.tensor.matmul(o[:, a * keys:a * keys + keys], q_[0:KROWS, h, q * P:q * P + P], k_[0:KROWS, h, 0:keys], start=u.kind == "B", stop=u.kind == "B" or a == len(heads) - 1)
                last.then_inc(scores_ready, 1)

            def turn(u):
                pe.wait_ge(probs_ready, u.done)
                if u.turn_freed is not None:
                    pe.wait_ge(probsT_ready[u.turn], u.turn_freed)
                o, p = t_bank[u.turn], probs[u.buf]
                for j in range(4):
                    if u.kind == "A":
                        last = nc.tensor.transpose(o[:, j * P:j * P + P], p[:, j * P:j * P + P], ident[:, :])
                    else:
                        last = nc.tensor.transpose(o[0:SE, j * P:j * P + P], p[:, j * SE:j * SE + SE], ident[:, :])
                last.then_inc(turned, 1)

            def values(u):
                pe.wait_ge(probsT_ready[u.turn], u.turn_done)
                p = probsT[u.buf]
                if u.m == 0:
                    if isinstance(u.b, int) and u.b == 0:
                        pe.wait_ge(consts_dve, 1)
                    pe.wait_ge(vz_ready if u.kind == "A" else v2z_ready, u.b + 1)
                    if u.after is not None:
                        pe.wait_ge(oT_ready[u.after[0]], u.after[1] + 1)
                    if isinstance(u.b, int) and u.kind == "B" and u.b == B - 1:
                        pe.wait_ge(y_ready, EARLY_BEFORE - 1)
                if u.kind == "A":
                    c, q, heads, keys = a_unit(u.m)
                    n = keys // P
                    for kt in range(n):
                        for a, s_ in enumerate(heads):
                            par, strip, h = s_ // STRIPS, s_ % STRIPS, head_of(c, s_)
                            last = nc.tensor.matmul(o_bank[32 * strip:32 * strip + 32, c * S + q * P:c * S + q * P + P],
                                                    vz[:, kt, 32 * h:32 * h + 32], p[:, (a * n + kt) * P:(a * n + kt) * P + P],
                                                    start=par == 0 and kt == 0, stop=par == 1 and kt == n - 1)
                else:
                    c, q, heads, keys = b_unit(u.m)
                    for a, s_ in enumerate(heads):
                        par, strip, h = s_ // STRIPS, s_ % STRIPS, head_of(c, s_)
                        last = nc.tensor.matmul(o_bank[32 * strip:32 * strip + 32, c * S + q * P:c * S + q * P + P],
                                                v2z[:, 32 * h:32 * h + 32], p[0:SE, a * P:a * P + P], start=par == 0, stop=par == 1)
                last.then_inc(values_done, 1)

            def rows_of_rinv(w, k, b):
                o = open_bank(w)
                pe.wait_ge(rinv_ready[k], b + 1)
                for q in range(QT_N):
                    last = nc.tensor.transpose(o[0:H, q * P:q * P + P], rinv[k][:, q, :], ident[:, :])
                last.then_inc(work_filled, 1)

            def spread_rinv(w, k, b):
                o = open_bank(w)
                pe.wait_ge(rT_ready[k], b + 1)
                for c in range(DC):
                    last = nc.tensor.matmul(o[:, c * S:c * S + S], spread[:, c, :], rT[:, :], start=True, stop=True)
                last.then_inc(work_filled, 1)

            def turn_biases():
                pe.wait_ge(rows_loaded, 16 * 5)
                nc.tensor.transpose(t_bank[0][:, 0:4 * DC], bias_rows, ident[0:4 * DC, 0:4 * DC])
                nc.tensor.transpose(t_bank[1][:, 0:E * FC], b1_rows, ident[0:E * FC, 0:E * FC]).then_inc(bias_turned, 1)

            h_bank, x_bank = (bank[0:2], bank[2:4]), bank[4]

            def turn_x(j):
                n = j if isinstance(j, int) else j[2]
                pe.wait_ge(blk_loaded[n % RING], 32 * (j // RING) + 32 if isinstance(j, int) else j[1] * 32 + j[2] // RING * 32 + 32)
                if n > 0:
                    pe.wait_ge(xbT_ready, counted(j, 0))
                for c in range(DC):
                    last = nc.tensor.transpose(x_bank[:, c * P:c * P + P], xb[n % RING][:, c * P:c * P + P], ident[:, :])
                last.then_inc(xbT_filled, 1)

            def up(j):
                n = j if isinstance(j, int) else j[2]
                pe.wait_ge(xbT_ready, counted(j, 1))
                pe.wait_ge(w1_now_ready, counted(j, 1))
                w1_now = w1_early if n < EARLY else w1_later
                if n > 1:
                    pe.wait_ge(gelu_ready, counted(j, -1))
                for f in range(FC):
                    for k in range(DC):
                        last = nc.tensor.matmul(h_bank[n % 2][f // 4][:, f % 4 * P:f % 4 * P + P], w1_now[:, k, f * P:f * P + P],
                                                xbT[:, k, :], start=k == 0, stop=k == DC - 1)
                last.then_inc(hT_filled, 1)

            def down(j):
                n = j if isinstance(j, int) else j[2]
                if n < EARLY:
                    e = EARLY_W2[n]
                    pe.wait_ge(early_w2_loaded[e], 16 * EARLY_W2[0:n + 1].count(e))
                    pe.wait_ge(oT_ready["B"], B - 1 if n < EARLY_BEFORE - 1 else B)
                else:
                    e = bass.ds(pe.value_load(blk_e[0:1, bass.ds(counted(j, 0), 1)], min_val=0, max_val=E - 1), 1)
                pe.wait_ge(gelu_ready, counted(j, 1))
                if n > 0:
                    pe.wait_ge(y_ready, counted(j, 0 if n < EARLY else -1))
                for f in range(FC):
                    last = nc.tensor.matmul(y_of(n), gT[n % 2][:, f, :], w2[:, e, f, :], start=f == 0, stop=f == FC - 1)
                last.then_inc(yb_filled, 1)

            scope = ExitStack()
            for name, what, w in batch_script(lambda: scope.enter_context(pe.Fori(0, NL))):
                if name == "leave":
                    scope.close()
                elif name == "xT":
                    if isinstance(what, int) and what == 0:
                        pe.wait_ge(ident_ready, 1)
                    pe.wait_ge(x_loaded, what * 16 + 16)
                    turn4(w, x_in)
                elif name in ("q", "k"):
                    if isinstance(what, int) and what == 0 and name == "k":
                        pe.wait_ge(wqk_loaded, 16 * 2)
                    pe.wait_ge(xT_ready, what + 1)
                    across(w, wA["w" + name], xT, S)
                    if isinstance(what, int) and what == 0 and name == "k":
                        turn_biases()
                elif name == "v":
                    if isinstance(what, int) and what == 0:
                        pe.wait_ge(wvo_loaded, 16 * 2)
                    along(w, wA["wv"], xT)
                elif name == "cT":
                    o = open_bank(w)
                    if isinstance(what, int) and what == 0:
                        pe.wait_ge(wB_loaded, 16 * 5)
                    pe.wait_ge(ctx_loaded, what * 16 + 16)
                    for c in range(DC):
                        last = nc.tensor.transpose(o[:, c * SE:c * SE + SE], ctx_in[:, c * P:c * P + P], ident[0:SE, 0:SE])
                    last.then_inc(work_filled, 1)
                elif name == "k2":
                    pe.wait_ge(cT_ready, what + 1)
                    across(w, wB["wk"], cT, SE)
                elif name == "v2":
                    o = open_bank(w)
                    for k in range(DC):
                        last = nc.tensor.matmul(o[0:SE, 0:D], cT[:, k, :], wB["wv"][:, k, :], start=k == 0, stop=k == DC - 1)
                    last.then_inc(work_filled, 1)
                elif name == "x1T":
                    pe.wait_ge(x1_ready, what + 1)
                    turn4(w, x1)
                elif name == "q2":
                    pe.wait_ge(x1T_ready, what + 1)
                    across(w, wB["wq"], x12T, S)
                elif name == "x2T":
                    pe.wait_ge(x2_ready, what + 1)
                    turn4(w, rows[:, 0, :, :])
                elif name == "route":
                    o = open_bank(w)
                    pe.wait_ge(x2T_ready, what + 1)
                    for tt in range(QT_N):
                        for k in range(DC):
                            last = nc.tensor.matmul(o[:, tt * E:tt * E + E], x12T[:, k, tt * P:tt * P + P], rw[:, k, :], start=k == 0, stop=k == DC - 1)
                    last.then_inc(work_filled, 1)
                elif name == "rank":
                    o = open_bank(w)
                    pe.wait_ge(member_ready, what + 1)
                    m = member[:, :, :].rearrange("p t e -> p (t e)")
                    nc.tensor.matmul(o[:, 0:QT_N * E], before[:, :], m, start=True, stop=True)
                    nc.tensor.matmul(o[:, QT_N * E:2 * QT_N * E], onesb[:, :], m, start=True, stop=True).then_inc(work_filled, 1)
                elif name in ("rTA", "rTB"):
                    rows_of_rinv(w, name[-1], what)
                elif name in ("RA", "RB"):
                    spread_rinv(w, name[-1], what)
                elif name in ("woA", "woB"):
                    pe.wait_ge(oT_ready[name[-1]], what + 1)
                    along(w, (wA if name == "woA" else wB)["wo"], oT)
                elif name == "scores":
                    scores(what)
                elif name == "turn":
                    turn(what)
                elif name == "values":
                    values(what)
                elif name == "eT":
                    turn_x(what)
                elif name == "eU":
                    up(what)
                elif name == "eD":
                    down(what)

            def step(j, prev, nxt):
                up(j)
                if nxt is not None:
                    turn_x(nxt)
                down(prev)

            pe.wait_ge(tables_ready, 1)
            step(EARLY, EARLY - 1, EARLY + 1)
            up(EARLY + 1)
            turn_x(EARLY + 2)
            pe.wait_ge(late_loaded, 16 * LATE)
            down(EARLY)
            turns = (LATER - 3) // RING
            with pe.Fori(0, turns) as i:
                for s in range(EARLY + 1, EARLY + 1 + RING):
                    step(("loop", i, s + 1), ("loop", i, s), ("loop", i, s + 2))
            for j in range(EARLY + turns * RING + 2, NBLK):
                step(j, j - 1, j + 1 if j + 1 < NBLK else None)
            down(NBLK - 1)

            for s in range(B):
                if s in SUMMED_BY_DVE:
                    continue
                pe.wait_ge(parts_loaded[s], 16 * TOPK)
                for tt in range(QT_N):
                    for k in range(TOPK):
                        last = nc.tensor.matmul(tail_sum[s][:, tt, :], ident[:, :], tail_y[s][:, k, tt, :], start=k == 0, stop=k == TOPK - 1)
                last.then_inc(sum_filled, 1)

        @block.scalar
        def _(act):
            def shifted(w, dst, n, col):
                act.wait_ge(work_filled, w.filled)
                for c in range(DC):
                    last = nc.scalar.activation(dst[:, c, :], w_bank[w.bank][:, c * n:c * n + n], ACT.Identity, bias=bias[:, col + c:col + c + 1])
                return last

            flat = lambda x: x[:, :, :].rearrange("p c n -> p (c n)")

            def high(k, src, b, ready):
                act.wait_ge(ready, b + 1)
                if k == "q2":
                    act.wait_ge(parts_written["q"], 16 * min(b + 2, B) if isinstance(b, int) else b * 16 + 32)
                elif not (isinstance(b, int) and b == 0):
                    act.wait_ge(parts_written[k], b * 16)
                    if k == "q" and not (isinstance(b, int) and b < 2):
                        act.wait_ge(parts_written["q2"], b * 16 - 16)
                dst = operand[k][1]
                nc.scalar.copy(flat(dst[:, high_at(k), :, :]), flat(src)).then_inc(high_ready[k], 1)
            h_bank, x_bank = (bank[0:2], bank[2:4]), bank[4]

            def take_x(j):
                act.wait_ge(xbT_filled, counted(j, 1))
                nc.scalar.copy(xbT.rearrange("p c n -> p (c n)"), x_bank[:, 0:D]).then_inc(xbT_ready, 1)

            def gelu(j):
                n = j if isinstance(j, int) else j[2]
                if n == 0:
                    act.wait_ge(early_tables_ready, 1)
                    act.wait_ge(x1_ready, B)
                e = act.value_load(blk_e[0:1, bass.ds(counted(j, 0), 1)], min_val=0, max_val=E - 1)
                act.wait_ge(hT_filled, counted(j, 1))
                if n > 1:
                    act.wait_ge(yb_filled, counted(j, -1))
                for f in range(FC):
                    last = nc.scalar.activation(gT[n % 2][:, f, :], h_bank[n % 2][f // 4][:, f % 4 * P:f % 4 * P + P], ACT.Gelu, bias=b1[:, bass.ds(e * FC + f, 1)])
                last.then_inc(gelu_ready, 1)

            scope = ExitStack()
            for name, what, w in batch_script(lambda: scope.enter_context(act.Fori(0, NL))):
                b = what
                if name == "leave":
                    scope.close()
                elif name in ("xT", "x1T", "x2T"):
                    ready = {"xT": xT_ready, "x1T": x1T_ready, "x2T": x2T_ready}[name]
                    act.wait_ge(work_filled, w.filled)
                    ins = nc.scalar.copy(flat(xT if name == "xT" else x12T), w_bank[w.bank][:, :])
                    ins.then_inc(ready, 1)
                elif name in ("k", "k2"):
                    dst, n, col, ready = (kT, S, DC, kT_ready) if name == "k" else (k2T, SE, 3 * DC, k2T_ready)
                    if isinstance(b, int) and b == 0:
                        if name == "k":
                            act.wait_ge(bias_turned, 1)
                            nc.scalar.copy(bias[:, :], t_bank[0][:, 0:4 * DC])
                            nc.scalar.copy(b1[:, :], t_bank[1][:, 0:E * FC]).then_inc(bias_ready, 1)
                            act.wait_ge(bias_ready, 1)
                    else:
                        act.wait_ge(parts_ready[name], b)
                    shifted(w, dst, n, col).then_inc(ready, 1)
                    high(name, dst, b, ready)
                elif name == "q":
                    high(name, qT, b, q_ready)
                elif name == "q2":
                    high(name, q2T, b, q2_ready)
                elif name in ("km", "qm", "k2m", "q2m"):
                    k = name[:-1]
                    src, dst = operand[k]
                    act.wait_ge(left_ready[k], b + 1)
                    nc.scalar.copy(flat(dst[:, 1, :, :]), flat(src)).then_inc(middle_ready[k], 1)
                elif name == "zB":
                    act.wait_ge(x2_ready, b + 1)
                    nc.scalar.copy(y_b, rows[:, 0, :, 0:D]).then_inc(rows_ready, 1)
                elif name == "cT":
                    act.wait_ge(work_filled, w.filled)
                    ins = nc.scalar.copy(flat(cT), w_bank[w.bank][:, 0:DC * SE])
                    ins.then_inc(cT_ready, 1)
                elif name in ("rTA", "rTB"):
                    act.wait_ge(work_filled, w.filled)
                    ins = nc.scalar.copy(rT[:, :], w_bank[w.bank][0:H, 0:S])
                    ins.then_inc(rT_ready[name[-1]], 1)
                elif name in ("RA", "RB"):
                    act.wait_ge(work_filled, w.filled)
                    ins = nc.scalar.copy(flat(rexp), w_bank[w.bank][:, :])
                    ins.then_inc(rexp_ready[name[-1]], 1)
                elif name == "scores":
                    u = what
                    act.wait_ge(max_ready, u.done)
                    p = probs[u.buf]
                    c, q, heads, keys = a_unit(u.m) if u.kind == "A" else b_unit(u.m)
                    for a, s_ in enumerate(heads):
                        h = head_of(c, s_)
                        last = nc.scalar.activation(p[:, a * keys:a * keys + keys], s_bank[u.bank][:, a * keys:a * keys + keys], ACT.Exp,
                                                    bias=nmax[u.bank][:, a:a + 1], accum_out=sums[u.kind][:, q, h:h + 1])
                    last.then_inc(probs_ready, 1)
                elif name == "turn":
                    u = what
                    if turns_on(u.kind, u.m) == "act":
                        act.wait_ge(turned, u.done)
                        n = P if u.kind == "A" else SE
                        nc.scalar.copy(probsT[u.buf][0:n, :], t_bank[u.turn][0:n, :]).then_inc(probsT_ready[u.turn], 1)
                elif name == "route":
                    act.wait_ge(rmax_ready, b + 1)
                    for tt in range(QT_N):
                        last = nc.scalar.activation(etop[:, tt, :], top[:, tt, :], ACT.Exp, bias=ntop[:, tt:tt + 1], accum_out=esum[:, tt:tt + 1])
                    last.then_inc(rexps_ready, 1)
                elif name == "gate":
                    act.wait_ge(pdif_ready, b + 1)
                    nc.scalar.activation(pexp[:, :], pdif[:, :], ACT.Exp).then_inc(pexp_ready, 1)
                elif name == "eT":
                    take_x(what)
                elif name == "eU":
                    gelu(what)
                elif name == "pads":
                    write_pads(act, range(E // 2, E))

            act.wait_ge(tables_ready, 1)
            gelu(EARLY)
            take_x(EARLY + 1)
            turns = (LATER - 2) // RING
            with act.Fori(0, turns) as i:
                for s in range(EARLY, EARLY + RING):
                    gelu(("loop", i, s + 1))
                    take_x(("loop", i, s + 2))
            for j in range(EARLY + turns * RING + 1, NBLK):
                gelu(j)
                if j + 1 < NBLK:
                    take_x(j + 1)

            for s in range(B):
                act.wait_ge(tail_rstd_ready, s + 1)
                for tt in range(QT_N):
                    last = nc.scalar.activation(tail_x[s][:, tt, :], tail_sum[s][:, tt, :], ACT.Copy, scale=tail_rstd[s][:, tt:tt + 1])
                last.then_inc(tail_z_ready, 1)

        @block.gpsimd
        def _(pool):
            own = Chain(pool, pool_own, POOL_LINKS, NL)
            gp = nc.gpsimd
            own.link(gp.memset(ident[:, :], 0.0))
            gp.affine_select(out=ident[:, :], in_=ident[:, :], compare_op=ALU.not_equal, fill=1.0, base=0, pattern=[[-1, P]], channel_multiplier=1).then_inc(ident_ready, 1)
            own.link(gp.memset(identb[:, :], 0.0))
            own.link(gp.affine_select(out=identb[:, :], in_=identb[:, :], compare_op=ALU.not_equal, fill=1.0, base=0, pattern=[[-1, P]], channel_multiplier=1))
            own.link(gp.memset(causal[:, :], 0.0))
            own.link(gp.affine_select(out=causal[:, :], in_=causal[:, :], compare_op=ALU.is_ge, fill=MASKED, base=P, pattern=[[-1, S]], channel_multiplier=1))
            own.link(gp.memset(before[:, :], 1.0))
            own.link(gp.affine_select(out=before[:, :], in_=before[:, :], compare_op=ALU.is_gt, fill=0.0, base=0, pattern=[[1, P]], channel_multiplier=-1))
            own.link(gp.memset(spread[:, :, :], 1.0))
            own.link(gp.affine_select(out=spread[:, :, :], in_=spread[:, :, :], compare_op=ALU.is_ge, fill=0.0, base=0, pattern=[[P, DC], [1, P]], channel_multiplier=-HD))
            own.link(gp.affine_select(out=spread[:, :, :], in_=spread[:, :, :], compare_op=ALU.is_ge, fill=0.0, base=HD - 1, pattern=[[-P, DC], [-1, P]], channel_multiplier=HD))
            own.link(gp.iota(iota8[:, :], pattern=[[1, E]], base=0, channel_multiplier=0, allow_small_or_imprecise_dtypes=True))
            own.link(gp.iota(base[:, :], pattern=[[REGION, E]], base=0, channel_multiplier=0, allow_small_or_imprecise_dtypes=True))
            own.link(gp.iota(run[:, :], pattern=[[REGION, E]], base=0, channel_multiplier=0, allow_small_or_imprecise_dtypes=True))
            own.link(gp.iota(idf[:, :, :], pattern=[[T, TOPK], [P, QT_N]], base=0, channel_multiplier=1, allow_small_or_imprecise_dtypes=True))
            own.link(gp.iota(jgrid[:, :], pattern=[[1, LATER]], base=0, channel_multiplier=0, allow_small_or_imprecise_dtypes=True))
            own.link(gp.memset(dummy_meta[:, :, :], 0.0))
            gp.iota(dummy_meta[:, :, 0:1].bitcast(I32), pattern=[[P, NDUMMY], [0, 1]], base=Y_PAD + E * P, channel_multiplier=1).then_inc(consts_pool, 1)
            own.link(gp.memset(pad_rows[:, :], 0.0))
            gp.iota(pad_rows[:, D:D + 2 * E].rearrange("p (e a) -> p e a", a=2)[:, :, 0:1].bitcast(I32), pattern=[[P, E], [0, 1]], base=Y_PAD, channel_multiplier=1).then_inc(pad_rows_ready, 1)

            def two(x):
                return x[:, None, :].to_broadcast([P, QT_N, D])

            def put(j):
                n = j if isinstance(j, int) else j[2]
                s = n % RING
                pool.wait_ge(y_ready, j + 1 if isinstance(j, int) else j[1] * RING + (j[2] + 1))
                pool.sem_inc(held["pool"], 1)
                gp.indirect_dma_start(out=y_dram, out_offset=bass.IndirectOffsetOnAxis(ap=xb[s][:, D:D + 1].bitcast(U32), axis=0),
                                      in_=xb[s][:, 0:D], in_offset=None).then_inc(y_written[s], 16)

            scope = ExitStack()

            def loop():
                i = scope.enter_context(pool.Fori(0, NL))
                own.enter(i)
                return i

            for name, what, w in batch_script(loop):
                b = what
                first = isinstance(b, int) and b == 0
                if name == "leave":
                    own.leave()
                    scope.close()
                elif name == "xres":
                    if first:
                        pool.wait_ge(vecA_loaded, 16 * 2)
                    pool.wait_ge(x_loaded, b * 16 + 16)
                    if not first:
                        pool.wait_ge(x1_ready, b)
                    gp.tensor_tensor(xres, x_in, two(vecs["boA"]), ALU.add).then_inc(xres_ready, 1)
                elif name in ("q", "k", "q2", "k2"):
                    if splits(name, b) == "pool":
                        leave_high(pool, name, b)
                elif name in ("km", "qm", "k2m", "q2m"):
                    if splits(name, b) == "pool":
                        leave_middle(pool, name[:-1], b)
                elif name in ("nA", "nB"):
                    k = name[-1]
                    pool.wait_ge(var_ready[k], b + 1)
                    gp.tensor_tensor(rstd[k][:, :], var[k][:, :], half[:, :], ALU.pow).then_inc(rstd_ready[k], 1)
                elif name == "x1res":
                    if first:
                        pool.wait_ge(vec_loaded, 16 * 9)
                    pool.wait_ge(x1_ready, b + 1)
                    if not first:
                        pool.wait_ge(sum_ready["B"], b)
                    gp.tensor_tensor(x1res[:, :, :], x1[:, :, :], two(vecs["boB"]), ALU.add).then_inc(x1res_ready, 1)
                elif name == "rank":
                    pool.wait_ge(slots_ready, b + 1)
                    pool.wait_ge(rows_ready, b + 1)
                    pool.sem_inc(held["pool"], 1)
                    for k in range(TOPK):
                        for tt in range(QT_N):
                            gp.indirect_dma_start(out=xs_dram, out_offset=bass.IndirectOffsetOnAxis(ap=slot[:, k, tt:tt + 1], axis=0),
                                                  in_=rows[:, k, tt, :], in_offset=None).then_inc(dispatched, 16)
                elif name == "eD":
                    put(what)

            put(EARLY - 1)
            turns = LATER // RING
            with pool.Fori(0, turns) as i:
                for s in range(EARLY, EARLY + RING):
                    put(("loop", i, s))
            for j in range(EARLY + turns * RING, NBLK):
                put(j)

            late = Chain(pool, pool_late, 0, 1)

            def raised(s):
                pool.wait_ge(tail_var_ready, s + 1)
                late.link(gp.tensor_tensor(tail_rstd[s], tail_var[s], half[:, :], ALU.pow))
                gp.tensor_tensor(tail_shift[s], tail_mv[s][:, :, 0], tail_rstd[s], ALU.mult).then_inc(tail_rstd_ready, 1)

            def finish(s):
                pool.wait_ge(tail_g_ready, s + 1)
                gp.tensor_tensor(tail_x[s], tail_x[s], two(vecs["be3"]), ALU.add).then_inc(tail_out[s], 1)

            for s in range(B + 2):
                if s < B:
                    raised(s)
                if s > 1 and s - 2 not in SHIFTED_BY_DVE:
                    finish(s - 2)

        @block.vector
        def _(dve):
            v = nc.vector
            own = Chain(dve, dve_own, DVE_LINKS, NL)
            v.memset(onesb[:, :], 1.0)
            v.memset(half[:, :], -0.5)
            v.memset(ones8[:, :], 1.0)
            v.memset(vz, 0.0)
            v.memset(v2z[:, :], 0.0).then_inc(consts_dve, 1)
            dve.wait_ge(consts_dve, 1)
            dve.wait_ge(consts_pool, 1)
            dve.wait_ge(bias_ready, 1)

            def norm(k, y, res, resem, b, first, w):
                dve.wait_ge(work_filled, w.filled)
                dve.wait_ge(resem, b + 1)
                if k == "B" and not first:
                    dve.wait_ge(dispatched, b * (16 * QT_N * TOPK))
                ins = v.tensor_tensor(y, w_bank[w.bank][:, :].rearrange("p (t d) -> p t d", t=QT_N), res, ALU.add)
                ins.then_inc(sum_ready[k], 1)
                dve.wait_ge(sum_ready[k], b + 1)
                for tt in range(QT_N):
                    ins = v.bn_stats(stats[k][:, tt, :], y[:, tt, :])
                own.link(ins)
                dve.sem_inc(held["dve"], 1)
                for tt in range(QT_N):
                    ins = v.bn_aggr(mv[k][:, tt, :], stats[k][:, tt, :])
                own.link(ins)
                v.tensor_scalar(var[k][:, :], mv[k][:, :, 1], EPS, None, ALU.add).then_inc(var_ready[k], 1)
                for tt in range(QT_N):
                    ins = v.scalar_tensor_tensor(out=y[:, tt, :], in0=y[:, tt, :], scalar=mv[k][:, tt, 0:1], in1=vecs["g1" if k == "A" else "g2"][:, :],
                                                 op0=ALU.subtract, op1=ALU.mult)
                ins.then_inc(z_ready[k], 1)

            def normalised(k, y, b, first):
                dst, shift_, ready = (x1, "be1", x1_ready) if k == "A" else (rows[:, 0, :, 0:D], "be2", x2_ready)
                dve.wait_ge(z_ready[k], b + 1)
                dve.wait_ge(rstd_ready[k], b + 1)
                if k == "A" and not first:
                    dve.wait_ge(x1res_ready, b)
                for tt in range(QT_N):
                    ins = v.scalar_tensor_tensor(out=dst[:, tt, :], in0=y[:, tt, :], scalar=rstd[k][:, tt:tt + 1], in1=vecs[shift_][:, :],
                                                 op0=ALU.mult, op1=ALU.add)
                ins.then_inc(ready, 1)

            def scaled_q(w, dst, col, ready, split, b, first):
                dve.wait_ge(work_filled, w.filled)
                if not first:
                    dve.wait_ge(split, b)
                for c in range(DC):
                    ins = v.tensor_scalar(dst[:, c, :], w_bank[w.bank][:, c * S:c * S + S], bias[:, col + c:col + c + 1], HD ** -0.5, ALU.add, ALU.mult)
                ins.then_inc(ready, 1)

            def spread_v(dst, src, bv, n):
                d4 = dst.rearrange("p (s a x) -> p s a x", s=H // 2, a=2)
                s4 = src.rearrange("p (s a x) -> p s a x", s=H // 2, a=2)
                b4 = bv[0:n, :].rearrange("p (s a x) -> p s a x", s=H // 2, a=2)
                for par in range(2):
                    ins = v.tensor_tensor(d4[:, :, par, par * HD:par * HD + HD], s4[:, :, par, :], b4[:, :, par, :], ALU.add)
                return ins

            def find(cum, j_at, weight, j_row, ge, skipped, blkf, first, n):
                wide = lambda x: x[:, None, :].to_broadcast([P, n, E])
                own.link(v.tensor_tensor(ge, j_at[:, :, None].to_broadcast([P, n, E]), wide(cum), ALU.is_ge))
                own.link(v.tensor_reduce(blkf, ge, AX, ALU.add))
                own.link(v.tensor_tensor(ge, ge, wide(weight), ALU.mult))
                own.link(v.tensor_reduce(skipped, ge, AX, ALU.add))
                own.link(v.tensor_tensor(skipped, j_row, skipped, ALU.subtract))
                own.link(v.tensor_scalar(skipped, skipped, float(P), None, ALU.mult))
                own.link(v.scalar_tensor_tensor(out=blk_row[:, first:first + n], in0=blkf, scalar=float(REGION), in1=skipped, op0=ALU.mult, op1=ALU.add))
                return v.tensor_scalar(blk_e[:, first:first + n], blkf, float(E - 1), None, ALU.min)

            def blocks_of_rows(more):
                own.link(v.tensor_tensor(nb[:, :], run[:, :], base[:, :], ALU.subtract))
                own.link(v.tensor_scalar(nb[:, :], nb[:, :], float(more), None, ALU.add))
                own.link(v.tensor_copy(nbi[:, :], nb[:, :]))
                own.link(v.tensor_single_scalar(nbi[:, :], nbi[:, :], P.bit_length() - 1, ALU.arith_shift_right))
                own.link(v.tensor_copy(nb[:, :], nbi[:, :]))

            def early_table():
                blocks_of_rows(0)
                own.link(v.tensor_tensor_scan(cum[:, :], ones8[:, :], nb[:, :], 0.0, ALU.mult, ALU.add))
                own.link(find(cum, jgrid[:, 0:EARLY], nb, jgrid[:, 0:EARLY], ge_early[:, :, :], skipped_early[:, :], blkf_early[:, :], 0, EARLY))
                v.memset(early_next[:, :], 0.0).then_inc(early_tables_ready, 1)
                own.link(v.tensor_tensor(early_of[:, :], cum[:, :], nb[:, :], ALU.subtract))
                own.link(v.tensor_scalar(early_of[:, :], early_of[:, :], float(EARLY), None, ALU.min))
                own.link(v.scalar_tensor_tensor(out=early_of[:, :], in0=cum[:, :], scalar=float(EARLY), in1=early_of[:, :], op0=ALU.min, op1=ALU.subtract))
                v.tensor_copy(early_next[:, 0:E - 1], early_of[:, 1:E])
                own.link(v.tensor_scalar(jlater[:, :], jgrid[:, :], early_of[:, 0:1], None, ALU.add))

            def later_table():
                blocks_of_rows(P - 1)
                v.tensor_tensor(weighed[:, :], nb[:, :], early_next[:, :], ALU.subtract)
                own.link(v.tensor_tensor(nb[:, :], nb[:, :], early_of[:, :], ALU.subtract))
                own.link(v.tensor_tensor_scan(cum[:, :], ones8[:, :], nb[:, :], 0.0, ALU.mult, ALU.add))
                find(cum, jgrid[:, :], weighed, jlater[:, :], ge, skipped, blkf, EARLY, LATER).then_inc(tables_ready, 1)

            moe = Chain(dve, dve_moe, 2 * RING, (LATER - 2) // RING)

            def take_w1(j):
                n = j if isinstance(j, int) else j[2]
                e = dve.value_load(blk_e[0:1, bass.ds(counted(j, 0), 1)], min_val=0, max_val=E - 1)
                if n > 0:
                    dve.wait_ge(hT_filled, counted(j, 0))
                w1_now = w1_early if n < EARLY else w1_later
                if n == 0:
                    dve.wait_ge(scores_ready, units_to("A", B - 1))
                    dve.wait_ge(experts_loaded, 16 * (2 * E - LATE))
                v.tensor_copy(w1_now, w1[:, :, bass.ds(e, 1), :].rearrange("p k a f -> p k (a f)")).then_inc(w1_now_ready, 1)

            def take_y(j):
                n = j if isinstance(j, int) else j[2]
                s = n % RING
                dve.wait_ge(yb_filled, counted(j, 1))
                moe.link(v.tensor_tensor(y_sum, y_of(n), b2b[s], ALU.add))
                moe.link(v.tensor_scalar(y_sum, y_sum, xb[s][:, D + 1:D + 2], None, ALU.mult))
                v.scalar_tensor_tensor(out=xb[s][:, 0:D], in0=xb[s][:, 0:D], scalar=1.0 / TOPK, in1=y_sum, op0=ALU.mult, op1=ALU.add).then_inc(y_ready, 1)
                dve.wait_ge(y_ready, counted(j, 1))

            scope = ExitStack()

            def loop():
                i = scope.enter_context(dve.Fori(0, NL))
                own.enter(i)
                return i

            for name, what, w in batch_script(loop):
                b = what
                first = isinstance(b, int) and b == 0
                if name == "leave":
                    own.leave()
                    scope.close()
                elif name in ("q", "k"):
                    if name == "q":
                        scaled_q(w, qT, 0, q_ready, parts_ready["q"], b, first)
                    if splits(name, b) == "dve":
                        leave_high(dve, name, b)
                elif name in ("qm", "km"):
                    if splits(name, b) == "dve":
                        leave_middle(dve, name[:-1], b)
                elif name == "q2":
                    scaled_q(w, q2T, 2 * DC, q2_ready, parts_ready["q2"], b, first)
                elif name == "v":
                    dve.wait_ge(work_filled, w.filled)
                    if first:
                        dve.wait_ge(vecA_loaded, 16 * 2)
                    for tt in range(QT_N):
                        ins = spread_v(vz[:, tt, :], w_bank[w.bank][:, tt * D:tt * D + D], vecs["bvA"], P)
                    ins.then_inc(vz_ready, 1)
                elif name == "v2":
                    dve.wait_ge(work_filled, w.filled)
                    if first:
                        dve.wait_ge(vec_loaded, 16 * 9)
                    ins = spread_v(v2z[:, :], w_bank[w.bank][0:SE, 0:D], vecs["bvB"], SE)
                    ins.then_inc(v2z_ready, 1)
                elif name == "scores":
                    u = what
                    dve.wait_ge(scores_ready, u.done)
                    c, q, heads, keys = a_unit(u.m) if u.kind == "A" else b_unit(u.m)
                    n = len(heads)
                    v.tensor_reduce(nmax[u.bank][:, 0:n], s_bank[u.bank][:, 0:n * keys].rearrange("p (h k) -> p h k", h=n), AX, ALU.max, negate=True).then_inc(max_ready, 1)
                elif name == "turn":
                    u = what
                    if turns_on(u.kind, u.m) == "dve":
                        dve.wait_ge(turned, u.done)
                        n = P if u.kind == "A" else SE
                        v.tensor_copy(probsT[u.buf][0:n, :], t_bank[u.turn][0:n, :]).then_inc(probsT_ready[u.turn], 1)
                elif name in ("rTA", "rTB"):
                    k = name[-1]
                    dve.wait_ge(probs_ready, units_to(k, b))
                    if not first:
                        dve.wait_ge(rT_ready[k], b)
                    v.reciprocal(rinv[k][:, :, :], sums[k][:, :, :]).then_inc(rinv_ready[k], 1)
                elif name in ("oTA", "oTB"):
                    k = name[-1]
                    dve.wait_ge(rexp_ready[k], b + 1)
                    dve.wait_ge(values_done, units_to(k, b))
                    v.tensor_tensor(oT[:, :, :].rearrange("p c n -> p (c n)"), o_bank[:, :], rexp[:, :, :].rearrange("p c n -> p (c n)"), ALU.mult).then_inc(oT_ready[k], 1)
                elif name in ("woA", "woB"):
                    w_norm = w
                elif name == "nA":
                    if first:
                        dve.wait_ge(vec_loaded, 16 * 9)
                    norm("A", y_a, xres, xres_ready, b, first, w_norm)
                elif name in ("zA", "zB"):
                    normalised(name[-1], y_a if name == "zA" else y_b, b, first)
                elif name == "nB":
                    norm("B", y_b, x1res[:, :, :], x1res_ready, b, first, w_norm)
                elif name == "route":
                    dve.wait_ge(work_filled, w.filled)
                    ins = v.tensor_tensor(lg[:, :, :], w_bank[w.bank][:, 0:QT_N * E].rearrange("p (t e) -> p t e", t=QT_N), rb[:, None, :].to_broadcast([P, QT_N, E]), ALU.add)
                    ins.then_inc(logits_ready, 1)
                    dve.wait_ge(logits_ready, b + 1)
                    dve.sem_inc(held["dve"], 1)
                    for tt in range(QT_N):
                        ins = v.max(top[:, tt, :], lg[:, tt, :])
                    own.link(ins)
                    v.tensor_scalar(ntop[:, :], top[:, :, 0], -1.0, None, ALU.mult).then_inc(rmax_ready, 1)
                    for tt in range(QT_N):
                        ins = v.max_index(topi[:, tt, :], top[:, tt, :], lg[:, tt, :])
                    own.link(ins)
                    own.link(v.tensor_copy(topf[:, :, :], topi[:, :, 0:TOPK]))
                    for k in range(TOPK):
                        for tt in range(QT_N):
                            ins = v.tensor_scalar(hot[:, k, tt, :], iota8[:, :], topf[:, tt, k:k + 1], None, ALU.is_equal)
                    own.link(ins)
                    v.tensor_tensor(member[:, :, :], hot[:, 0, :, :], hot[:, 1, :, :], ALU.add).then_inc(member_ready, 1)
                elif name == "gate":
                    dve.wait_ge(rexps_ready, b + 1)
                    own.link(v.reciprocal(erec[:, :], esum[:, :]))
                    own.link(v.tensor_tensor(pdif[:, :], etop[:, :, 1], etop[:, :, 0], ALU.subtract))
                    ins = v.tensor_tensor(pdif[:, :], pdif[:, :], erec[:, :], ALU.mult)
                    ins.then_inc(pdif_ready, 1)
                    dve.wait_ge(pexp_ready, b + 1)
                    own.link(v.tensor_scalar(den[:, :], pexp[:, :], 1.0, None, ALU.add))
                    own.link(v.reciprocal(cw[:, 0, :], den[:, :]))
                    own.link(v.tensor_tensor(cw[:, 1, :], pexp[:, :], cw[:, 0, :], ALU.mult))
                elif name == "rank":
                    dve.wait_ge(work_filled, w.filled)
                    o = w_bank[w.bank]
                    own.link(v.tensor_tensor(run1[:, :], run[:, :], o[:, 2 * E:3 * E], ALU.add))
                    v.tensor_tensor(place[:, 0, :], o[:, 0:E], run[:, :], ALU.add)
                    own.link(v.tensor_tensor(place[:, 1, :], o[:, E:2 * E], run1[:, :], ALU.add))
                    v.tensor_tensor(run[:, :], run1[:, :], o[:, 3 * E:4 * E], ALU.add).then_inc(places_ready, 1)
                    dve.wait_ge(places_ready, b + 1)
                    own.link(v.tensor_tensor(picked[:, :, :, :], hot[:, :, :, :], place[:, None, :, :].to_broadcast([P, TOPK, QT_N, E]), ALU.mult))
                    own.link(v.tensor_reduce(slotf[:, :, :], picked[:, :, :, :], AX, ALU.add))
                    if not first:
                        dve.wait_ge(dispatched, b * (16 * QT_N * TOPK))
                    v.tensor_copy(slot[:, :, :], slotf[:, :, :])
                    v.tensor_copy(rows[:, :, :, D:D + 1].bitcast(I32), idf[:, :, :, None])
                    own.link(v.tensor_copy(rows[:, :, :, D + 1:D + 2], cw[:, :, :, None]))
                    v.tensor_scalar(idf[:, :, :], idf[:, :, :], float(S), None, ALU.add).then_inc(slots_ready, 1)
                    if isinstance(b, int) and b == B - 1:
                        v.tensor_copy(pad_row[:, :], run[:, :]).then_inc(ends_ready, 1)
                elif name == "table":
                    early_table()
                elif name == "later":
                    later_table()
                elif name == "eW":
                    if what == EARLY:
                        dve.wait_ge(tables_ready, 1)
                    take_w1(what)
                elif name == "eD":
                    take_y(what)

            take_w1(EARLY + 1)
            take_y(EARLY - 1)
            turns = (LATER - 2) // RING
            with dve.Fori(0, turns) as i:
                moe.enter(i)
                for s in range(EARLY, EARLY + RING):
                    take_w1(("loop", i, s + 2))
                    take_y(("loop", i, s))
                moe.leave()
            for j in range(EARLY + turns * RING, NBLK):
                if j + 2 < NBLK:
                    take_w1(j + 2)
                take_y(j)

            tail = Chain(dve, dve_tail, 0, 1)

            def begin(s):
                if s in SUMMED_BY_DVE:
                    dve.wait_ge(parts_loaded[s], 16 * TOPK)
                    tail.link(v.tensor_tensor(tail_x[s], tail_x[s], tail_y[s][:, 1, :, :], ALU.add))
                else:
                    dve.wait_ge(sum_filled, s + 1 - len(SUMMED_BY_DVE))
                for tt in range(QT_N):
                    ins = v.bn_stats(tail_stats[s][:, tt, :], tail_sum[s][:, tt, :])
                ins.then_inc(stats_ready, 1)

            def variance(s):
                dve.wait_ge(stats_ready, s + 1)
                dve.sem_inc(held["dve"], 1)
                for tt in range(QT_N):
                    ins = v.bn_aggr(tail_mv[s][:, tt, :], tail_stats[s][:, tt, :])
                tail.link(ins)
                v.tensor_scalar(tail_var[s], tail_mv[s][:, :, 1], EPS, None, ALU.add).then_inc(tail_var_ready, 1)

            def scaled(s):
                x = tail_x[s]
                dve.wait_ge(tail_z_ready, s + 1)
                for tt in range(QT_N):
                    ins = v.scalar_tensor_tensor(out=x[:, tt, :], in0=x[:, tt, :], scalar=tail_shift[s][:, tt:tt + 1], in1=vecs["g3"][:, :], op0=ALU.subtract, op1=ALU.mult)
                ins.then_inc(tail_g_ready, 1)

            def shifted(s):
                dve.wait_ge(tail_g_ready, s + 1)
                v.tensor_tensor(tail_x[s], tail_x[s], vecs["be3"][:, None, :].to_broadcast([P, QT_N, D]), ALU.add).then_inc(tail_out[s], 1)

            for s in range(B + 2):
                if s < B:
                    begin(s)
                if s > 1:
                    scaled(s - 2)
                if s < B:
                    variance(s)
                if s > 1 and s - 2 in SHIFTED_BY_DVE:
                    shifted(s - 2)


DVE_LINKS = 18
POOL_LINKS = 0

_SHORT = {"ctx": "ctx_1024", "x": "x"}
_LAYER = ["sa_wq", "sa_bq", "sa_wk", "sa_bk", "sa_wv", "sa_bv", "sa_wo", "sa_bo", "ca_wq", "ca_bq", "ca_wk", "ca_bk", "ca_wv", "ca_bv",
          "ca_wo", "ca_bo", "ln1_g", "ln1_b", "ln2_g", "ln2_b", "ln3_g", "ln3_b", "router_w", "router_b", "e_w1", "e_b1", "e_w2", "e_b2"]


def kernel(**inputs):
    import numpy as np
    import concourse.bacc as bacc
    from concourse.bass_utils import run_bass_kernel_spmd

    nc = bacc.Bacc("TRN2", target_bir_lowering=False, num_devices=1)
    names = {**_SHORT, **{k: f"L0_xattn_{k}" for k in _LAYER}}
    arrays, aps = {}, {}
    for short, name in names.items():
        a = np.ascontiguousarray(inputs[name])
        arrays[f"in_{short}"] = a
        aps[short] = nc.dram_tensor(f"in_{short}", a.shape, mybir.dt.from_np(a.dtype), kind="ExternalInput").ap()
    out = nc.dram_tensor("layer_out", (B, S, D), F32, kind="ExternalOutput").ap()
    decoder_layer(nc, aps, out)
    r = run_bass_kernel_spmd(nc, [arrays], core_ids=[0])
    return r.results[0]["layer_out"]
```
